# Optimizing a Trainium2 kernel written in Bass

```python
import numpy as np
import jax
import jax.numpy as jnp

def _softmax(x, axis=-1):
    return jax.nn.softmax(x, axis=axis)

def _gelu(x):
    return jax.nn.gelu(x, approximate=True)

def _silu(x):
    return jax.nn.silu(x)

def _sigmoid(x):
    return jax.nn.sigmoid(x)

def _layernorm(x, axis=-1, eps=1e-05):
    m = jnp.mean(x, axis=axis, keepdims=True)
    v = jnp.var(x, axis=axis, keepdims=True)
    return (x - m) / jnp.sqrt(v + eps)

def _scatter_add(tgt, idx, src, axis=0):
    return tgt.at[idx].add(src)

def _segment_sum(src, seg, n):
    return jax.ops.segment_sum(src, seg, n)
kernel_name = 'mk_xattn_ffn_d4_seqx_r8_dddd38'

def setup_inputs(seed: int=0):
    np.random.seed(seed)
    _w = jnp.asarray

    def _rec_inputs():
        import jax
        import jax.numpy as jnp
        _rk = jax.random.key(seed)
        x = -0.000125 + 0.9999 * jax.random.normal(jax.random.fold_in(_rk, 1), (4, 512, 128), jnp.float32)
        _lenS = 512 - jax.random.randint(jax.random.fold_in(_rk, 7), (4,), 0, max(1, 512 // 4) + 1, jnp.int32)
        _lenS2 = 154 - jax.random.randint(jax.random.fold_in(_rk, 8), (4,), 0, max(1, 154 // 4) + 1, jnp.int32)
        _ctx_1024P = jax.random.normal(jax.random.fold_in(_rk, 11), (4, 16, 128), jnp.float32)
        _ctx_1024c = jax.random.dirichlet(jax.random.fold_in(_rk, 511), 0.3 * jnp.ones((16,), jnp.float32), (4, 154))
        _ctx_1024t = jnp.einsum('bsk,bkd->bsd', _ctx_1024c, _ctx_1024P)
        _ctx_1024t = _ctx_1024t * jax.lax.rsqrt(jnp.mean(jnp.square(_ctx_1024t)) + 1e-12) * 0.953939
        ctx_1024 = 4.13588e-05 + 0.999923 * (_ctx_1024t + 0.3 * jax.random.normal(jax.random.fold_in(_rk, 611), (4, 154, 128), jnp.float32))
        _validS = jnp.arange(512)[None, :] < _lenS[:, None]
        _validS2 = jnp.arange(154)[None, :] < _lenS2[:, None]
        _causal = jnp.tril(jnp.ones((512, 512), dtype=bool))
        mask_Bx1xSxS2_bk0 = jnp.logical_not(jnp.broadcast_to(_validS2[:, None, None, :], (4, 1, 512, 154)))
        mask_BxS2_ff1 = jnp.where(jnp.ones((4, 154), dtype=bool), 1.0, 0.0).astype(jnp.float32)
        return (x, ctx_1024, mask_Bx1xSxS2_bk0, mask_BxS2_ff1)
    x, ctx_1024, mask_Bx1xSxS2_bk0, mask_BxS2_ff1 = _rec_inputs()

    def _L0_xattn_setup():
        import jax, jax.numpy as jnp
        import numpy as np
        key = jax.random.key(seed)
        k1, k2 = jax.random.split(key)
        hidden_states = jax.random.normal(k1, (8, 512, 128), dtype=jnp.float32)
        visual_hidden_state = jax.random.normal(k2, (8, 128, 128), dtype=jnp.float32)
        return {'hidden_states': hidden_states, 'visual_hidden_state': visual_hidden_state}
    _L0_xattn_all = _L0_xattn_setup()
    _L0_xattn_in = {k: v for k, v in _L0_xattn_all.items() if k in ()}
    del _L0_xattn_all

    def _L0_ffn_setup():
        import jax, jax.numpy as jnp
        import numpy as np
        B, S, D = (2, 128, 128)
        E, H, K, G = (8, 256, 2, 32)
        key = jax.random.key(seed)
        ks = jax.random.split(key, 5)
        return {'x': jax.random.normal(ks[0], (B, S, D), jnp.float32), 'wg1': jax.random.normal(ks[1], (D, G), jnp.float32) * 0.02, 'bg1': jnp.zeros((G,), jnp.float32), 'wg2': jax.random.normal(ks[2], (G, E), jnp.float32) * 0.02, 'w_in': jax.random.uniform(ks[3], (E, D, H), jnp.float32, -1.0 / D, 1.0 / D), 'w_out': jax.random.uniform(ks[4], (E, H, D), jnp.float32, -1.0 / H, 1.0 / H)}
    _L0_ffn_all = _L0_ffn_setup()
    _L0_ffn_in = {k: v for k, v in _L0_ffn_all.items() if k in ('wg1', 'bg1', 'wg2', 'w_in', 'w_out')}
    del _L0_ffn_all

    def _L1_xattn_setup():
        import jax, jax.numpy as jnp
        import numpy as np
        D_MODEL = 128
        N_HEADS = 16
        D_HEAD = D_MODEL // N_HEADS
        B = 4
        S = 256
        NEG_INF = -10000000000.0
        key = jax.random.key(seed)
        ks = jax.random.split(key, 8)
        queries = jax.random.normal(ks[0], (B, S, D_MODEL), dtype=jnp.float32)
        keys = jax.random.normal(ks[1], (B, S, D_MODEL), dtype=jnp.float32)
        values = jax.random.normal(ks[2], (B, S, D_MODEL), dtype=jnp.float32)
        causal = jnp.tril(jnp.ones((S, S), dtype=bool))
        mask = jnp.broadcast_to(causal[None, None, :, :], (B, 1, S, S))
        sc = 1.0 / np.sqrt(D_MODEL)
        W_q = jax.random.normal(ks[3], (D_MODEL, D_MODEL), dtype=jnp.float32) * sc
        W_k = jax.random.normal(ks[4], (D_MODEL, D_MODEL), dtype=jnp.float32) * sc
        W_v = jax.random.normal(ks[5], (D_MODEL, D_MODEL), dtype=jnp.float32) * sc
        W_proj = jax.random.normal(ks[6], (D_MODEL, D_MODEL), dtype=jnp.float32) * sc
        b_proj = jnp.zeros((D_MODEL,), dtype=jnp.float32)
        return {'queries': queries, 'keys': keys, 'values': values, 'mask': mask, 'W_q': W_q, 'W_k': W_k, 'W_v': W_v, 'W_proj': W_proj, 'b_proj': b_proj}
    _L1_xattn_all = _L1_xattn_setup()
    _L1_xattn_in = {k: v for k, v in _L1_xattn_all.items() if k in ('W_q', 'W_k', 'W_v', 'W_proj', 'b_proj')}
    del _L1_xattn_all

    def _L1_ffn_setup():
        import jax, jax.numpy as jnp
        import numpy as np
        B, S, D_MODEL, D_HIDDEN = (4, 256, 128, 512)

        def act_quant(x):
            scale = 127.0 / jnp.clip(jnp.max(jnp.abs(x), axis=-1, keepdims=True), 1e-05)
            return jnp.clip(jnp.round(x * scale), -128, 127) / scale

        def weight_quant(w):
            scale = 1.0 / jnp.clip(jnp.mean(jnp.abs(w)), 1e-05)
            return jnp.clip(jnp.round(w * scale), -1, 1) / scale

        def bit_linear(x, w):
            xq = x + jax.lax.stop_gradient(act_quant(x) - x)
            wq = w + jax.lax.stop_gradient(weight_quant(w) - w)
            return jnp.einsum('bsd,hd->bsh', xq, wq)

        def depthwise_conv1d(x_bcl, w, b):
            y = jax.lax.conv_general_dilated(x_bcl, w, window_strides=(1,), padding=[(1, 1)], dimension_numbers=('NCH', 'OIH', 'NCH'), feature_group_count=x_bcl.shape[1])
            return y + b[None, :, None]
        key = jax.random.key(seed)
        ks = jax.random.split(key, 5)
        lim1 = 1.0 / np.sqrt(D_MODEL)
        lim2 = 1.0 / np.sqrt(D_HIDDEN)
        limc = 1.0 / np.sqrt(3.0)
        return {'x': jax.random.normal(ks[0], (B, S, D_MODEL), dtype=jnp.float32), 'w1': jax.random.uniform(ks[1], (D_HIDDEN, D_MODEL), jnp.float32, -lim1, lim1), 'conv_w': jax.random.uniform(ks[2], (D_HIDDEN, 1, 3), jnp.float32, -limc, limc), 'conv_b': jax.random.uniform(ks[3], (D_HIDDEN,), jnp.float32, -limc, limc), 'w2': jax.random.uniform(ks[4], (D_MODEL, D_HIDDEN), jnp.float32, -lim2, lim2)}
    _L1_ffn_all = _L1_ffn_setup()
    _L1_ffn_in = {k: v for k, v in _L1_ffn_all.items() if k in ('w1', 'conv_w', 'conv_b', 'w2')}
    del _L1_ffn_all

    def _L2_xattn_setup():
        import jax, jax.numpy as jnp
        import numpy as np
        D_MODEL = 128
        HEADS = 16
        DEPTH = D_MODEL // HEADS
        B, S = (4, 512)
        EPS_K = 1e-06
        EPS_LN = 1e-06

        def _layernorm(x, g, b):
            m = jnp.mean(x, axis=-1, keepdims=True)
            var = jnp.var(x, axis=-1, keepdims=True)
            return (x - m) * jax.lax.rsqrt(var + EPS_LN) * g + b

        def _split_heads(x):
            bsz, sl, _ = x.shape
            return x.reshape(bsz, sl, HEADS, DEPTH).transpose(0, 2, 1, 3)
        key = jax.random.key(seed)
        ks = jax.random.split(key, 8)
        lecun = 1.0 / np.sqrt(D_MODEL)
        glorot = np.sqrt(2.0 / (D_MODEL + D_MODEL))
        return {'q': jax.random.normal(ks[0], (B, S, D_MODEL), jnp.float32), 'k': jax.random.normal(ks[1], (B, S, D_MODEL), jnp.float32), 'v': jax.random.normal(ks[2], (B, S, D_MODEL), jnp.float32), 'mask': jnp.ones((B, S), jnp.float32), 'wq': jax.random.normal(ks[3], (D_MODEL, D_MODEL), jnp.float32) * lecun, 'wk': jax.random.normal(ks[4], (D_MODEL, D_MODEL), jnp.float32) * lecun, 'wv': jax.random.normal(ks[5], (D_MODEL, D_MODEL), jnp.float32) * lecun, 'ln_gamma': jnp.ones((D_MODEL,), jnp.float32), 'ln_beta': jnp.zeros((D_MODEL,), jnp.float32), 'dense_w': jax.random.normal(ks[6], (D_MODEL, D_MODEL), jnp.float32) * glorot, 'dense_b': jnp.zeros((D_MODEL,), jnp.float32)}
    _L2_xattn_all = _L2_xattn_setup()
    _L2_xattn_in = {k: v for k, v in _L2_xattn_all.items() if k in ('wq', 'wk', 'wv', 'ln_gamma', 'ln_beta', 'dense_w', 'dense_b')}
    del _L2_xattn_all

    def _L2_ffn_setup():
        import jax, jax.numpy as jnp
        import numpy as np
        H = 128
        I = 128
        E = 8
        key = jax.random.key(seed)
        ks = jax.random.split(key, 8)
        s = 0.02
        x = jax.random.normal(ks[0], (4, 256, H), dtype=jnp.float32)
        Wg = jax.random.normal(ks[1], (H, E), dtype=jnp.float32) * s
        bg = jnp.zeros((E,), dtype=jnp.float32)
        W1 = jax.random.normal(ks[2], (E, H, I), dtype=jnp.float32) * s
        b1 = jnp.zeros((E, I), dtype=jnp.float32)
        W2 = jax.random.normal(ks[3], (E, I, H), dtype=jnp.float32) * s
        b2 = jnp.zeros((E, H), dtype=jnp.float32)
        return {'x': x, 'Wg': Wg, 'bg': bg, 'W1': W1, 'b1': b1, 'W2': W2, 'b2': b2}
    _L2_ffn_all = _L2_ffn_setup()
    _L2_ffn_in = {k: v for k, v in _L2_ffn_all.items() if k in ('Wg', 'bg', 'W1', 'b1', 'W2', 'b2')}
    del _L2_ffn_all

    def _L3_xattn_setup():
        import jax, jax.numpy as jnp
        import numpy as np
        HEADS = 16
        EPS = 1e-06

        def _rmsnorm(x, gamma):
            inv = jax.lax.rsqrt(jnp.mean(x * x, axis=-1, keepdims=True) + EPS)
            return x * inv * gamma
        key = jax.random.key(seed)
        ks = jax.random.split(key, 7)
        B, L, Lc, D, CTX = (4, 512, 128, 128, 128)
        hd = D // HEADS
        s = 1.0 / np.sqrt(D)
        return {'x': jax.random.normal(ks[0], (B, L, D), jnp.float32), 'ctx': jax.random.normal(ks[1], (B, Lc, CTX), jnp.float32), 'Wq': jax.random.normal(ks[2], (D, D), jnp.float32) * s, 'Wkv': jax.random.normal(ks[3], (CTX, 2 * D), jnp.float32) * s, 'Wproj': jax.random.normal(ks[4], (D, D), jnp.float32) * s, 'q_gamma': jnp.ones((hd,), jnp.float32), 'k_gamma': jnp.ones((hd,), jnp.float32)}
    _L3_xattn_all = _L3_xattn_setup()
    _L3_xattn_in = {k: v for k, v in _L3_xattn_all.items() if k in ('Wq', 'Wkv', 'Wproj', 'q_gamma', 'k_gamma')}
    del _L3_xattn_all

    def _L3_ffn_setup():
        import jax, jax.numpy as jnp
        import numpy as np
        B, S, D_MODEL, D_FF = (4, 256, 128, 512)

        def _quantum_transform(hidden, theta, w_real, w_imag):
            imag = w_imag * jnp.sin(theta + hidden * 0.1)
            quantum_phase = jnp.cos(theta) * w_real + jnp.sin(theta) * w_imag
            return hidden + quantum_phase * imag * 0.1
        key = jax.random.key(seed)
        ks = jax.random.split(key, 8)
        return {'x': jax.random.normal(ks[0], (B, S, D_MODEL), dtype=jnp.float32), 'W1': jax.random.normal(ks[1], (D_MODEL, D_FF), dtype=jnp.float32) * (1.0 / np.sqrt(D_MODEL)), 'b1': jnp.zeros((D_FF,), dtype=jnp.float32), 'quantum_phases': jax.random.normal(ks[2], (D_FF,), dtype=jnp.float32) * (2.0 * np.pi), 'quantum_weights_real': jax.random.normal(ks[3], (D_FF,), dtype=jnp.float32) * 0.1, 'quantum_weights_imag': jax.random.normal(ks[4], (D_FF,), dtype=jnp.float32) * 0.1, 'W2': jax.random.normal(ks[5], (D_FF, D_MODEL), dtype=jnp.float32) * (1.0 / np.sqrt(D_FF)), 'b2': jnp.zeros((D_MODEL,), dtype=jnp.float32)}
    _L3_ffn_all = _L3_ffn_setup()
    _L3_ffn_in = {k: v for k, v in _L3_ffn_all.items() if k in ('W1', 'b1', 'quantum_phases', 'quantum_weights_real', 'quantum_weights_imag', 'W2', 'b2')}
    del _L3_ffn_all
    return {'x': x, 'ctx_1024': ctx_1024, 'mask_Bx1xSxS2_bk0': mask_Bx1xSxS2_bk0, 'mask_BxS2_ff1': mask_BxS2_ff1, 'L0_ffn_wg1': _L0_ffn_in['wg1'], 'L0_ffn_bg1': _L0_ffn_in['bg1'], 'L0_ffn_wg2': _L0_ffn_in['wg2'], 'L0_ffn_w_in': _L0_ffn_in['w_in'], 'L0_ffn_w_out': _L0_ffn_in['w_out'], 'L1_xattn_W_q': _L1_xattn_in['W_q'], 'L1_xattn_W_k': _L1_xattn_in['W_k'], 'L1_xattn_W_v': _L1_xattn_in['W_v'], 'L1_xattn_W_proj': _L1_xattn_in['W_proj'], 'L1_xattn_b_proj': _L1_xattn_in['b_proj'], 'L1_ffn_w1': _L1_ffn_in['w1'], 'L1_ffn_conv_w': _L1_ffn_in['conv_w'], 'L1_ffn_conv_b': _L1_ffn_in['conv_b'], 'L1_ffn_w2': _L1_ffn_in['w2'], 'L2_xattn_wq': _L2_xattn_in['wq'], 'L2_xattn_wk': _L2_xattn_in['wk'], 'L2_xattn_wv': _L2_xattn_in['wv'], 'L2_xattn_ln_gamma': _L2_xattn_in['ln_gamma'], 'L2_xattn_ln_beta': _L2_xattn_in['ln_beta'], 'L2_xattn_dense_w': _L2_xattn_in['dense_w'], 'L2_xattn_dense_b': _L2_xattn_in['dense_b'], 'L2_ffn_Wg': _L2_ffn_in['Wg'], 'L2_ffn_bg': _L2_ffn_in['bg'], 'L2_ffn_W1': _L2_ffn_in['W1'], 'L2_ffn_b1': _L2_ffn_in['b1'], 'L2_ffn_W2': _L2_ffn_in['W2'], 'L2_ffn_b2': _L2_ffn_in['b2'], 'L3_xattn_Wq': _L3_xattn_in['Wq'], 'L3_xattn_Wkv': _L3_xattn_in['Wkv'], 'L3_xattn_Wproj': _L3_xattn_in['Wproj'], 'L3_xattn_q_gamma': _L3_xattn_in['q_gamma'], 'L3_xattn_k_gamma': _L3_xattn_in['k_gamma'], 'L3_ffn_W1': _L3_ffn_in['W1'], 'L3_ffn_b1': _L3_ffn_in['b1'], 'L3_ffn_quantum_phases': _L3_ffn_in['quantum_phases'], 'L3_ffn_quantum_weights_real': _L3_ffn_in['quantum_weights_real'], 'L3_ffn_quantum_weights_imag': _L3_ffn_in['quantum_weights_imag'], 'L3_ffn_W2': _L3_ffn_in['W2'], 'L3_ffn_b2': _L3_ffn_in['b2']}

def reference(x, ctx_1024, mask_Bx1xSxS2_bk0, mask_BxS2_ff1, L0_ffn_wg1, L0_ffn_bg1, L0_ffn_wg2, L0_ffn_w_in, L0_ffn_w_out, L1_xattn_W_q, L1_xattn_W_k, L1_xattn_W_v, L1_xattn_W_proj, L1_xattn_b_proj, L1_ffn_w1, L1_ffn_conv_w, L1_ffn_conv_b, L1_ffn_w2, L2_xattn_wq, L2_xattn_wk, L2_xattn_wv, L2_xattn_ln_gamma, L2_xattn_ln_beta, L2_xattn_dense_w, L2_xattn_dense_b, L2_ffn_Wg, L2_ffn_bg, L2_ffn_W1, L2_ffn_b1, L2_ffn_W2, L2_ffn_b2, L3_xattn_Wq, L3_xattn_Wkv, L3_xattn_Wproj, L3_xattn_q_gamma, L3_xattn_k_gamma, L3_ffn_W1, L3_ffn_b1, L3_ffn_quantum_phases, L3_ffn_quantum_weights_real, L3_ffn_quantum_weights_imag, L3_ffn_W2, L3_ffn_b2):
    import jax
    import jax.numpy as jnp

    def _L0_xattn_ref(hidden_states, visual_hidden_state):
        import jax, jax.numpy as jnp
        import numpy as np
        fusion_scores = jnp.einsum('bsd,bvd->bsv', hidden_states, visual_hidden_state)
        fusion_probs = jax.nn.softmax(fusion_scores, axis=-1)
        fusion_output = jnp.einsum('bsv,bvd->bsd', fusion_probs, visual_hidden_state)
        return fusion_output

    def _L0_ffn_ref(x, wg1, bg1, wg2, w_in, w_out):
        import jax, jax.numpy as jnp
        import numpy as np
        B, S, D = (2, 128, 128)
        E, H, K, G = (8, 256, 2, 32)
        b, s, d = x.shape
        xt = x.reshape(-1, d)
        n = xt.shape[0]
        g = jax.nn.gelu(xt @ wg1 + bg1, approximate=False)
        logits = g @ wg2
        probs = jax.nn.softmax(logits, axis=-1)
        top_vals, top_idx = jax.lax.top_k(probs, K)
        gates = jnp.zeros_like(probs).at[jnp.arange(n)[:, None], top_idx].set(top_vals)
        h = jax.nn.gelu(jnp.einsum('nd,edh->enh', xt, w_in), approximate=False)
        o = jnp.einsum('enh,ehd->end', h, w_out)
        y = jnp.einsum('ne,end->nd', gates, o)
        return y.reshape(b, s, d)

    def _L1_xattn_ref(queries, keys, values, mask, W_q, W_k, W_v, W_proj, b_proj):
        import jax, jax.numpy as jnp
        import numpy as np
        D_MODEL = 128
        N_HEADS = 16
        D_HEAD = D_MODEL // N_HEADS
        B = 4
        S = 256
        NEG_INF = -10000000000.0
        b, sq, _ = queries.shape
        Q = (queries @ W_q.T).reshape(b, sq, N_HEADS, D_HEAD).transpose(0, 2, 1, 3)
        K = (keys @ W_k.T).reshape(b, -1, N_HEADS, D_HEAD).transpose(0, 2, 1, 3)
        V = (values @ W_v.T).reshape(b, -1, N_HEADS, D_HEAD).transpose(0, 2, 1, 3)
        scale = jnp.sqrt(jnp.float32(D_HEAD))
        scores = jnp.einsum('bhqd,bhkd->bhqk', Q, K) / scale
        scores = jnp.where(mask, scores, NEG_INF)
        attention = jax.nn.softmax(scores, axis=-1)
        heads_out = jnp.einsum('bhqk,bhkd->bhqd', attention, V)
        heads_out = heads_out.transpose(0, 2, 1, 3).reshape(b, sq, D_MODEL)
        out = heads_out @ W_proj.T + b_proj
        return out

    def _L1_ffn_ref(x, w1, conv_w, conv_b, w2):
        import jax, jax.numpy as jnp
        import numpy as np
        B, S, D_MODEL, D_HIDDEN = (4, 256, 128, 512)

        def act_quant(x):
            scale = 127.0 / jnp.clip(jnp.max(jnp.abs(x), axis=-1, keepdims=True), 1e-05)
            return jnp.clip(jnp.round(x * scale), -128, 127) / scale

        def weight_quant(w):
            scale = 1.0 / jnp.clip(jnp.mean(jnp.abs(w)), 1e-05)
            return jnp.clip(jnp.round(w * scale), -1, 1) / scale

        def bit_linear(x, w):
            xq = x + jax.lax.stop_gradient(act_quant(x) - x)
            wq = w + jax.lax.stop_gradient(weight_quant(w) - w)
            return jnp.einsum('bsd,hd->bsh', xq, wq)

        def depthwise_conv1d(x_bcl, w, b):
            y = jax.lax.conv_general_dilated(x_bcl, w, window_strides=(1,), padding=[(1, 1)], dimension_numbers=('NCH', 'OIH', 'NCH'), feature_group_count=x_bcl.shape[1])
            return y + b[None, :, None]
        h = bit_linear(x, w1)
        h = depthwise_conv1d(h.transpose(0, 2, 1), conv_w, conv_b)
        h = h.transpose(0, 2, 1)
        h = jax.nn.silu(h)
        return bit_linear(h, w2)

    def _L2_xattn_ref(q, k, v, mask, wq, wk, wv, ln_gamma, ln_beta, dense_w, dense_b):
        import jax, jax.numpy as jnp
        import numpy as np
        D_MODEL = 128
        HEADS = 16
        DEPTH = D_MODEL // HEADS
        B, S = (4, 512)
        EPS_K = 1e-06
        EPS_LN = 1e-06

        def _layernorm(x, g, b):
            m = jnp.mean(x, axis=-1, keepdims=True)
            var = jnp.var(x, axis=-1, keepdims=True)
            return (x - m) * jax.lax.rsqrt(var + EPS_LN) * g + b

        def _split_heads(x):
            bsz, sl, _ = x.shape
            return x.reshape(bsz, sl, HEADS, DEPTH).transpose(0, 2, 1, 3)
        bsz = q.shape[0]
        em = mask[:, None, :, None]
        qh = _split_heads(_layernorm(q @ wq, ln_gamma, ln_beta))
        kh = _split_heads(_layernorm(k @ wk, ln_gamma, ln_beta))
        vh = _split_heads(_layernorm(v @ wv, ln_gamma, ln_beta))
        q_prime = jax.nn.relu(qh) + EPS_K
        k_prime = (jax.nn.relu(kh) + EPS_K) * em
        vh = vh * em
        kv = jnp.einsum('bhnd,bhne->bhde', k_prime, vh)
        z = 1.0 / (jnp.einsum('bhnd,bhd->bhn', q_prime, k_prime.sum(axis=-2)) + EPS_K)
        att = jnp.einsum('bhnd,bhde,bhn->bhne', q_prime, kv, z)
        att = att.reshape(bsz, -1, D_MODEL)
        out = att @ dense_w + dense_b
        return _layernorm(out, ln_gamma, ln_beta)

    def _L2_ffn_ref(x, Wg, bg, W1, b1, W2, b2):
        import jax, jax.numpy as jnp
        import numpy as np
        H = 128
        I = 128
        E = 8
        B, S, Hd = x.shape
        xf = x.reshape(-1, Hd)
        logits = xf @ Wg + bg
        gates = jax.nn.softmax(logits, axis=-1)
        idx = jnp.argmax(gates, axis=-1)
        h = jax.nn.gelu(jnp.einsum('th,ehi->tei', xf, W1) + b1, approximate=False)
        y = jnp.einsum('tei,eih->teh', h, W2) + b2
        out = jnp.take_along_axis(y, idx[:, None, None], axis=1)[:, 0, :]
        return out.reshape(B, S, Hd)

    def _L3_xattn_ref(x, ctx, Wq, Wkv, Wproj, q_gamma, k_gamma):
        import jax, jax.numpy as jnp
        import numpy as np
        HEADS = 16
        EPS = 1e-06

        def _rmsnorm(x, gamma):
            inv = jax.lax.rsqrt(jnp.mean(x * x, axis=-1, keepdims=True) + EPS)
            return x * inv * gamma
        B, L, D = x.shape
        Lc = ctx.shape[1]
        H = HEADS
        hd = D // H
        q = (x @ Wq).reshape(B, L, H, hd).transpose(0, 2, 1, 3)
        kv = (ctx @ Wkv).reshape(B, Lc, 2, H, hd).transpose(2, 0, 3, 1, 4)
        k, v = (kv[0], kv[1])
        q = _rmsnorm(q, q_gamma)
        k = _rmsnorm(k, k_gamma)
        scale = 1.0 / np.sqrt(hd)
        attn = jnp.einsum('bhld,bhmd->bhlm', q, k) * scale
        attn = jax.nn.softmax(attn, axis=-1)
        out = jnp.einsum('bhlm,bhmd->bhld', attn, v)
        out = out.transpose(0, 2, 1, 3).reshape(B, L, D)
        return out @ Wproj

    def _L3_ffn_ref(x, W1, b1, quantum_phases, quantum_weights_real, quantum_weights_imag, W2, b2):
        import jax, jax.numpy as jnp
        import numpy as np
        B, S, D_MODEL, D_FF = (4, 256, 128, 512)

        def _quantum_transform(hidden, theta, w_real, w_imag):
            imag = w_imag * jnp.sin(theta + hidden * 0.1)
            quantum_phase = jnp.cos(theta) * w_real + jnp.sin(theta) * w_imag
            return hidden + quantum_phase * imag * 0.1
        hidden = jnp.einsum('bsd,df->bsf', x, W1) + b1
        q = _quantum_transform(hidden, quantum_phases, quantum_weights_real, quantum_weights_imag)
        act = jax.nn.relu(q)
        return jnp.einsum('bsf,fd->bsd', act, W2) + b2
    x = x + _L0_xattn_ref(_layernorm(x, axis=-1), ctx_1024)
    x = x + _L0_ffn_ref(_layernorm(x, axis=-1), L0_ffn_wg1, L0_ffn_bg1, L0_ffn_wg2, L0_ffn_w_in, L0_ffn_w_out)
    x = x + _L1_xattn_ref(_layernorm(x, axis=-1), ctx_1024, ctx_1024, mask_Bx1xSxS2_bk0, L1_xattn_W_q, L1_xattn_W_k, L1_xattn_W_v, L1_xattn_W_proj, L1_xattn_b_proj)
    x = x + _L1_ffn_ref(_layernorm(x, axis=-1), L1_ffn_w1, L1_ffn_conv_w, L1_ffn_conv_b, L1_ffn_w2)
    x = x + _L2_xattn_ref(_layernorm(x, axis=-1), ctx_1024, ctx_1024, mask_BxS2_ff1, L2_xattn_wq, L2_xattn_wk, L2_xattn_wv, L2_xattn_ln_gamma, L2_xattn_ln_beta, L2_xattn_dense_w, L2_xattn_dense_b)
    x = x + _L2_ffn_ref(_layernorm(x, axis=-1), L2_ffn_Wg, L2_ffn_bg, L2_ffn_W1, L2_ffn_b1, L2_ffn_W2, L2_ffn_b2)
    x = x + _L3_xattn_ref(_layernorm(x, axis=-1), ctx_1024, L3_xattn_Wq, L3_xattn_Wkv, L3_xattn_Wproj, L3_xattn_q_gamma, L3_xattn_k_gamma)
    x = x + _L3_ffn_ref(_layernorm(x, axis=-1), L3_ffn_W1, L3_ffn_b1, L3_ffn_quantum_phases, L3_ffn_quantum_weights_real, L3_ffn_quantum_weights_imag, L3_ffn_W2, L3_ffn_b2)
    return x

_drawn_inputs = setup_inputs


def setup_inputs(seed=0):
    import zlib

    import numpy as np

    out = dict(_drawn_inputs(seed))
    spreads = {'L0_ffn_bg1': (0.0, 0.8),
     'L1_xattn_b_proj': (0.0, 0.1),
     'L2_xattn_ln_gamma': (1.0, 0.2),
     'L2_xattn_ln_beta': (0.0, 0.1),
     'L2_xattn_dense_b': (0.0, 0.1),
     'L2_ffn_bg': (0.0, 0.1),
     'L2_ffn_b1': (0.0, 0.8),
     'L2_ffn_b2': (0.0, 0.1),
     'L3_xattn_q_gamma': (1.0, 0.6),
     'L3_xattn_k_gamma': (1.0, 0.549),
     'L3_ffn_b1': (0.0, 0.274),
     'L3_ffn_b2': (0.0, 0.1)}
    factors = {'L0_ffn_wg1': 8.0,
     'L0_ffn_wg2': 8.0,
     'L0_ffn_w_in': 8.0,
     'L0_ffn_w_out': 8.0,
     'L2_ffn_W1': 4.596,
     'L2_ffn_W2': 4.204,
     'L3_ffn_quantum_phases': 33.548,
     'L3_ffn_quantum_weights_real': 64.0,
     'L3_ffn_quantum_weights_imag': 26.028}
    for name, (base, spread) in spreads.items():
        noise = np.random.default_rng([zlib.crc32(name.encode()), seed]).standard_normal(out[name].shape)
        drawn = base * np.exp(spread * noise) if base else spread * noise
        out[name] = jnp.asarray(drawn.astype(out[name].dtype))
    for name, factor in factors.items():
        out[name] = (out[name] * factor).astype(out[name].dtype)
    return out
```

```python
from contextlib import ExitStack

import numpy as np

import concourse.bass as bass
from concourse import mybir

F32 = mybir.dt.float32
F32R = mybir.dt.float32r
BF16 = mybir.dt.bfloat16
U8 = mybir.dt.uint8
U32 = mybir.dt.uint32
ALU = mybir.AluOpType
ACT = mybir.ActivationFunctionType
AX = mybir.AxisListType.X

P = 128
NB, S, D = 4, 512, 128
T = S // P
C = 154
CR = C - P
H, E8 = 16, 8
G, J = 4, 4
W = 32
NE = 8
HID0 = 256
FF = 512
NH = FF // P
SLOTS, ROUNDS = 2, 2
RING = 4
CH = 3
NCH = -(-H // CH)
NPT = 10
NHT = 8
BIG = 2.0 ** 100
MAGIC = 1.5 * 2.0 ** 23
TWO_PI = 2 * np.pi
PI_A, PI_B = 6.28125, 0.0019350051879882812
PI_C = float(TWO_PI - PI_A - PI_B)
SIN_SCALE = 6.283185
RSQ8 = float(1 / np.sqrt(8.0))

XT_ORDER = {0: 0, 1: 1, 2: 2, 4: 3, 5: 4, 6: 5, 7: 6}

FILLS = {1: (14, 2), 2: (50, 20), 3: (118, 82), 4: (130, 100), 5: (136, 112), 6: (156, 132), 7: (224, 194), 8: (234, 196)}
NLN = {1: 2, 2: 4, 3: 6, 4: 8, 5: 16, 6: 18, 7: 20, 8: 22}

CONSTS = {}
_at = 0
for _n, _w in (("ident", 128), ("blk", 128), ("rsel", 128), ("ind16", 16), ("jind", 16), ("jrem", 16), ("ind4", 4), ("desc", 8)):
    CONSTS[_n] = (_at, _at + _w)
    _at += _w
NCONST = _at


def constants():
    c = np.zeros((P, NCONST), np.float32)
    p = np.arange(P)[:, None]

    def put(name, v):
        a, b = CONSTS[name]
        c[:, a:b] = v

    q = np.arange(P)[None]
    put("ident", p == q)
    put("blk", p // E8 == q // E8)
    put("rsel", (q % W == p) & (p < CR))
    h = np.arange(H)[None]
    put("ind16", p // E8 == h)
    put("jind", p // W == h % J)
    put("jrem", (p // W == h % J) & (p % W < CR))
    put("ind4", p // W == np.arange(J)[None])
    put("desc", NE - np.arange(NE)[None] + 0 * p)
    return c


def build(nc, t, out, last_layer=8):
    ctx = ExitStack()
    with ctx:
        def sb(name, shape, dt=F32):
            return ctx.enter_context(nc.sbuf_tensor(name, shape, dt))

        def sem(name):
            return ctx.enter_context(nc.semaphore(name))

        bank_a = [ctx.enter_context(nc.psum_tensor(f"act_bank{i}", [P, 512], F32)) for i in range(RING)]
        bank_v = [ctx.enter_context(nc.psum_tensor(f"dve_bank{i}", [P, 512], F32)) for i in range(RING)]

        consts = sb("consts", [P, NCONST])

        def const(name):
            a, b = CONSTS[name]
            return consts[:, a:b]

        ident = const("ident")
        ident_bf = sb("ident_bf", [P, P], BF16)
        rsel_bf = sb("rsel_bf", [P, P], BF16)
        ones_row = sb("ones_row", [P, P])

        two = lambda name, shape, dt=F32: [sb(f"{name}{s}", shape, dt) for s in range(SLOTS)]
        X = two("X", [P, T, D])
        XN = two("XN", [P, T, D])
        XT = two("XT", [P, S])
        CT = two("CT", [P, C])
        CT4 = two("CT4", [P, J, W])
        CN = two("CN", [P, D])
        CL = two("CL", [CR, D])
        MRAW = two("MRAW", [P, T * C // 4], U32)
        MTRAW = two("MTRAW", [P, S // 4], U32)
        MLRAW = two("MLRAW", [CR, S // 4], U32)
        MN = two("MN", [P, T, C], BF16)
        MT = two("MT", [P, S], BF16)
        ML = two("ML", [CR, S], BF16)
        EM = two("EM", [P, 2])
        KBN = two("KBN", [P, H, C], F32R)
        KBM = two("KBM", [P, G, J, P], F32R)
        KBL = two("KBL", [P, G, J, W], F32R)
        VA = two("VA", [P, H, W])
        VL = two("VL", [P, H, W])
        QTC = two("QTC", [P, S], F32R)
        QN = two("QN", [P, T, H, W])
        KVB = two("KVB", [P, D + H])
        GATE = two("GATE", [P, T, NE])

        QH = sb("QH", [P, T, D], F32R)
        KH = sb("KH", [P, 2, D], F32R)
        KN = sb("KN", [P, H, W])
        KNL = sb("KNL", [CR, H, W])
        KTC = sb("KTC", [P, C])
        KS = sb("KS", [P, G, C])
        QS = [sb(f"QS{i}", [P, S], F32R) for i in range(2)]
        PT = sb("PT", [P, NPT, S])
        HT = sb("HT", [P, NHT, S])
        UT = sb("UT", [P, 2, S])
        K2 = sb("K2", [P, 4, D])
        V2 = sb("V2", [P, 2, D + 1])
        SQ = sb("SQ", [P, T, D])
        HP = sb("HP", [P, NH, S + 2])
        sn = PT[:, 0:4, :]
        CV = PT[:, 4:8, :]
        PNT, PNL = PT[:, 8, :], PT[0:CR, 9, :]
        GT, OHT, SB_ = UT[0:32, 0, :], UT[0:NE, 1, :], UT[:, 0, :]
        AT = UT[:, 1, :]
        HEADS_T = [HT[:, s, :] for s in range(SLOTS)]
        GROUPS_T = [HT[:, 4 + s, :] for s in range(SLOTS)]
        exchange = [nc.dram_tensor(f"exchange{s}", [P, S], F32).ap() for s in range(SLOTS)]
        ATT = HT[:, 7, :].rearrange("p (t d) -> p t d", t=T)
        Q32 = HT[:, 6, :].rearrange("p (t d) -> p t d", t=T)
        PN = PT[:, 0:2, :].rearrange("p a n -> p (a n)")[:, 0:T * C].rearrange("p (t c) -> p t c", t=T)
        XQ = [HT[:, 4, :].bitcast(BF16)[:, s * S:(s + 1) * S].rearrange("p (t d) -> p t d", t=T) for s in range(SLOTS)]
        XQT = HT[:, 5, :].bitcast(BF16)[:, 0:S]
        ht_bf = HT[:, 0:4, :].bitcast(BF16)
        ZQ = ht_bf[:, 0:2, :].rearrange("p a (b n) -> p (a b) n", b=2)
        ZT = ht_bf[:, 2:4, :].rearrange("p a (b n) -> p (a b) n", b=2)
        stats = sb("stats", [P, T, 6])
        mv = sb("mv", [P, T, 2])
        var = sb("var", [P, T])
        rstd = sb("rstd", [P, T])
        mhalf = sb("mhalf", [P, T])
        mx = sb("mx", [P, T])
        sums = sb("sums", [P, T])
        rsum = sb("rsum", [P, T])
        r16 = sb("r16", [P, T, J])
        den = sb("den", [P, 2, H])
        ms = sb("ms", [P, T * H])
        msk = sb("msk", [P, 2 * H])
        lg = sb("lg", [P, 8, T, NE])
        gm = sb("gm", [P, 8, T])
        amax = sb("amax", [P, 5, T])
        th = sb("th", [P, 12, NH])

        wshape = dict(
            wg1=[D, 32], bg1=[32, 1], wg2=[32, NE], w_in=[D, NE, HID0], w_out=[P, 2 * NE, D],
            wq1=[D, D], wkv1=[D, 2, D], wp1=[D, D], bp1=[P, D],
            cw=[P, NH, 3], cb=[P, NH],
            wq2=[D, D], wkv2=[D, 2, D], lng=[P, D], lnb=[P, D], wd2=[D, D], bd2=[P, D],
            wg=[D, NE], bg=[P, NE], w1e=[D, NE, P], b1e=[P, NE], w2e=[P, NE, D], b2e=[NE, D],
            wq3=[D, D], wkv3=[D, 2 * D], wp3=[D, D], qg=[P, E8], kg=[P, E8],
            w13=[D, FF], b13=[P, NH], ph=[P, NH], wr=[P, NH], wi=[P, NH], w23=[P, NH, D], b23=[P, D],
        )
        w = {k: sb("w_" + k, v) for k, v in wshape.items()}
        w["w1b"], w["w2b"] = PT[:, 0, :], PT[:, 1, :].rearrange("p (k d) -> p k d", k=NH)
        w1q = sb("w1q", [D, FF], BF16)
        w2q = sb("w2q", [P, NH, D], BF16)
        wsum = sb("wsum", [P, 8])
        gk = sb("gk", [P, E8])

        per_round = {}

        class Signal:
            def __init__(self, name, n):
                self.sem, self.n, self.name = sem(name), n, name
                per_round[name] = n
                self.seen = 0

            def at(self, rnd, n, step=1):
                assert 1 <= n <= self.n, (self.name, n)
                return rnd * (self.n * step) + n * step

        L = last_layer
        fills_a, fills_v = FILLS[L]
        act_filled, act_free = Signal("act_bank_filled", fills_a), Signal("act_bank_free", fills_a)
        dve_filled, dve_free = Signal("dve_bank_filled", fills_v), Signal("dve_bank_free", fills_v)
        loaded = [sem(n) for n in ("first_weights_loaded", "layer0_weights_loaded", "weights_loaded")]
        consts_loaded = sem("consts_loaded")
        setup_pool = sem("setup_pool")
        setup_dve = sem("setup_dve")
        setup_act = sem("setup_act")
        setup_pe = sem("setup_pe")
        n_heads = 2 * ((L > 2) + (L > 6))
        x_done = Signal("x_done", 2)
        x_loaded = [Signal(f"x_loaded{s}", 1) for s in range(SLOTS)]
        ctx_loaded = [Signal(f"ctx_loaded{s}", 5 + J) for s in range(SLOTS)]
        mask_loaded = [Signal(f"mask_loaded{s}", 3) for s in range(SLOTS)]
        stored = [Signal(f"stored{s}", 1) for s in range(SLOTS)]
        mask_ready = Signal("mask_ready", 2)
        ln_var = Signal("ln_var", NLN[L])
        ln_rstd = Signal("ln_rstd", NLN[L])
        xn_ready = Signal("xn_ready", 2 * L)
        x_added = Signal("x_added", 2 * (L > 2) + 2 * (L > 7))
        dve_step = sem("dve_step")
        act_step = sem("act_step")
        pool_step = sem("pool_step")
        pool_waited = sem("pool_waited")
        l0_shift = Signal("l0_shift", 2 * T)
        l0_shifted = Signal("l0_shifted", 2)
        l0_exps = Signal("l0_exps", 2)
        kn_ready = Signal("kn_ready", n_heads)
        kh_ready = Signal("kh_ready", n_heads)
        kbn_ready = Signal("kbn_ready", n_heads)
        kb_ready = Signal("kb_ready", n_heads)
        kms_ready = Signal("kms_ready", 2)
        krt_ready = Signal("krt_ready", 2)
        qms_ready = Signal("qms_ready", 2)
        qrt_ready = Signal("qrt_ready", 2)
        qh_ready = Signal("qh_ready", n_heads)
        qhh_ready = Signal("qhh_ready", n_heads)
        max_done = Signal("max_done", n_heads * T)
        att_ready = Signal("att_ready", n_heads + 2 * (L > 4))
        exchange_written = Signal("exchange_written", 2)
        exchange_read = [Signal(f"exchange_read{s}", H) for s in range(SLOTS)]
        xq_ready = Signal("xq_ready", 2)
        rs_ready = Signal("rs_ready", 2)
        hp_ready = Signal("hp_ready", 2 * NH)
        tap_ready = Signal("tap_ready", 2 * NH)
        conv_ready = Signal("conv_ready", 2 * NH)
        z_ready = Signal("z_ready", 2 * NH)
        zq_ready = Signal("zq_ready", 2 * T)
        kv2_ready = Signal("kv2_ready", 2)
        kvb_ready = Signal("kvb_ready", 2)
        to_pool2 = Signal("to_pool2", 6)
        gamma_done = Signal("gamma_done", 6)
        pool2 = Signal("pool2", 6)
        q2_ready = Signal("q2_ready", 2)
        oh_ready = Signal("oh_ready", 2)
        turn_ready = Signal("turn_ready", 2 * NH)
        phase_ready = Signal("phase_ready", 2 * NH)
        relu_ready = Signal("relu_ready", 2 * NH)
        sin_ready = Signal("sin_ready", 2 * NH)

        block = ctx.enter_context(nc.Block())

        a_no, v_no = {}, {}

        def drained(sig, rnd, n):
            return rnd * sig.n + RING + n + 1

        def free_value(sig, rnd, n):
            return rnd * sig.n + max(RING, n + 1)

        r = lambda n, pat, **k: t[n].rearrange(pat, **k)
        row = lambda n: t[n].rearrange("(o n) -> o n", o=1).broadcast_to([P, t[n].shape[0]])
        wsrc = [[
            (w["w1b"], t["w1b"]), (w["w2b"], r("w2b", "(k p) d -> p k d", p=P)),
            (w["qg"][:], row("qg")), (w["kg"][:], row("kg")),
            (w["b13"][:], t["b13"]), (w["ph"][:], t["ph"]),
            (w["wr"][:], t["wr"]), (w["wi"][:], t["wi"]),
        ], [
            (w["wg1"][:], t["wg1"]), (w["bg1"][:], t["bg1"]), (w["wg2"][:], t["wg2"]),
            (w["w_in"][:], r("w_in", "e d h -> d e h")), (w["w_out"][:], r("w_out", "e (k p) d -> p (e k) d", p=P)),
        ], [
            (w["wkv1"][:, 0, :], t["wk1"]), (w["wkv1"][:, 1, :], t["wv1"]), (w["wq1"][:], t["wq1"]),
            (w["wp1"][:], t["wp1"]), (w["bp1"][:], row("bp1")),
            (w["cw"][:], t["cw"]), (w["cb"][:], t["cb"]),
            (w["wq2"][:], t["wq2"]), (w["wkv2"][:, 0, :], t["wk2"]), (w["wkv2"][:, 1, :], t["wv2"]),
            (w["lng"][:], row("lng")), (w["lnb"][:], row("lnb")), (w["wd2"][:], t["wd2"]), (w["bd2"][:], row("bd2")),
            (w["wg"][:], t["wg"]), (w["bg"][:], row("bg")), (w["w1e"][:], r("w1e", "e d h -> d e h")),
            (w["b1e"][:], t["b1e"]), (w["w2e"][:], r("w2e", "e h d -> h e d")), (w["b2e"][:], t["b2e"]),
            (w["wq3"][:], t["wq3"]), (w["wkv3"][:], t["wkv3"]), (w["wp3"][:], t["wp3"]),
            (w["w13"][:], t["w13"]),
            (w["w23"][:], r("w23", "(k p) d -> p k d", p=P)), (w["b23"][:], row("b23")),
        ]]

        def wait_weights(eng, k):
            eng.wait_ge(loaded[k], 16 * len(wsrc[k]))

        @block.tensor
        def _(pe):
            pe.wait_ge(consts_loaded, 16)
            pe.wait_ge(setup_pool, 2)
            pe.wait_ge(setup_dve, 1)
            pe.matmul(bank_v[0][:, 0:2], ones_row[:], wsum[:, 0:2], start=True, stop=True).then_inc(setup_pe, 1)
            pe.wait_ge(setup_dve, 3)

            with pe.Fori(0, ROUNDS) as rnd:
                n_a, n_v = [0], [0]

                def open_a(*holds):
                    a_no[holds] = n_a[0]
                    pe.wait_ge(act_free.sem, free_value(act_free, rnd, n_a[0]))
                    n_a[0] += 1
                    return bank_a[(n_a[0] - 1) % RING]

                def open_v(*holds):
                    v_no[holds] = n_v[0]
                    pe.wait_ge(dve_free.sem, free_value(dve_free, rnd, n_v[0]))
                    n_v[0] += 1
                    return bank_v[(n_v[0] - 1) % RING]

                def wait_a(*holds):
                    pe.wait_ge(act_free.sem, drained(act_free, rnd, a_no[holds]))

                def wait_v(*holds):
                    pe.wait_ge(dve_free.sem, drained(dve_free, rnd, v_no[holds]))

                def mm(o, lhs, rhs, start=True, stop=True, **k):
                    return pe.matmul(o, lhs, rhs, start=start, stop=stop, **k)

                def tr(o, i, id_=None):
                    k = i.shape[0]
                    return pe.matmul(o, i, (ident if id_ is None else id_)[0:k, 0:k], start=True, stop=True, is_transpose=True)

                def four_transposes(holds, src, rows=P):
                    b = open_a(*holds)
                    for i in range(T):
                        last = tr(b[0:rows, i * P:(i + 1) * P], src(i))
                    last.then_inc(act_filled.sem, 1)

                def norm_t(layer, s):
                    pe.wait_ge(xn_ready.sem, xn_ready.at(rnd, 2 * layer + s + 1))
                    four_transposes(("XT", layer, s), lambda i: XN[s][:, i, :])

                def wait_xt(layer, s):
                    wait_a("XT", layer, s)

                def tile(a, i):
                    return a[:, i * P:(i + 1) * P]

                def project(holds, src, wt):
                    b = open_v(*holds)
                    for i in range(T):
                        last = mm(tile(b, i), tile(src, i), wt)
                    last.then_inc(dve_filled.sem, 1)

                def l0_attention(s):
                    wait_xt(0, s)
                    pe.wait_ge(ctx_loaded[s].sem, rnd * ctx_loaded[s].n * 16 + 16 * ctx_loaded[s].n)
                    for i in range(T):
                        b = open_a("l0_scores", s, i)
                        mm(b[:, 0:C], tile(XT[s], i), CT[s][:]).then_inc(act_filled.sem, 1)
                    wait_a("l0_scores", s, T - 1)
                    four_transposes(("PNT", s), lambda i: PN[:, i, 0:P])
                    four_transposes(("PNL", s), lambda i: PN[:, i, P:C], CR)
                    wait_a("PNL", s)
                    b = open_v("l0_out", s)
                    for i in range(T):
                        mm(tile(b, i), tile(PNT, i), CN[s][:], stop=False)
                        last = mm(tile(b, i), tile(PNL, i), CL[s][:], start=False)
                    last.then_inc(dve_filled.sem, 1)

                def expert_up(n, s, wt):
                    b = open_a("hidden", n)
                    mm(b[:], wt, XT[s][:]).then_inc(act_filled.sem, 1)

                def expert_down(n, wts):
                    b = open_v("down", n)
                    wait_a("hidden", n + len(wts) - 1)
                    for i in range(T):
                        for k, wt in enumerate(wts):
                            last = mm(tile(b, i), tile(HT[:, (n + k) % NHT, :], i), wt, start=k == 0, stop=k == len(wts) - 1)
                    last.then_inc(dve_filled.sem, 1)

                def l0_ffn(s):
                    wait_xt(1, s)
                    b = open_a("GT", s)
                    mm(b[0:32, :], w["wg1"][:], XT[s][:]).then_inc(act_filled.sem, 1)
                    base = s * 2 * NE
                    up = lambda e: [expert_up(base + 2 * e + k, s, w["w_in"][:, e, k * P:(k + 1) * P]) for k in range(2)]
                    up(0)
                    wait_a("GT", s)
                    b = open_v("l0_logits", s)
                    for i in range(T):
                        last = mm(b[:, i * NE:(i + 1) * NE], GT[:, i * P:(i + 1) * P], w["wg2"][:])
                    last.then_inc(dve_filled.sem, 1)
                    for e in range(NE):
                        if e + 1 < NE:
                            up(e + 1)
                        expert_down(base + 2 * e, [w["w_out"][:, 2 * e + k, :] for k in range(2)])

                def kv_products(a, s):
                    wk, wv = (w["wkv1"][:, 0, :], w["wkv1"][:, 1, :]) if a == 0 else (w["wkv3"][:, 0:D], w["wkv3"][:, D:2 * D])
                    b = open_v("kv", a, s)
                    mm(b[:, 0:128], CT[s][:, 0:P], wk)
                    mm(b[:, 128:256], CT[s][:, 0:P], wv)
                    mm(b[0:CR, 256:384], CT[s][:, P:C], wk)
                    mm(b[:, 384:512], CT4[s][:, :, :].rearrange("p j w -> p (j w)"), wv).then_inc(dve_filled.sem, 1)

                def k_transposes(a, s):
                    n = 2 * a + s + 1
                    pe.wait_ge(kh_ready.sem, kh_ready.at(rnd, n))
                    b = open_a("KTC", a, s)
                    tr(b[:, 0:P], KH[:, 0, :].bitcast(F32))
                    tr(b[:, P:C], KH[0:CR, 1, :].bitcast(F32)).then_inc(act_filled.sem, 1)
                    pe.wait_ge(kn_ready.sem, kn_ready.at(rnd, n))
                    for g0, g1 in ((0, 3), (3, G)):
                        b = open_a("KS", a, s, g0)
                        for g in range(g0, g1):
                            o = (g - g0) * C
                            tr(b[:, o:o + P], KN[:, J * g:J * g + J, :].rearrange("p j w -> p (j w)"))
                            last = tr(b[:, o + P:o + C], KNL[:, J * g:J * g + J, :].rearrange("p j w -> p (j w)"))
                        last.then_inc(act_filled.sem, 1)

                def queries(a, s):
                    norm_t(2 if a == 0 else 6, s)
                    wait_xt(2 if a == 0 else 6, s)
                    project(("q", a, s), XT[s], w["wq1"][:] if a == 0 else w["wq3"][:])
                    pe.wait_ge(qh_ready.sem, qh_ready.at(rnd, 2 * a + s + 1))
                    four_transposes(("QTC", a, s), lambda i: QH[:, i, :].bitcast(F32))
                    wait_a("QTC", a, s)
                    pe.wait_ge(kbn_ready.sem, kbn_ready.at(rnd, 2 * a + s + 1))
                    if a == 0:
                        pe.wait_ge(mask_ready.sem, mask_ready.at(rnd, s + 1))

                def natural_scores(a, s, i):
                    for c in range(NCH):
                        n = min(CH, H - c * CH)
                        b = open_v("natural", a, s, i, c)
                        o = b[:, 0:n * C]
                        last = mm(o, tile(QTC[s], i), KBN[s][:, c * CH:c * CH + n, :], stop=a == 1)
                        if a == 0:
                            m = MN[s][:, i:i + 1, :].broadcast_to([P, n, C])
                            last = mm(o, ident_bf[:], m, start=False)
                        last.then_inc(dve_filled.sem, 1)

                def split_queries(a, s, g):
                    if g == 0:
                        pe.wait_ge(max_done.sem, max_done.at(rnd, (2 * a + s + 1) * T))
                        pe.wait_ge(qhh_ready.sem, qhh_ready.at(rnd, 2 * a + s + 1))
                        pe.wait_ge(kb_ready.sem, kb_ready.at(rnd, 2 * a + s + 1))
                    four_transposes(("QS", a, s, g), lambda i: QN[s][:, i, J * g:J * g + J, :].rearrange("p j w -> p (j w)"))

                def scores(a, s, g):
                    n = (2 * a + s) * G + g
                    wait_a("QS", a, s, g)
                    q = QS[n % 2]
                    for j in range(J):
                        b = open_a("scores", a, s, g, j)
                        last = mm(b[:], KBM[s][:, g, j, :], q[:], stop=a == 1)
                        if a == 0:
                            last = mm(b[:], ident_bf[:], MT[s][:], start=False)
                        last.then_inc(act_filled.sem, 1)
                    b = open_a("scores", a, s, g, J)
                    last = mm(b[:], KBL[s][:, g, :, :].rearrange("p j w -> p (j w)"), q[:], stop=a == 1)
                    if a == 0:
                        last = mm(b[:], rsel_bf[0:CR, :], ML[s][:], start=False)
                    last.then_inc(act_filled.sem, 1)

                def values(a, s, g):
                    n = (2 * a + s) * G + g
                    if g == 0:
                        wait_v("kv", a, s)
                    b = open_a("UT", a, s, g)
                    base = (n % 2) * (J + 1)
                    wait_a("scores", a, s, g, J)
                    for j in range(J):
                        mm(b[W * j:W * j + W, :], VA[s][:, J * g + j, :], PT[:, base + j, :], stop=False, tile_position=(0, W * j))
                    for j in range(J):
                        last = mm(b[W * j:W * j + W, :], VL[s][:, J * g + j, :], PT[:, base + J, :], start=False, tile_position=(0, W * j))
                    last.then_inc(act_filled.sem, 1)

                def heads_back(a, s, g):
                    n = (2 * a + s) * G + g
                    wait_a("UT", a, s, g)
                    b = open_v("heads", a, s, g)
                    for i in range(T):
                        last = tr(tile(b, i), tile(UT[:, n % 2, :], i))
                    last.then_inc(dve_filled.sem, 1)

                def attention_out(n, wt):
                    pe.wait_ge(att_ready.sem, att_ready.at(rnd, n + 1))
                    four_transposes(("AT", n), lambda i: ATT[:, i, :])
                    wait_a("AT", n)
                    project(("att_out", n), AT, wt)

                def attention(a):
                    queries(a, 0)
                    for i in range(T):
                        natural_scores(a, 0, i)
                    queries(a, 1)
                    for s in range(SLOTS):
                        split_queries(a, s, 0)
                        for g in range(G + 2):
                            if s == 0 and g < T:
                                natural_scores(a, 1, g)
                            if g + 1 < G:
                                split_queries(a, s, g + 1)
                            if g < G:
                                scores(a, s, g)
                            if 1 <= g <= G:
                                values(a, s, g - 1)
                            if g >= 2:
                                heads_back(a, s, g - 2)
                        attention_out(4 * a + s, w["wp1"][:] if a == 0 else w["wp3"][:])

                def l1_ffn(s):
                    pe.wait_ge(xq_ready.sem, xq_ready.at(rnd, s + 1))
                    b = open_a("XQT", s)
                    for i in range(T):
                        last = tr(b[:].bitcast(BF16)[:, i * P:(i + 1) * P], XQ[s][:, i, :], ident_bf)
                    last.then_inc(act_filled.sem, 1)
                    pe.wait_ge(rs_ready.sem, rs_ready.at(rnd, s + 1))
                    b = open_a("SBC", s)
                    for i in range(T):
                        last = mm(tile(b, i), amax[:, 3 + s, i:i + 1].broadcast_to([P, P]), ident)
                    last.then_inc(act_filled.sem, 1)
                    wait_a("XQT", s)
                    for k in range(NH):
                        b = open_v("l1_hidden", s, k)
                        mm(b[:], w1q[:, k * P:(k + 1) * P], XQT[:]).then_inc(dve_filled.sem, 1)
                    for i in range(T):
                        b = open_v("z", s, i)
                        for k in range(NH):
                            if i == 0:
                                pe.wait_ge(z_ready.sem, z_ready.at(rnd, s * NH + k + 1))
                            last = tr(tile(b, k), CV[:, k, i * P:(i + 1) * P])
                        last.then_inc(dve_filled.sem, 1)
                    for i in range(T):
                        b = open_a("ZT", s, i)
                        pe.wait_ge(zq_ready.sem, zq_ready.at(rnd, s * T + i + 1))
                        for k in range(NH):
                            last = tr(b[:].bitcast(BF16)[:, k * P:(k + 1) * P], ZQ[:, i, k * P:(k + 1) * P], ident_bf)
                        last.then_inc(act_filled.sem, 1)
                    b = open_v("l1_out", s)
                    for i in range(T):
                        wait_a("ZT", s, i)
                        for k in range(NH):
                            last = mm(tile(b, i), ZT[:, k, i * P:(i + 1) * P], w2q[:, k, :], start=k == 0, stop=k == NH - 1)
                    last.then_inc(dve_filled.sem, 1)

                def kv2_products(s):
                    b = open_v("kv2", s)
                    r = w["wkv2"][:].rearrange("p i d -> p (i d)")
                    mm(b[:, 0:256], CT[s][:, 0:P], r)
                    mm(b[0:CR, 256:512], CT[s][:, P:C], r).then_inc(dve_filled.sem, 1)

                def kv2_sum(s):
                    pe.wait_ge(kv2_ready.sem, kv2_ready.at(rnd, s + 1))
                    b = open_v("kv2_sum", s)
                    mm(b[:, 0:D + 1], K2[:, 0, :], V2[:, 0, :], stop=False)
                    mm(b[:, 0:D + 1], K2[0:CR, 2, :], V2[0:CR, 1, :], start=False).then_inc(dve_filled.sem, 1)

                def l2_attention(s):
                    wait_xt(4, s)
                    project(("q2", s), XT[s], w["wq2"][:])
                    pe.wait_ge(q2_ready.sem, q2_ready.at(rnd, s + 1))
                    four_transposes(("Q2T", s), lambda i: Q32[:, i, :])
                    wait_a("Q2T", s)
                    pe.wait_ge(kvb_ready.sem, kvb_ready.at(rnd, s + 1))
                    for i in range(0, T, 2):
                        b = open_v("linear", s, i)
                        mm(b[:, 0:D + H], tile(AT, i), KVB[s][:])
                        mm(b[:, D + H:2 * (D + H)], tile(AT, i + 1), KVB[s][:]).then_inc(dve_filled.sem, 1)
                    pe.wait_ge(att_ready.sem, att_ready.at(rnd, 2 + s + 1))
                    four_transposes(("AT", 2 + s), lambda i: ATT[:, i, :])
                    pe.wait_ge(exchange_read[s].sem, exchange_read[s].at(rnd, H, 16))
                    project(("att_out", 2 + s), GROUPS_T[s], w["wd2"][:])

                def l2_ffn(s):
                    wait_xt(5, s)
                    b = open_v("l2_logits", s)
                    for i in range(T):
                        last = mm(b[:, i * NE:(i + 1) * NE], tile(XT[s], i), w["wg"][:])
                    last.then_inc(dve_filled.sem, 1)
                    base = SLOTS * 2 * NE + s * NE
                    up = lambda e: expert_up(base + e, s, w["w1e"][:, e, :])
                    up(0)
                    up(1)
                    for e in range(NE):
                        if e + 2 < NE:
                            up(e + 2)
                        if e == 1:
                            pe.wait_ge(oh_ready.sem, oh_ready.at(rnd, s + 1))
                            b = open_a("OHT", s)
                            for i in range(T):
                                last = tr(b[0:NE, i * P:(i + 1) * P], GATE[s][:, i, :])
                            last.then_inc(act_filled.sem, 1)
                        expert_down(base + e, [w["w2e"][:, e, :]])
                    wait_a("OHT", s)
                    b = open_v("b2", s)
                    for i in range(T):
                        last = mm(tile(b, i), OHT[:, i * P:(i + 1) * P], w["b2e"][:])
                    last.then_inc(dve_filled.sem, 1)

                def l3_ffn(s):
                    wait_xt(7, s)
                    base = SLOTS * 3 * NE + s * NH
                    for k in range(NH):
                        expert_up(base + k, s, w["w13"][:, k * P:(k + 1) * P])
                    b = open_v("l3_out", s)
                    pe.wait_ge(relu_ready.sem, relu_ready.at(rnd, (s + 1) * NH))
                    for i in range(T):
                        for k in range(NH):
                            last = mm(tile(b, i), HT[:, (base + k) % NHT, i * P:(i + 1) * P], w["w23"][:, k, :], start=k == 0, stop=k == NH - 1)
                    last.then_inc(dve_filled.sem, 1)

                for s in range(SLOTS):
                    norm_t(0, s)
                    l0_attention(s)
                wait_weights(pe, 1)
                wait_weights(pe, 2)
                if L > 2:
                    kv_products(0, 0)
                for s in range(SLOTS if L > 1 else 0):
                    norm_t(1, s)
                    l0_ffn(s)
                    if L > 2:
                        k_transposes(0, s)
                        if s == 0:
                            kv_products(0, 1)
                if L > 2:
                    attention(0)
                if L > 4:
                    kv2_products(0)
                    kv2_sum(0)
                for s in range(SLOTS if L > 3 else 0):
                    l1_ffn(s)
                if L > 4:
                    kv2_products(1)
                    kv2_sum(1)
                for s in range(SLOTS if L > 4 else 0):
                    norm_t(4, s)
                    l2_attention(s)
                if L > 6:
                    kv_products(1, 0)
                for s in range(SLOTS if L > 5 else 0):
                    norm_t(5, s)
                    l2_ffn(s)
                    if L > 6:
                        k_transposes(1, s)
                        if s == 0:
                            kv_products(1, 1)
                if L > 6:
                    attention(1)
                for s in range(SLOTS if L > 7 else 0):
                    norm_t(7, s)
                    l3_ffn(s)
                assert (n_a[0], n_v[0]) == (fills_a, fills_v), (n_a[0], n_v[0])

        @block.sync
        def _(sp):
            sp.dma_start(consts[:], t["consts"]).then_inc(consts_loaded, 16)

            def load_slot(rnd, s, ctx_part):
                b = rnd * SLOTS + s
                if not ctx_part:
                    sp.dma_start(X[s][:], t["x"].rearrange("b (t p) d -> b p t d", p=P)[b]).then_inc(x_loaded[s].sem, 16)
                    return
                sp.dma_start(CT[s][:], t["ctxT"][b]).then_inc(ctx_loaded[s].sem, 16)
                sp.dma_start(CN[s][:], t["ctx"][b, 0:P, :]).then_inc(ctx_loaded[s].sem, 16)
                sp.dma_start(CL[s][:], t["ctx"][b, P:C, :]).then_inc(ctx_loaded[s].sem, 16)
                for j in range(J):
                    sp.dma_start(CT4[s][:, j, 0:CR], t["ctxT"][b, :, P:C]).then_inc(ctx_loaded[s].sem, 16)
                sp.dma_start(EM[s][:, 0:1], t["em"][b, 0:P, :]).then_inc(ctx_loaded[s].sem, 16)
                sp.dma_start(EM[s][0:CR, 1:2], t["em"][b, P:C, :]).then_inc(ctx_loaded[s].sem, 16)
                sp.dma_start(MRAW[s][:], t["mask"][b]).then_inc(mask_loaded[s].sem, 16)
                sp.dma_start(MTRAW[s][:], t["maskT"][b, 0:P, :]).then_inc(mask_loaded[s].sem, 16)
                sp.dma_start(MLRAW[s][:], t["maskT"][b, P:C, :]).then_inc(mask_loaded[s].sem, 16)

            load_slot(0, 0, False)
            for dst, src in wsrc[0]:
                sp.dma_start(dst, src).then_inc(loaded[0], 16)
            sp.wait_ge(setup_pool, 1)
            load_slot(0, 0, True)
            load_slot(0, 1, False)
            load_slot(0, 1, True)
            for k in (1, 2):
                for dst, src in wsrc[k]:
                    sp.dma_start(dst, src).then_inc(loaded[k], 16)

            def store(rnd, s):
                sp.wait_ge(x_done.sem, x_done.at(rnd, s + 1))
                sp.dma_start(out.rearrange("b (t p) d -> b p t d", p=P)[rnd * SLOTS + s], X[s][:]).then_inc(stored[s].sem, 16)

            def exchange_heads(rnd, s):
                sp.wait_ge(act_free.sem, drained(act_free, rnd, a_no["AT", 2 + s]))
                sp.dma_start(exchange[s], HEADS_T[s]).then_inc(exchange_written.sem, 16)
                sp.wait_ge(exchange_written.sem, exchange_written.at(rnd, s + 1, 16))
                rows = exchange[s].rearrange("(h e) (m q) -> m e h q", h=H, m=H)
                for m in range(H):
                    sp.dma_start(GROUPS_T[s][m * E8:(m + 1) * E8, :].rearrange("p (h q) -> p h q", h=H), rows[m]).then_inc(exchange_read[s].sem, 16)

            with sp.Fori(0, ROUNDS - 1) as rnd:
                for s in range(SLOTS if L > 4 else 0):
                    exchange_heads(rnd, s)
                for s in range(SLOTS):
                    if L > 6:
                        sp.wait_ge(kn_ready.sem, kn_ready.at(rnd, 2 + s + 1))
                        sp.wait_ge(mask_ready.sem, mask_ready.at(rnd, s + 1))
                        load_slot(rnd + 1, s, True)
                for s in range(SLOTS):
                    store(rnd, s)
                    sp.wait_ge(stored[s].sem, stored[s].at(rnd, 1, 16))
                    load_slot(rnd + 1, s, False)
                    if L <= 6:
                        sp.wait_ge(x_done.sem, x_done.at(rnd, 2))
                        sp.wait_ge(mask_ready.sem, mask_ready.at(rnd, 2))
                        load_slot(rnd + 1, s, True)
            for s in range(SLOTS if L > 4 else 0):
                exchange_heads(ROUNDS - 1, s)
            for s in range(SLOTS):
                store(ROUNDS - 1, s)
            for s in range(SLOTS):
                sp.wait_ge(stored[s].sem, 16 * ROUNDS)

        @block.scalar
        def _(act):
            act.sem_inc(act_free.sem, RING)
            act.wait_ge(consts_loaded, 16)
            act.wait_ge(setup_dve, 2)
            act.activation(th[:, 4, :], th[:, 2, :], ACT.Sin, scale=SIN_SCALE)
            act.activation(th[:, 5, :], th[:, 3, :], ACT.Sin, scale=SIN_SCALE).then_inc(setup_act, 1)

            with act.Fori(0, ROUNDS) as rnd:
                n_a = [0]

                def bank():
                    n_a[0] += 1
                    act.wait_ge(act_filled.sem, act_filled.at(rnd, n_a[0]))
                    return bank_a[(n_a[0] - 1) % RING]

                def free(ins):
                    ins.then_inc(act_free.sem, 1)

                def drain(dst, src):
                    b = bank()
                    act.activation(dst, src(b), ACT.Copy).then_inc(act_free.sem, 1)

                whole = lambda b: b[:]

                def norm_t(s):
                    drain(XT[s][:], whole)

                def l0_attention(s):
                    for i in range(T):
                        b = bank()
                        act.wait_ge(l0_shift.sem, l0_shift.at(rnd, s * T + i + 1))
                        ins = act.activation(PN[:, i, :], b[:, 0:C], ACT.Exp, bias=mx[:, i:i + 1], accum_out=sums[:, i:i + 1])
                        ins.then_inc(act_free.sem, 1)
                    drain(PNT[:], whole)
                    drain(PNL[:], lambda b: b[0:CR, :])

                def hidden(n, func, bias=None):
                    b = bank()
                    if bias is None:
                        ins = act.activation(HT[:, n % NHT, :], b[:], func)
                    else:
                        ins = act.activation(HT[:, n % NHT, :], b[:], func, bias=bias)
                    ins.then_inc(act_free.sem, 1)

                def l0_ffn(s):
                    b = bank()
                    ins = act.activation(GT[:], b[0:32, :], ACT.Gelu, bias=w["bg1"][:])
                    ins.then_inc(act_free.sem, 1)
                    for n in range(2 * NE):
                        hidden(s * 2 * NE + n, ACT.Gelu)
                        if n == 3:
                            act.wait_ge(l0_shifted.sem, l0_shifted.at(rnd, s + 1))
                            act.activation(lg[:, 6], lg[:, 5], ACT.Exp).then_inc(l0_exps.sem, 1)

                def k_transposes(a, s):
                    if 2 * a + s > 0:
                        act.wait_ge(kb_ready.sem, kb_ready.at(rnd, 2 * a + s))
                    drain(KTC[:], lambda b: b[:, 0:C])
                    b = bank()
                    act.activation(KS[:, 0:3, :], b[:, 0:3 * C].rearrange("p (g c) -> p g c", c=C), ACT.Copy).then_inc(act_free.sem, 1)
                    b = bank()
                    ins = act.activation(KS[:, 3, :], b[:, 0:C], ACT.Copy)
                    ins.then_inc(act_free.sem, 1)

                def k3_root(s):
                    act.wait_ge(kms_ready.sem, kms_ready.at(rnd, s + 1))
                    act.activation(msk[:], msk[:], ACT.Sqrt).then_inc(krt_ready.sem, 1)

                def queries(a, s):
                    norm_t(s)
                    if a == 1:
                        act.wait_ge(qms_ready.sem, qms_ready.at(rnd, s + 1))
                        act.activation(ms[:], ms[:], ACT.Sqrt).then_inc(qrt_ready.sem, 1)
                    drain(QTC[s][:], whole)

                def split_queries(a, s, g):
                    drain(QS[((2 * a + s) * G + g) % 2][:], whole)

                def exps(a, s, g):
                    n = (2 * a + s) * G + g
                    for j in range(J + 1):
                        b = bank()
                        ins = act.activation(PT[:, (n % 2) * (J + 1) + j, :], b[:], ACT.Exp)
                        ins.then_inc(act_free.sem, 1)

                def values(a, s, g):
                    drain(UT[:, ((2 * a + s) * G + g) % 2, :], whole)

                def attention_out():
                    drain(AT[:], whole)

                def attention(a):
                    queries(a, 0)
                    queries(a, 1)
                    for s in range(SLOTS):
                        split_queries(a, s, 0)
                        for g in range(G + 2):
                            if g + 1 < G:
                                split_queries(a, s, g + 1)
                            if g < G:
                                exps(a, s, g)
                            if 1 <= g <= G:
                                values(a, s, g - 1)
                        attention_out()

                def l1_ffn(s):
                    drain(XQT[:], lambda b: b[:].bitcast(BF16)[:, 0:S])
                    drain(SB_[:], whole)
                    for k in range(NH + 1):
                        if k < NH:
                            act.wait_ge(hp_ready.sem, hp_ready.at(rnd, s * NH + k + 1))
                            act.activation(CV[:, k, :], HP[:, k, 1:S + 1], ACT.Identity, scale=w["cw"][:, k, 1:2], bias=w["cb"][:, k:k + 1]).then_inc(tap_ready.sem, 1)
                        if k > 0:
                            act.wait_ge(conv_ready.sem, conv_ready.at(rnd, s * NH + k))
                            act.activation(CV[:, k - 1, :], CV[:, k - 1, :], ACT.Silu).then_inc(z_ready.sem, 1)
                    for i in range(T):
                        drain(ZT[:, :, i * P:(i + 1) * P], lambda b: b[:].bitcast(BF16)[:, 0:S].rearrange("p (k c) -> p k c", k=NH))

                def l2_attention(s):
                    drain(AT[:], whole)
                    b = bank()
                    act.activation(HEADS_T[s].rearrange("p (m q) -> p q m", m=H), b[:].rearrange("p (q m) -> p q m", m=H), ACT.Copy).then_inc(act_free.sem, 1)

                def l2_ffn(s):
                    for n in range(NE + 1):
                        if n == 4:
                            drain(OHT[:], lambda b: b[0:NE, :])
                        if n < NE:
                            hidden(SLOTS * 2 * NE + s * NE + n, ACT.Gelu, w["b1e"][:, n:n + 1])

                def l3_ffn(s):
                    for k in range(NH):
                        b = bank()
                        act.wait_ge(turn_ready.sem, turn_ready.at(rnd, s * NH + k + 1))
                        ins = act.activation(CV[:, k, :], b[:], ACT.Identity, bias=w["b13"][:, k:k + 1])
                        ins.then_inc(act_free.sem, 1)
                        act.wait_ge(phase_ready.sem, phase_ready.at(rnd, s * NH + k + 1))
                        act.activation(HP[:, k, 1:S + 1], HP[:, k, 1:S + 1], ACT.Sin, scale=SIN_SCALE).then_inc(sin_ready.sem, 1)

                for s in range(SLOTS):
                    norm_t(s)
                    l0_attention(s)
                wait_weights(act, 1)
                wait_weights(act, 2)
                for s in range(SLOTS if L > 1 else 0):
                    norm_t(s)
                    l0_ffn(s)
                    if L > 2:
                        k_transposes(0, s)
                if L > 2:
                    attention(0)
                for s in range(SLOTS if L > 3 else 0):
                    l1_ffn(s)
                for s in range(SLOTS if L > 4 else 0):
                    norm_t(s)
                    l2_attention(s)
                if L > 6:
                    k3_root(0)
                for s in range(SLOTS if L > 5 else 0):
                    norm_t(s)
                    l2_ffn(s)
                    if L > 6:
                        k_transposes(1, s)
                        if s == 0:
                            k3_root(1)
                if L > 6:
                    attention(1)
                for s in range(SLOTS if L > 7 else 0):
                    norm_t(s)
                    l3_ffn(s)

        @block.gpsimd
        def _(pool):
            steps = [0]

            def step(ins):
                ins.then_inc(pool_step, 1)
                steps[0] += 1
                pool.wait_ge(pool_step, steps[0])

            for s in range(SLOTS):
                last = pool.memset(CT4[s][:], 0.0)
            last.then_inc(setup_pool, 1)
            pool.memset(ones_row[:], 1.0)
            pool.memset(mhalf[:], -0.5)
            pool.memset(mv[:], 1.0)
            for s in range(SLOTS):
                for a in (KBL[s], VA[s], VL[s], QN[s]):
                    last = pool.memset(a[:].bitcast(F32) if a is KBL[s] else a[:], 0.0)
            for a in (KN, KNL, K2, V2, HP, msk, KH):
                last = pool.memset(a[:].bitcast(F32) if a is KH else a[:], 0.0)
            step(last)
            for s in range(SLOTS):
                pool.memset(VA[s][:, :, E8:E8 + 1], 1.0)
            pool.memset(KN[:, :, 3 * E8:3 * E8 + 1], 1.0)
            pool.memset(KNL[:, :, 3 * E8:3 * E8 + 1], 1.0)
            pool.memset(V2[:, :, D:D + 1], 1.0).then_inc(setup_pool, 1)
            pool.wait_ge(consts_loaded, 16)

            with pool.Fori(0, ROUNDS) as rnd:
                n_ln, n_2 = [0], [0]
                base = steps[0]

                def drained_a(*holds):
                    pool.wait_ge(act_free.sem, drained(act_free, rnd, a_no[holds]))

                def power(times=1):
                    for _ in range(times):
                        n_ln[0] += 1
                        pool.wait_ge(ln_var.sem, ln_var.at(rnd, n_ln[0]))
                        pool.tensor_tensor(rstd[:], var[:], mhalf[:], ALU.pow).then_inc(ln_rstd.sem, 1)

                def masks():
                    for s in range(SLOTS):
                        pool.wait_ge(mask_loaded[s].sem, mask_loaded[s].at(rnd, mask_loaded[s].n, 16))
                        pool.sem_inc(pool_waited, 1)
                        pool.tensor_scalar(MN[s][:], MRAW[s][:].bitcast(U8).rearrange("p (t c) -> p t c", t=T), BIG, -BIG, ALU.mult, ALU.add)
                        pool.tensor_scalar(MT[s][:], MTRAW[s][:].bitcast(U8), BIG, -BIG, ALU.mult, ALU.add)
                        pool.tensor_scalar(ML[s][:], MLRAW[s][:].bitcast(U8), BIG, -BIG, ALU.mult, ALU.add).then_inc(mask_ready.sem, 1)

                def block_diagonal(a, s):
                    drained_a("KTC", a, s)
                    pool.tensor_tensor(KBN[s][:], KTC[:].rearrange("p (o c) -> p o c", o=1).broadcast_to([P, H, C]),
                                       const("ind16").rearrange("p (h o) -> p h o", o=1).broadcast_to([P, H, C]),
                                       ALU.mult).then_inc(kbn_ready.sem, 1)
                    drained_a("KS", a, s, 3)
                    i4 = const("ind4")
                    for g in range(G):
                        o1 = i4.rearrange("p (j o) -> p j o", o=1)
                        pool.tensor_tensor(KBM[s][:, g], KS[:, g, 0:P].rearrange("p (o c) -> p o c", o=1).broadcast_to([P, J, P]),
                                           o1.broadcast_to([P, J, P]), ALU.mult)
                        last = pool.tensor_tensor(KBL[s][:, g, :, 0:CR], KS[:, g, P:C].rearrange("p (o c) -> p o c", o=1).broadcast_to([P, J, CR]),
                                                  o1.broadcast_to([P, J, CR]), ALU.mult)
                    last.then_inc(kb_ready.sem, 1)

                def high_halves(a, s):
                    pool.wait_ge(qh_ready.sem, qh_ready.at(rnd, 2 * a + s + 1))
                    pool.sem_inc(pool_waited, 1)
                    q = QH[:].bitcast(F32).rearrange("p t (h e) -> p (t h) e", h=H)
                    n = QN[s][:].rearrange("p t h w -> p (t h) w")
                    for k in range(2):
                        last = pool.tensor_copy(n[:, :, k * E8:(k + 1) * E8], q)
                    last.then_inc(qhh_ready.sem, 1)

                def add_bias(n, s, bias, layer):
                    pool.wait_ge(xn_ready.sem, xn_ready.at(rnd, 2 * layer + s + 1))
                    pool.tensor_tensor(X[s][:], X[s][:], bias[:].rearrange("p (o d) -> p o d", o=1).broadcast_to([P, T, D]),
                                       ALU.add).then_inc(x_added.sem, 1)

                def gamma_beta(tile_):
                    n_2[0] += 1
                    pool.wait_ge(to_pool2.sem, to_pool2.at(rnd, n_2[0]))
                    wide = lambda v: v[:].rearrange("p (o d) -> p o d", o=1).broadcast_to([P, T, D])
                    pool.tensor_tensor(tile_[:], tile_[:], wide(w["lng"]), ALU.mult).then_inc(gamma_done.sem, 1)
                    pool.wait_ge(gamma_done.sem, gamma_done.at(rnd, n_2[0]))
                    pool.tensor_tensor(tile_[:], tile_[:], wide(w["lnb"]), ALU.add).then_inc(pool2.sem, 1)

                power(2)
                if L > 1:
                    power(2)
                masks()
                wait_weights(pool, 2)
                if L > 2:
                    power()
                    block_diagonal(0, 0)
                    add_bias(0, 0, w["bp1"], 2)
                    power()
                    high_halves(0, 0)
                    block_diagonal(0, 1)
                    add_bias(0, 1, w["bp1"], 2)
                    high_halves(0, 1)
                if L > 3:
                    power(2)
                if L > 4:
                    for s in range(SLOTS):
                        if s == 0:
                            power()
                            gamma_beta(K2)
                        power()
                    power()
                    gamma_beta(K2)
                    for s in range(SLOTS):
                        power()
                        gamma_beta(Q32)
                        power()
                        gamma_beta(SQ)
                        if L > 5:
                            power()
                if L > 6:
                    power()
                    block_diagonal(1, 0)
                    power()
                    high_halves(1, 0)
                    block_diagonal(1, 1)
                    high_halves(1, 1)
                if L > 7:
                    for s in range(SLOTS):
                        power()
                        add_bias(1, s, w["b23"], 7)

        @block.vector
        def _(dve):
            steps = [0]

            def note(ins):
                ins.then_inc(dve_step, 1)
                steps[0] += 1

            def sync():
                dve.wait_ge(dve_step, steps[0])

            def link(ins):
                note(ins)
                sync()

            ts, tt, stt, red, cp = dve.tensor_scalar, dve.tensor_tensor, dve.scalar_tensor_tensor, dve.tensor_reduce, dve.tensor_copy
            dve.wait_ge(consts_loaded, 16)
            cp(ident_bf[:], ident)
            cp(rsel_bf[:], const("rsel"))
            dve.wait_ge(setup_pool, 2)
            for s in range(SLOTS):
                cp(VL[s][:, :, E8:E8 + 1], const("jrem").rearrange("p (h o) -> p h o", o=1))
            wait_weights(dve, 0)
            red(wsum[:, 0:1], w["w1b"], AX, ALU.add, apply_absolute_value=True)
            red(wsum[:, 1:2], w["w2b"].rearrange("p k d -> p (k d)"), AX, ALU.add, apply_absolute_value=True).then_inc(setup_dve, 1)
            link(ts(th[:, 0, :], w["ph"][:], 1 / TWO_PI, MAGIC, ALU.mult, ALU.add))
            link(ts(th[:, 0, :], th[:, 0, :], -MAGIC, None, ALU.add))
            link(stt(th[:, 1, :], th[:, 0, :], -PI_A, w["ph"][:], ALU.mult, ALU.add))
            link(stt(th[:, 1, :], th[:, 0, :], -PI_B, th[:, 1, :], ALU.mult, ALU.add))
            link(stt(th[:, 1, :], th[:, 0, :], -PI_C, th[:, 1, :], ALU.mult, ALU.add))
            link(ts(th[:, 1, :], th[:, 1, :], 1 / TWO_PI, None, ALU.mult))
            for k, ahead in ((2, 0.0), (3, 0.25)):
                link(ts(th[:, 6, :], th[:, 1, :], ahead, MAGIC, ALU.add, ALU.add))
                link(ts(th[:, 6, :], th[:, 6, :], -MAGIC, None, ALU.add))
                link(stt(th[:, k, :], th[:, 1, :], ahead, th[:, 6, :], ALU.add, ALU.subtract))
            dve.sem_inc(setup_dve, 1)
            dve.wait_ge(setup_pe, 1)
            link(ts(wsum[:, 2:4], bank_v[0][:, 0:2], 1 / (D * FF), 1e-5, ALU.mult, ALU.max))
            link(dve.reciprocal(wsum[:, 4:6], wsum[:, 2:4]))
            for src, dst, k in ((w["w1b"], w1q[:], 4), (w["w2b"], w2q[:], 5)):
                link(ts(src, src, wsum[:, k:k + 1], MAGIC, ALU.mult, ALU.add))
                link(ts(src, src, -MAGIC, 1.0, ALU.add, ALU.min))
                last = ts(dst, src, -1.0, None, ALU.max)
            last.then_inc(setup_dve, 1)
            note(ts(wsum[:, 6:8], wsum[:, 2:4], 1 / 127.0, None, ALU.mult))
            dve.wait_ge(setup_act, 1)
            note(tt(th[:, 6, :], th[:, 5, :], w["wr"][:], ALU.mult))
            link(tt(th[:, 7, :], th[:, 4, :], w["wi"][:], ALU.mult))
            link(tt(th[:, 6, :], th[:, 6, :], th[:, 7, :], ALU.add))
            note(stt(th[:, 8, :], th[:, 6, :], 0.1, w["wi"][:], ALU.mult, ALU.mult))
            note(stt(th[:, 9, :], w["b13"][:], 0.1 / TWO_PI, th[:, 2, :], ALU.mult, ALU.add))
            link(stt(gk[:], w["qg"][:], RSQ8, w["kg"][:], ALU.mult, ALU.mult))
            dve.sem_inc(dve_free.sem, RING)

            with dve.Fori(0, ROUNDS) as rnd:
                dve.wait_ge(dve_step, 1)
                dve.sem_clear(dve_step)
                steps[0] = 0
                n_v, n_ln, n_2 = [0], [0], [0]

                def bank(*holds):
                    assert v_no[holds] == n_v[0], (holds, v_no[holds], n_v[0])
                    n_v[0] += 1
                    dve.wait_ge(dve_filled.sem, dve_filled.at(rnd, n_v[0]))
                    return bank_v[(n_v[0] - 1) % RING]

                def free(ins):
                    ins.then_inc(dve_free.sem, 1)

                def freed():
                    dve.wait_ge(dve_free.sem, drained(dve_free, rnd, n_v[0] - 1))

                def drained_a(*holds):
                    dve.wait_ge(act_free.sem, drained(act_free, rnd, a_no[holds]))

                tile = lambda a, i: a[:, i * P:(i + 1) * P]
                quarters = lambda b: b[:].rearrange("p (t d) -> p t d", t=T)
                by_head = lambda a: a.rearrange("p (h e) -> p h e", e=E8)

                def over_d(v, n):
                    return v.rearrange("p (a o) -> p a o", o=1).broadcast_to([P, v.shape[1], n])

                def norm(srcs, dst, eps, rows=None):
                    rows = rows or [P] * T
                    for i in range(T):
                        last = dve.bn_stats(stats[0:rows[i], i, :], srcs(i))
                    link(last)
                    for i in range(T):
                        last = dve.bn_aggr(mv[0:rows[i], i, :], stats[0:rows[i], i, :])
                    link(last)
                    ts(var[:], mv[:, :, 1], eps, None, ALU.add).then_inc(ln_var.sem, 1)
                    n_ln[0] += 1
                    dve.wait_ge(ln_rstd.sem, ln_rstd.at(rnd, n_ln[0]))
                    for i in range(T):
                        k = rows[i]
                        last = ts(dst(i), srcs(i), mv[0:k, i, 0:1], rstd[0:k, i:i + 1], ALU.subtract, ALU.mult)
                        if i < T - 1:
                            pass
                    return last

                def layer_norm(s):
                    norm(lambda i: X[s][:, i, :], lambda i: XN[s][:, i, :], 1e-5).then_inc(xn_ready.sem, 1)

                def add_to_x(s, b):
                    free(tt(X[s][:], X[s][:], quarters(b), ALU.add))
                    freed()

                def l0_attention(s):
                    for i in range(T):
                        dve.wait_ge(act_filled.sem, act_filled.at(rnd, a_no["l0_scores", s, i] + 1))
                        b = bank_a[a_no["l0_scores", s, i] % RING]
                        red(mx[:, i:i + 1], b[:, 0:C], AX, ALU.max, negate=True).then_inc(l0_shift.sem, 1)
                    drained_a("l0_scores", s, T - 1)
                    link(dve.reciprocal(rsum[:], sums[:]))
                    b = bank("l0_out", s)
                    for i in range(T):
                        last = stt(X[s][:, i, :], tile(b, i), rsum[:, i:i + 1], X[s][:, i, :], ALU.mult, ALU.add)
                    free(last)
                    freed()

                def first_best(x, k):
                    link(red(gm[:, k, :], lg[:, x], AX, ALU.max))
                    link(tt(lg[:, k], lg[:, x], over_d(gm[:, k, :], NE), ALU.is_equal))
                    link(tt(lg[:, k], lg[:, k], const("desc").rearrange("p (o e) -> p o e", o=1).broadcast_to([P, T, NE]), ALU.mult))
                    link(red(gm[:, 7, :], lg[:, k], AX, ALU.max))
                    link(tt(lg[:, k], lg[:, k], over_d(gm[:, 7, :], NE), ALU.is_equal))

                def l0_gates(s):
                    b = bank("l0_logits", s)
                    free(cp(lg[:, 0].rearrange("p t e -> p (t e)"), b[:, 0:T * NE]))
                    freed()
                    link(red(gm[:, 0, :], lg[:, 0], AX, ALU.max))
                    tt(lg[:, 5], lg[:, 0], over_d(gm[:, 0, :], NE), ALU.subtract).then_inc(l0_shifted.sem, 1)
                    first_best(0, 1)
                    link(stt(lg[:, 2], lg[:, 1], -3.0e38, lg[:, 0], ALU.mult, ALU.add))
                    first_best(2, 3)
                    link(tt(lg[:, 3], lg[:, 3], lg[:, 1], ALU.add))
                    dve.wait_ge(l0_exps.sem, l0_exps.at(rnd, s + 1))
                    link(red(gm[:, 4, :], lg[:, 6], AX, ALU.add))
                    note(dve.reciprocal(gm[:, 5, :], gm[:, 4, :]))
                    link(tt(lg[:, 3], lg[:, 3], lg[:, 6], ALU.mult))
                    link(tt(GATE[s][:], lg[:, 3], over_d(gm[:, 5, :], NE), ALU.mult))

                def expert_sums(s, base, per):
                    for e in range(NE):
                        b = bank("down", base + per * e)
                        for i in range(T):
                            last = stt(X[s][:, i, :], tile(b, i), GATE[s][:, i, e:e + 1], X[s][:, i, :], ALU.mult, ALU.add)
                        free(last)
                        freed()

                def keys(a, s):
                    b = bank("kv", a, s)
                    kb = b[:].rearrange("p (x d) -> p x d", d=D)
                    if a == 0:
                        note(ts(KH[:, 0, :], kb[:, 0], RSQ8, None, ALU.mult))
                        ts(KH[0:CR, 1, :], kb[0:CR, 2], RSQ8, None, ALU.mult).then_inc(kh_ready.sem, 1)
                        dve.wait_ge(kh_ready.sem, kh_ready.at(rnd, s + 1))
                        hi = KH[:].bitcast(F32)
                        stt(KN[:, :, E8:2 * E8], by_head(kb[:, 0]), RSQ8, by_head(hi[:, 0, :]), ALU.mult, ALU.subtract)
                        stt(KNL[:, :, E8:2 * E8], by_head(kb[0:CR, 2]), RSQ8, by_head(hi[0:CR, 1, :]), ALU.mult, ALU.subtract)
                    else:
                        k32 = SQ[:, 0:2, :]
                        note(cp(k32[:, 0, :], kb[:, 0]))
                        link(cp(k32[0:CR, 1, :], kb[0:CR, 2]))
                        note(tt(SQ[:, 2, :], k32[:, 0, :], k32[:, 0, :], ALU.mult))
                        link(tt(SQ[0:CR, 3, :], k32[0:CR, 1, :], k32[0:CR, 1, :], ALU.mult))
                        note(red(msk[:, 0:H], by_head(SQ[:, 2, :]), AX, ALU.add))
                        link(red(msk[0:CR, H:2 * H], by_head(SQ[0:CR, 3, :]), AX, ALU.add))
                        ts(msk[:], msk[:], 1 / E8, 1e-6, ALU.mult, ALU.add).then_inc(kms_ready.sem, 1)
                        dve.wait_ge(krt_ready.sem, krt_ready.at(rnd, s + 1))
                        link(dve.reciprocal(msk[:], msk[:]))
                        for i, k in ((0, P), (1, CR)):
                            wide = msk[0:k, i * H:(i + 1) * H].rearrange("p (h o) -> p h o", o=1).broadcast_to([k, H, E8])
                            last = tt(by_head(k32[0:k, i, :]), by_head(k32[0:k, i, :]), wide, ALU.mult)
                        link(last)
                        for i, k in ((0, P), (1, CR)):
                            wide = gk[0:k].rearrange("p (o e) -> p o e", o=1).broadcast_to([k, H, E8])
                            last = tt(by_head(k32[0:k, i, :]), by_head(k32[0:k, i, :]), wide, ALU.mult)
                        link(last)
                        note(cp(KH[:, 0, :], k32[:, 0, :]))
                        cp(KH[0:CR, 1, :], k32[0:CR, 1, :]).then_inc(kh_ready.sem, 1)
                        dve.wait_ge(kh_ready.sem, kh_ready.at(rnd, 2 + s + 1))
                        hi = KH[:].bitcast(F32)
                        tt(KN[:, :, E8:2 * E8], by_head(k32[:, 0, :]), by_head(hi[:, 0, :]), ALU.subtract)
                        tt(KNL[:, :, E8:2 * E8], by_head(k32[0:CR, 1, :]), by_head(hi[0:CR, 1, :]), ALU.subtract)
                    for k in (0, 2):
                        cp(KN[:, :, k * E8:(k + 1) * E8], by_head(hi[:, 0, :]))
                        last = cp(KNL[:, :, k * E8:(k + 1) * E8], by_head(hi[0:CR, 1, :]))
                    last.then_inc(kn_ready.sem, 1)
                    cp(VA[s][:, :, 0:E8], by_head(kb[:, 1]))
                    free(tt(VL[s][:, :, 0:E8], by_head(kb[:, 3]),
                            const("jind").rearrange("p (h o) -> p h o", o=1).broadcast_to([P, H, E8]), ALU.mult))

                def queries(a, s):
                    b = bank("q", a, s)
                    n = 2 * a + s + 1
                    lo = QN[s][:].rearrange("p t h w -> p (t h) w")[:, :, 2 * E8:3 * E8]
                    heads = lambda v: v.rearrange("p t (h e) -> p (t h) e", e=E8)
                    if n > 1:
                        dve.wait_ge(qhh_ready.sem, qhh_ready.at(rnd, n - 1))
                    if a == 0:
                        cp(QH[:], quarters(b)).then_inc(qh_ready.sem, 1)
                        dve.wait_ge(qh_ready.sem, qh_ready.at(rnd, n))
                        free(tt(lo, by_head(b[:]), heads(QH[:].bitcast(F32)), ALU.subtract))
                    else:
                        free(cp(Q32[:], quarters(b)))
                        freed()
                        link(tt(SQ[:], Q32[:], Q32[:], ALU.mult))
                        link(red(ms[:], heads(SQ[:]), AX, ALU.add))
                        ts(ms[:], ms[:], 1 / E8, 1e-6, ALU.mult, ALU.add).then_inc(qms_ready.sem, 1)
                        dve.wait_ge(qrt_ready.sem, qrt_ready.at(rnd, s + 1))
                        link(dve.reciprocal(ms[:], ms[:]))
                        link(tt(heads(Q32[:]), heads(Q32[:]), over_d(ms[:], E8), ALU.mult))
                        cp(QH[:], Q32[:]).then_inc(qh_ready.sem, 1)
                        dve.wait_ge(qh_ready.sem, qh_ready.at(rnd, n))
                        note(tt(lo, heads(Q32[:]), heads(QH[:].bitcast(F32)), ALU.subtract))

                def maxima(a, s, i):
                    for c in range(NCH):
                        n = min(CH, H - c * CH)
                        b = bank("natural", a, s, i, c)
                        last = red(QN[s][:, i, c * CH:c * CH + n, 3 * E8], b[:, 0:n * C].rearrange("p (h c) -> p h c", c=C), AX, ALU.max, negate=True)
                        free(last)
                    dve.wait_ge(dve_free.sem, drained(dve_free, rnd, n_v[0] - 1))
                    dve.sem_inc(max_done.sem, 1)

                def heads_back(a, s, g):
                    b = bank("heads", a, s, g)
                    if g > 0:
                        dve.wait_ge(dve_free.sem, drained(dve_free, rnd, v_no["heads", a, s, g - 1]))
                    v = b[:].rearrange("p (t j w) -> p t j w", t=T, j=J)
                    link(dve.reciprocal(r16[:], v[:, :, :, E8]))
                    o = ATT[:].rearrange("p t (g j e) -> p t g j e", g=G, j=J)[:, :, g]
                    free(tt(o, v[:, :, :, 0:E8], r16[:].rearrange("p t (j o) -> p t j o", o=1).broadcast_to([P, T, J, E8]), ALU.mult))

                def attention(a):
                    queries(a, 0)
                    for i in range(T):
                        maxima(a, 0, i)
                    queries(a, 1)
                    for s in range(SLOTS):
                        for g in range(G + 2):
                            if s == 0 and g < T:
                                maxima(a, 1, g)
                            if g >= 2:
                                heads_back(a, s, g - 2)
                        freed()
                        dve.sem_inc(att_ready.sem, 1)
                        dve.wait_ge(x_added.sem, x_added.at(rnd, s + 1)) if a == 0 else None
                        add_to_x(s, bank("att_out", 4 * a + s))
                        if L > 2 + 4 * a + 1:
                            layer_norm(s)
                            if a == 0:
                                quantise_x(s)

                def quantise_x(s):
                    dve.wait_ge(xn_ready.sem, xn_ready.at(rnd, 2 * 3 + s + 1))
                    link(red(amax[:, 0, :], XN[s][:], AX, ALU.max, apply_absolute_value=True))
                    link(ts(amax[:, 0, :], amax[:, 0, :], 1e-5, None, ALU.max))
                    link(dve.reciprocal(amax[:, 1, :], amax[:, 0, :]))
                    link(ts(amax[:, 1, :], amax[:, 1, :], 127.0, None, ALU.mult))
                    for i in range(T):
                        last = ts(SQ[:, i, :], XN[s][:, i, :], amax[:, 1, i:i + 1], MAGIC, ALU.mult, ALU.add)
                    link(last)
                    ts(XQ[s], SQ[:], -MAGIC, 127.0, ALU.add, ALU.min).then_inc(xq_ready.sem, 1)
                    ts(amax[:, 3 + s, :], amax[:, 0, :], wsum[:, 6:7], None, ALU.mult).then_inc(rs_ready.sem, 1)

                def l1_ffn(s):
                    drained_a("SBC", s)
                    for k in range(NH + 1):
                        if k < NH:
                            b = bank("l1_hidden", s, k)
                            ins = tt(HP[:, k, 1:S + 1], b[:], SB_[:], ALU.mult)
                            free(ins)
                            freed()
                            dve.sem_inc(hp_ready.sem, 1)
                        if k > 0:
                            j = k - 1
                            dve.wait_ge(tap_ready.sem, tap_ready.at(rnd, s * NH + j + 1))
                            link(stt(CV[:, j, :], HP[:, j, 0:S], w["cw"][:, j, 0:1], CV[:, j, :], ALU.mult, ALU.add))
                            stt(CV[:, j, :], HP[:, j, 2:S + 2], w["cw"][:, j, 2:3], CV[:, j, :], ALU.mult, ALU.add).then_inc(conv_ready.sem, 1)
                    zb = []
                    for i in range(T):
                        b = bank("z", s, i)
                        zb.append(b)
                        last = red(amax[:, 0, i:i + 1], b[:], AX, ALU.max, apply_absolute_value=True)
                    link(last)
                    link(ts(amax[:, 0, :], amax[:, 0, :], 1e-5, None, ALU.max))
                    link(dve.reciprocal(amax[:, 1, :], amax[:, 0, :]))
                    note(ts(amax[:, 2, :], amax[:, 0, :], wsum[:, 7:8], None, ALU.mult))
                    link(ts(amax[:, 1, :], amax[:, 1, :], 127.0, None, ALU.mult))
                    for i in range(T):
                        z = sn[:, i, :]
                        free(ts(z, zb[i][:], amax[:, 1, i:i + 1], MAGIC, ALU.mult, ALU.add))
                        dve.wait_ge(dve_free.sem, drained(dve_free, rnd, v_no["z", s, i]))
                        ts(ZQ[:, i, :], z, -MAGIC, 127.0, ALU.add, ALU.min).then_inc(zq_ready.sem, 1)
                    b = bank("l1_out", s)
                    for i in range(T):
                        last = stt(X[s][:, i, :], tile(b, i), amax[:, 2, i:i + 1], X[s][:, i, :], ALU.mult, ALU.add)
                    free(last)
                    freed()

                def keys2(s):
                    b = bank("kv2", s)
                    rows = [P, P, CR, CR]
                    src = lambda i: b[0:rows[i], i * D:(i + 1) * D]
                    free(norm(src, lambda i: K2[0:rows[i], i, :], 1e-6, rows))
                    freed()
                    dve.sem_inc(to_pool2.sem, 1)
                    n_2[0] += 1
                    dve.wait_ge(pool2.sem, pool2.at(rnd, n_2[0]))
                    for i, k in ((0, P), (2, CR)):
                        last = ts(K2[0:k, i, :], K2[0:k, i, :], 0.0, 1e-6, ALU.max, ALU.add)
                    link(last)
                    for i, k, m in ((0, P, 0), (2, CR, 1)):
                        ts(K2[0:k, i, :], K2[0:k, i, :], EM[s][0:k, m:m + 1], None, ALU.mult)
                        last = ts(V2[0:k, m, 0:D], K2[0:k, i + 1, :], EM[s][0:k, m:m + 1], None, ALU.mult)
                    last.then_inc(kv2_ready.sem, 1)
                    b = bank("kv2_sum", s)
                    tt(KVB[s][:, 0:D], b[:, 0:D], const("blk"), ALU.mult)
                    free(tt(KVB[s][:, D:D + H], b[:, D:D + 1].broadcast_to([P, H]), const("ind16"), ALU.mult))
                    freed()
                    dve.sem_inc(kvb_ready.sem, 1)

                def l2_attention(s):
                    b = bank("q2", s)
                    free(norm(lambda i: tile(b, i), lambda i: Q32[:, i, :], 1e-6))
                    freed()
                    dve.sem_inc(to_pool2.sem, 1)
                    n_2[0] += 1
                    dve.wait_ge(pool2.sem, pool2.at(rnd, n_2[0]))
                    ts(Q32[:], Q32[:], 0.0, 1e-6, ALU.max, ALU.add).then_inc(q2_ready.sem, 1)
                    for i in range(0, T, 2):
                        b = bank("linear", s, i)
                        if i > 0:
                            dve.wait_ge(dve_free.sem, drained(dve_free, rnd, v_no["linear", s, i - 2]))
                        v = b[:, 0:2 * (D + H)].rearrange("p (t x) -> p t x", t=2)
                        link(ts(den[:], v[:, :, D:D + H], 1e-6, None, ALU.add))
                        link(dve.reciprocal(den[:], den[:]))
                        o = ATT[:, i:i + 2, :].rearrange("p t (h e) -> p t h e", h=H)
                        free(tt(o, v[:, :, 0:D].rearrange("p t (h e) -> p t h e", h=H),
                                den[:].rearrange("p t (h o) -> p t h o", o=1).broadcast_to([P, 2, H, E8]), ALU.mult))
                    freed()
                    dve.sem_inc(att_ready.sem, 1)
                    b = bank("att_out", 2 + s)
                    free(tt(Q32[:], quarters(b), w["bd2"][:].rearrange("p (o d) -> p o d", o=1).broadcast_to([P, T, D]), ALU.add))
                    freed()
                    link(norm(lambda i: Q32[:, i, :], lambda i: SQ[:, i, :], 1e-6))
                    dve.sem_inc(to_pool2.sem, 1)
                    n_2[0] += 1
                    dve.wait_ge(pool2.sem, pool2.at(rnd, n_2[0]))
                    link(tt(X[s][:], X[s][:], SQ[:], ALU.add))

                def l2_ffn(s):
                    b = bank("l2_logits", s)
                    free(tt(lg[:, 0], b[:, 0:T * NE].rearrange("p (t e) -> p t e", e=NE),
                            w["bg"][:].rearrange("p (o e) -> p o e", o=1).broadcast_to([P, T, NE]), ALU.add))
                    freed()
                    first_best(0, 1)
                    cp(GATE[s][:], lg[:, 1]).then_inc(oh_ready.sem, 1)
                    dve.wait_ge(oh_ready.sem, oh_ready.at(rnd, s + 1))
                    expert_sums(s, SLOTS * 2 * NE + s * NE, 1)
                    add_to_x(s, bank("b2", s))

                def l3_ffn(s):
                    base = SLOTS * 3 * NE + s * NH
                    for k in range(NH + 1):
                        if k < NH:
                            m = s * NH + k
                            u, r_ = sn[:, m % 2, :], PT[:, 8 + m % 2, :]
                            if m >= 2:
                                dve.wait_ge(phase_ready.sem, phase_ready.at(rnd, m - 1))
                            n = a_no["hidden", base + k]
                            dve.wait_ge(act_filled.sem, act_filled.at(rnd, n + 1))
                            ts(u, bank_a[n % RING][:], 0.1 / TWO_PI, th[:, 9, k:k + 1], ALU.mult, ALU.add).then_inc(turn_ready.sem, 1)
                            dve.wait_ge(turn_ready.sem, turn_ready.at(rnd, s * NH + k + 1))
                            link(ts(r_, u, MAGIC, -MAGIC, ALU.add, ALU.add))
                            tt(HP[:, k, 1:S + 1], u, r_, ALU.subtract).then_inc(phase_ready.sem, 1)
                        if k > 0:
                            j = k - 1
                            m = s * NH + j
                            v = sn[:, 2 + m % 2, :]
                            if m >= 2:
                                dve.wait_ge(relu_ready.sem, relu_ready.at(rnd, m - 1))
                            dve.wait_ge(sin_ready.sem, sin_ready.at(rnd, m + 1))
                            link(stt(v, HP[:, j, 1:S + 1], th[:, 8, j:j + 1], CV[:, j, :], ALU.mult, ALU.add))
                            ts(HT[:, (base + j) % NHT, :], v, 0.0, None, ALU.max).then_inc(relu_ready.sem, 1)
                    dve.wait_ge(x_added.sem, x_added.at(rnd, 2 + s + 1))
                    add_to_x(s, bank("l3_out", s))

                for s in range(SLOTS):
                    dve.wait_ge(x_loaded[s].sem, x_loaded[s].at(rnd, 1, 16))
                    layer_norm(s)
                for s in range(SLOTS):
                    l0_attention(s)
                    if L > 1:
                        layer_norm(s)
                wait_weights(dve, 2)
                if L > 2:
                    keys(0, 0)
                for s in range(SLOTS if L > 1 else 0):
                    l0_gates(s)
                    expert_sums(s, s * 2 * NE, 2)
                    if L > 2:
                        layer_norm(s)
                        if s == 0:
                            keys(0, 1)
                if L > 2:
                    attention(0)
                if L > 4:
                    keys2(0)
                for s in range(SLOTS if L > 3 else 0):
                    l1_ffn(s)
                    if L > 4:
                        layer_norm(s)
                if L > 4:
                    keys2(1)
                for s in range(SLOTS if L > 4 else 0):
                    l2_attention(s)
                    if L > 5:
                        layer_norm(s)
                if L > 6:
                    keys(1, 0)
                for s in range(SLOTS if L > 5 else 0):
                    l2_ffn(s)
                    if L > 6:
                        layer_norm(s)
                        if s == 0:
                            keys(1, 1)
                if L > 6:
                    attention(1)
                for s in range(SLOTS if L > 7 else 0):
                    l3_ffn(s)
                    dve.sem_inc(x_done.sem, 1)
                if L < 8:
                    sync()
                    dve.sem_inc(x_done.sem, 2)
                sync()
                assert n_v[0] == fills_v, n_v
                assert n_ln[0] == ln_var.n, n_ln


def kernel(**inputs):
    import concourse.bacc as bacc
    from concourse.bass_utils import run_bass_kernel_spmd

    a = {k: np.asarray(v) for k, v in inputs.items()}
    tiles = lambda v: v.reshape(NH, P).T
    words = lambda v: np.ascontiguousarray(v).view(np.uint32)
    laid = dict(
        consts=constants(),
        x=a["x"], ctx=a["ctx_1024"], ctxT=a["ctx_1024"].transpose(0, 2, 1),
        mask=words(a["mask_Bx1xSxS2_bk0"].reshape(NB, T, P, C).transpose(0, 2, 1, 3).reshape(NB, P, T * C)),
        maskT=words(a["mask_Bx1xSxS2_bk0"][:, 0].transpose(0, 2, 1)),
        em=a["mask_BxS2_ff1"][:, :, None],
        wg1=a["L0_ffn_wg1"], bg1=a["L0_ffn_bg1"][:, None], wg2=a["L0_ffn_wg2"], w_in=a["L0_ffn_w_in"], w_out=a["L0_ffn_w_out"],
        wq1=a["L1_xattn_W_q"].T, wk1=a["L1_xattn_W_k"].T, wv1=a["L1_xattn_W_v"].T, wp1=a["L1_xattn_W_proj"].T, bp1=a["L1_xattn_b_proj"],
        w1b=a["L1_ffn_w1"].T, cw=a["L1_ffn_conv_w"].reshape(NH, P, 3).transpose(1, 0, 2), cb=tiles(a["L1_ffn_conv_b"]), w2b=a["L1_ffn_w2"].T,
        wq2=a["L2_xattn_wq"], wk2=a["L2_xattn_wk"], wv2=a["L2_xattn_wv"], lng=a["L2_xattn_ln_gamma"], lnb=a["L2_xattn_ln_beta"],
        wd2=a["L2_xattn_dense_w"], bd2=a["L2_xattn_dense_b"],
        wg=a["L2_ffn_Wg"], bg=a["L2_ffn_bg"], w1e=a["L2_ffn_W1"], b1e=a["L2_ffn_b1"].T, w2e=a["L2_ffn_W2"], b2e=a["L2_ffn_b2"],
        wq3=a["L3_xattn_Wq"], wkv3=a["L3_xattn_Wkv"], wp3=a["L3_xattn_Wproj"], qg=a["L3_xattn_q_gamma"], kg=a["L3_xattn_k_gamma"],
        w13=a["L3_ffn_W1"], b13=tiles(a["L3_ffn_b1"]), ph=tiles(a["L3_ffn_quantum_phases"]), wr=tiles(a["L3_ffn_quantum_weights_real"]),
        wi=tiles(a["L3_ffn_quantum_weights_imag"]), w23=a["L3_ffn_W2"], b23=a["L3_ffn_b2"],
    )
    nc = bacc.Bacc("TRN2", target_bir_lowering=False, num_devices=1)
    arrays, aps = {}, {}
    for name, v in laid.items():
        v = np.ascontiguousarray(v)
        arrays[f"in_{name}"] = v
        aps[name] = nc.dram_tensor(f"in_{name}", v.shape, mybir.dt.from_np(v.dtype), kind="ExternalInput").ap()
    out = nc.dram_tensor("out", (NB, S, D), F32, kind="ExternalOutput").ap()
    build(nc, aps, out)
    return run_bass_kernel_spmd(nc, [arrays], core_ids=[0]).results[0]["out"]
```

```python
from contextlib import ExitStack

import numpy as np

import concourse.bass as bass
from concourse import mybir

F32 = mybir.dt.float32
F32R = mybir.dt.float32r
BF16 = mybir.dt.bfloat16
U8 = mybir.dt.uint8
U32 = mybir.dt.uint32
ALU = mybir.AluOpType
ACT = mybir.ActivationFunctionType
AX = mybir.AxisListType.X

P = 128
NB, S, D = 4, 512, 128
T = S // P
C = 154
CR = C - P
H, E8 = 16, 8
G, J = 4, 4
W = 32
NE = 8
HID0 = 256
FF = 512
NH = FF // P
SLOTS, ROUNDS = 2, 2
RING = 4
CH = 3
NCH = -(-H // CH)
NPT = 10
NHT = 8
BIG = 2.0 ** 100
MAGIC = 1.5 * 2.0 ** 23
TWO_PI = 2 * np.pi
PI_A, PI_B = 6.28125, 0.0019350051879882812
PI_C = float(TWO_PI - PI_A - PI_B)
SIN_SCALE = 6.283185
RSQ8 = float(1 / np.sqrt(8.0))

XT_ORDER = {0: 0, 1: 1, 2: 2, 4: 3, 5: 4, 6: 5, 7: 6}

FILLS = {1: (14, 2), 2: (50, 20), 3: (118, 82), 4: (130, 100), 5: (136, 112), 6: (156, 132), 7: (224, 194), 8: (234, 196)}
NLN = {1: 2, 2: 4, 3: 6, 4: 8, 5: 16, 6: 18, 7: 20, 8: 22}

CONSTS = {}
_at = 0
for _n, _w in (("ident", 128), ("blk", 128), ("rsel", 128), ("ind16", 16), ("jind", 16), ("jrem", 16), ("ind4", 4), ("desc", 8)):
    CONSTS[_n] = (_at, _at + _w)
    _at += _w
NCONST = _at


def constants():
    c = np.zeros((P, NCONST), np.float32)
    p = np.arange(P)[:, None]

    def put(name, v):
        a, b = CONSTS[name]
        c[:, a:b] = v

    q = np.arange(P)[None]
    put("ident", p == q)
    put("blk", p // E8 == q // E8)
    put("rsel", (q % W == p) & (p < CR))
    h = np.arange(H)[None]
    put("ind16", p // E8 == h)
    put("jind", p // W == h % J)
    put("jrem", (p // W == h % J) & (p % W < CR))
    put("ind4", p // W == np.arange(J)[None])
    put("desc", NE - np.arange(NE)[None] + 0 * p)
    return c


def build(nc, t, out, last_layer=8):
    ctx = ExitStack()
    with ctx:
        def sb(name, shape, dt=F32):
            return ctx.enter_context(nc.sbuf_tensor(name, shape, dt))

        def sem(name):
            return ctx.enter_context(nc.semaphore(name))

        bank_a = [ctx.enter_context(nc.psum_tensor(f"act_bank{i}", [P, 512], F32)) for i in range(RING)]
        bank_v = [ctx.enter_context(nc.psum_tensor(f"dve_bank{i}", [P, 512], F32)) for i in range(RING)]

        consts = sb("consts", [P, NCONST])

        def const(name):
            a, b = CONSTS[name]
            return consts[:, a:b]

        ident = const("ident")
        ident_bf = sb("ident_bf", [P, P], BF16)
        rsel_bf = sb("rsel_bf", [P, P], BF16)
        ones_row = sb("ones_row", [P, P])

        two = lambda name, shape, dt=F32: [sb(f"{name}{s}", shape, dt) for s in range(SLOTS)]
        X = two("X", [P, T, D])
        XN = two("XN", [P, T, D])
        XT = two("XT", [P, S])
        CT = two("CT", [P, C])
        CT4 = two("CT4", [P, J, W])
        CN = two("CN", [P, D])
        CL = two("CL", [CR, D])
        MRAW = two("MRAW", [P, T * C // 4], U32)
        MTRAW = two("MTRAW", [P, S // 4], U32)
        MLRAW = two("MLRAW", [CR, S // 4], U32)
        MN = two("MN", [P, T, C], BF16)
        MT = two("MT", [P, S], BF16)
        ML = two("ML", [CR, S], BF16)
        EM = two("EM", [P, 2])
        KBN = two("KBN", [P, H, C], F32R)
        KBM = two("KBM", [P, G, J, P], F32R)
        KBL = two("KBL", [P, G, J, W], F32R)
        VA = two("VA", [P, H, W])
        VL = two("VL", [P, H, W])
        QTC = two("QTC", [P, S], F32R)
        QN = two("QN", [P, T, H, W])
        KVB = two("KVB", [P, D + H])
        GATE = two("GATE", [P, T, NE])

        QH = sb("QH", [P, T, D], F32R)
        KH = sb("KH", [P, 2, D], F32R)
        KN = sb("KN", [P, H, W])
        KNL = sb("KNL", [CR, H, W])
        KTC = sb("KTC", [P, C])
        KS = sb("KS", [P, G, C])
        QS = [sb(f"QS{i}", [P, S], F32R) for i in range(2)]
        PT = sb("PT", [P, NPT, S])
        HT = sb("HT", [P, NHT, S])
        UT = sb("UT", [P, 2, S])
        K2 = sb("K2", [P, 4, D])
        V2 = sb("V2", [P, 2, D + 1])
        SQ = sb("SQ", [P, T, D])
        HP = sb("HP", [P, NH, S + 2])
        sn = PT[:, 0:4, :]
        CV = PT[:, 4:8, :]
        PNT, PNL = [PT[:, 4 + s, :] for s in range(SLOTS)], [PT[0:CR, 6 + s, :] for s in range(SLOTS)]
        GT, OHT, SB_ = UT[0:32, 0, :], UT[0:NE, 1, :], UT[:, 0, :]
        AT = UT[:, 1, :]
        tokens = lambda a: a.rearrange("p (t d) -> p t d", t=T)
        HEADS_T = [HT[:, s, :] for s in range(SLOTS)]
        Q2 = [tokens(PT[:, s, :]) for s in range(SLOTS)]
        ATT2 = [tokens(PT[:, 2 + s, :]) for s in range(SLOTS)]
        Q2T = [UT[:, s, :] for s in range(SLOTS)]
        GROUPS_T = [HT[:, 4 + s, :] for s in range(SLOTS)]
        exchange = [nc.dram_tensor(f"exchange{s}", [H, P, S // H], F32).ap() for s in range(SLOTS)]
        ATT = HT[:, 7, :].rearrange("p (t d) -> p t d", t=T)
        Q32 = HT[:, 6, :].rearrange("p (t d) -> p t d", t=T)
        PN = [PT[:, 2 * s:2 * s + 2, :].rearrange("p a n -> p (a n)")[:, 0:T * C].rearrange("p (t c) -> p t c", t=T) for s in range(SLOTS)]
        XQ = [HT[:, 4, :].bitcast(BF16)[:, s * S:(s + 1) * S].rearrange("p (t d) -> p t d", t=T) for s in range(SLOTS)]
        XQT = HT[:, 5, :].bitcast(BF16)[:, 0:S]
        ht_bf = HT[:, 0:4, :].bitcast(BF16)
        ZQ = ht_bf[:, 0:2, :].rearrange("p a (b n) -> p (a b) n", b=2)
        ZT = ht_bf[:, 2:4, :].rearrange("p a (b n) -> p (a b) n", b=2)
        stats = sb("stats", [P, T, 6])
        mv = sb("mv", [P, 2, T, 2])
        var = sb("var", [P, 2, T])
        rstd = sb("rstd", [P, 2, T])
        mhalf = sb("mhalf", [P, T])
        mx = sb("mx", [P, 2, T])
        sums = sb("sums", [P, 2, T])
        rsum = sb("rsum", [P, 2, T])
        r16 = sb("r16", [P, T, J])
        den = sb("den", [P, 2, H])
        ms = sb("ms", [P, T * H])
        msk = sb("msk", [P, 2 * H])
        lg = sb("lg", [P, 8, T, NE])
        gm = sb("gm", [P, 8, T])
        amax = sb("amax", [P, 5, T])
        th = sb("th", [P, 12, NH])

        wshape = dict(
            wg1=[D, 32], bg1=[32, 1], wg2=[32, NE], w_in=[D, NE, HID0], w_out=[P, 2 * NE, D],
            wq1=[D, D], wkv1=[D, 2, D], wp1=[D, D], bp1=[P, D],
            cw=[P, NH, 3], cb=[P, NH],
            wq2=[D, D], wkv2=[D, 2, D], lng=[P, D], lnb=[P, D], wd2=[D, D], bd2=[P, D],
            wg=[D, NE], bg=[P, NE], w1e=[D, NE, P], b1e=[P, NE], w2e=[P, NE, D], b2e=[NE, D],
            wq3=[D, D], wkv3=[D, 2 * D], wp3=[D, D], qg=[P, E8], kg=[P, E8],
            w13=[D, FF], b13=[P, NH], ph=[P, NH], wr=[P, NH], wi=[P, NH], w23=[P, NH, D], b23=[P, D],
        )
        w = {k: sb("w_" + k, v) for k, v in wshape.items()}
        w["w1b"], w["w2b"] = PT[:, 0, :], PT[:, 1, :].rearrange("p (k d) -> p k d", k=NH)
        w1q = sb("w1q", [D, FF], BF16)
        w2q = sb("w2q", [P, NH, D], BF16)
        wsum = sb("wsum", [P, 8])
        gk = sb("gk", [P, E8])

        per_round = {}

        class Signal:
            def __init__(self, name, n):
                self.sem, self.n, self.name = sem(name), n, name
                per_round[name] = n
                self.seen = 0

            def at(self, rnd, n, step=1):
                assert 1 <= n <= self.n, (self.name, n)
                return rnd * (self.n * step) + n * step

        L = last_layer
        fills_a, fills_v = FILLS[L]
        act_filled, act_free = Signal("act_bank_filled", fills_a), Signal("act_bank_free", fills_a)
        dve_filled, dve_free = Signal("dve_bank_filled", fills_v), Signal("dve_bank_free", fills_v)
        loaded = [sem(n) for n in ("first_weights_loaded", "layer0_weights_loaded", "weights_loaded")]
        consts_loaded = sem("consts_loaded")
        setup_pool = sem("setup_pool")
        setup_dve = sem("setup_dve")
        setup_act = sem("setup_act")
        setup_pe = sem("setup_pe")
        n_heads = 2 * ((L > 2) + (L > 6))
        x_done = Signal("x_done", 2)
        x_loaded = [Signal(f"x_loaded{s}", 1) for s in range(SLOTS)]
        ctx_loaded = [Signal(f"ctx_loaded{s}", 5 + J) for s in range(SLOTS)]
        mask_loaded = [Signal(f"mask_loaded{s}", 3) for s in range(SLOTS)]
        stored = [Signal(f"stored{s}", 1) for s in range(SLOTS)]
        mask_ready = Signal("mask_ready", 2)
        ln_var = Signal("ln_var", NLN[L])
        ln_rstd = Signal("ln_rstd", NLN[L])
        xn_ready = Signal("xn_ready", 2 * L)
        x_added = Signal("x_added", 2 * (L > 2) + 2 * (L > 7))
        dve_step = sem("dve_step")
        act_step = sem("act_step")
        pool_step = sem("pool_step")
        pool_waited = sem("pool_waited")
        l0_shift = Signal("l0_shift", 2 * T)
        l0_shifted = Signal("l0_shifted", 2)
        l0_exps = Signal("l0_exps", 2)
        kn_ready = Signal("kn_ready", n_heads)
        kh_ready = Signal("kh_ready", n_heads)
        kbn_ready = Signal("kbn_ready", n_heads)
        kb_ready = Signal("kb_ready", n_heads)
        kms_ready = Signal("kms_ready", 2)
        krt_ready = Signal("krt_ready", 2)
        qms_ready = Signal("qms_ready", 2)
        qrt_ready = Signal("qrt_ready", 2)
        qh_ready = Signal("qh_ready", n_heads)
        qhh_ready = Signal("qhh_ready", n_heads)
        max_done = Signal("max_done", n_heads * T)
        att_ready = Signal("att_ready", n_heads + 2 * (L > 4))
        exchange_written = Signal("exchange_written", 2)
        exchange_read = [Signal(f"exchange_read{s}", 1) for s in range(SLOTS)]
        xq_ready = Signal("xq_ready", 2)
        rs_ready = Signal("rs_ready", 2)
        hp_ready = Signal("hp_ready", 2 * NH)
        tap_ready = Signal("tap_ready", 2 * NH)
        conv_ready = Signal("conv_ready", 2 * NH)
        z_ready = Signal("z_ready", 2 * NH)
        zq_ready = Signal("zq_ready", 2 * T)
        kv2_ready = Signal("kv2_ready", 2)
        kvb_ready = Signal("kvb_ready", 2)
        q2_ready = Signal("q2_ready", 2)
        oh_ready = Signal("oh_ready", 2)
        turn_ready = Signal("turn_ready", 2 * NH)
        phase_ready = Signal("phase_ready", 2 * NH)
        relu_ready = Signal("relu_ready", 2 * NH)
        sin_ready = Signal("sin_ready", 2 * NH)

        block = ctx.enter_context(nc.Block())

        a_no, v_no = {}, {}

        def drained(sig, rnd, n):
            return rnd * sig.n + RING + n + 1

        def free_value(sig, rnd, n):
            return rnd * sig.n + max(RING, n + 1)

        r = lambda n, pat, **k: t[n].rearrange(pat, **k)
        row = lambda n: t[n].rearrange("(o n) -> o n", o=1).broadcast_to([P, t[n].shape[0]])
        wsrc = [[
            (w["w1b"], t["w1b"]), (w["w2b"], r("w2b", "(k p) d -> p k d", p=P)),
            (w["qg"][:], row("qg")), (w["kg"][:], row("kg")),
            (w["b13"][:], t["b13"]), (w["ph"][:], t["ph"]),
            (w["wr"][:], t["wr"]), (w["wi"][:], t["wi"]),
        ], [
            (w["wg1"][:], t["wg1"]), (w["bg1"][:], t["bg1"]), (w["wg2"][:], t["wg2"]),
            (w["w_in"][:], r("w_in", "e d h -> d e h")), (w["w_out"][:], r("w_out", "e (k p) d -> p (e k) d", p=P)),
        ], [
            (w["wkv1"][:, 0, :], t["wk1"]), (w["wkv1"][:, 1, :], t["wv1"]), (w["wq1"][:], t["wq1"]),
            (w["wp1"][:], t["wp1"]), (w["bp1"][:], row("bp1")),
            (w["cw"][:], t["cw"]), (w["cb"][:], t["cb"]),
            (w["wq2"][:], t["wq2"]), (w["wkv2"][:, 0, :], t["wk2"]), (w["wkv2"][:, 1, :], t["wv2"]),
            (w["lng"][:], row("lng")), (w["lnb"][:], row("lnb")), (w["wd2"][:], t["wd2"]), (w["bd2"][:], row("bd2")),
            (w["wg"][:], t["wg"]), (w["bg"][:], row("bg")), (w["w1e"][:], r("w1e", "e d h -> d e h")),
            (w["b1e"][:], t["b1e"]), (w["w2e"][:], r("w2e", "e h d -> h e d")), (w["b2e"][:], t["b2e"]),
            (w["wq3"][:], t["wq3"]), (w["wkv3"][:], t["wkv3"]), (w["wp3"][:], t["wp3"]),
            (w["w13"][:], t["w13"]),
            (w["w23"][:], r("w23", "(k p) d -> p k d", p=P)), (w["b23"][:], row("b23")),
        ]]

        def wait_weights(eng, k):
            eng.wait_ge(loaded[k], 16 * len(wsrc[k]))

        @block.tensor
        def _(pe):
            pe.wait_ge(consts_loaded, 16)
            pe.wait_ge(setup_pool, 2)
            pe.wait_ge(setup_dve, 1)
            pe.matmul(bank_v[0][:, 0:2], ones_row[:], wsum[:, 0:2], start=True, stop=True).then_inc(setup_pe, 1)
            pe.wait_ge(setup_dve, 3)

            with pe.Fori(0, ROUNDS) as rnd:
                n_a, n_v = [0], [0]

                def open_a(*holds):
                    a_no[holds] = n_a[0]
                    pe.wait_ge(act_free.sem, free_value(act_free, rnd, n_a[0]))
                    n_a[0] += 1
                    return bank_a[(n_a[0] - 1) % RING]

                def open_v(*holds):
                    v_no[holds] = n_v[0]
                    pe.wait_ge(dve_free.sem, free_value(dve_free, rnd, n_v[0]))
                    n_v[0] += 1
                    return bank_v[(n_v[0] - 1) % RING]

                def wait_a(*holds):
                    pe.wait_ge(act_free.sem, drained(act_free, rnd, a_no[holds]))

                def wait_v(*holds):
                    pe.wait_ge(dve_free.sem, drained(dve_free, rnd, v_no[holds]))

                def mm(o, lhs, rhs, start=True, stop=True, **k):
                    return pe.matmul(o, lhs, rhs, start=start, stop=stop, **k)

                def tr(o, i, id_=None):
                    k = i.shape[0]
                    return pe.matmul(o, i, (ident if id_ is None else id_)[0:k, 0:k], start=True, stop=True, is_transpose=True)

                def four_transposes(holds, src, rows=P):
                    b = open_a(*holds)
                    for i in range(T):
                        last = tr(b[0:rows, i * P:(i + 1) * P], src(i))
                    last.then_inc(act_filled.sem, 1)

                def norm_t(layer, s):
                    pe.wait_ge(xn_ready.sem, xn_ready.at(rnd, 2 * layer + s + 1))
                    four_transposes(("XT", layer, s), lambda i: XN[s][:, i, :])

                def wait_xt(layer, s):
                    wait_a("XT", layer, s)

                def tile(a, i):
                    return a[:, i * P:(i + 1) * P]

                def project(holds, src, wt):
                    b = open_v(*holds)
                    for i in range(T):
                        last = mm(tile(b, i), tile(src, i), wt)
                    last.then_inc(dve_filled.sem, 1)

                def l0_attention():
                    for s in range(SLOTS):
                        wait_xt(0, s)
                        pe.wait_ge(ctx_loaded[s].sem, ctx_loaded[s].at(rnd, ctx_loaded[s].n, 16))
                        for i in range(T):
                            b = open_a("l0_scores", s, i)
                            mm(b[:, 0:C], tile(XT[s], i), CT[s][:]).then_inc(act_filled.sem, 1)
                    for s in range(SLOTS):
                        wait_a("l0_scores", s, T - 1)
                        four_transposes(("PNT", s), lambda i: PN[s][:, i, 0:P])
                        four_transposes(("PNL", s), lambda i: PN[s][:, i, P:C], CR)
                    for s in range(SLOTS):
                        wait_a("PNL", s)
                        b = open_v("l0_out", s)
                        for i in range(T):
                            mm(tile(b, i), tile(PNT[s], i), CN[s][:], stop=False)
                            last = mm(tile(b, i), tile(PNL[s], i), CL[s][:], start=False)
                        last.then_inc(dve_filled.sem, 1)

                def expert_up(n, s, wt):
                    b = open_a("hidden", n)
                    mm(b[:], wt, XT[s][:]).then_inc(act_filled.sem, 1)

                def expert_down(n, wts):
                    b = open_v("down", n)
                    wait_a("hidden", n + len(wts) - 1)
                    for i in range(T):
                        for k, wt in enumerate(wts):
                            last = mm(tile(b, i), tile(HT[:, (n + k) % NHT, :], i), wt, start=k == 0, stop=k == len(wts) - 1)
                    last.then_inc(dve_filled.sem, 1)

                def l0_ffn(s):
                    wait_xt(1, s)
                    b = open_a("GT", s)
                    mm(b[0:32, :], w["wg1"][:], XT[s][:]).then_inc(act_filled.sem, 1)
                    base = s * 2 * NE
                    up = lambda e: [expert_up(base + 2 * e + k, s, w["w_in"][:, e, k * P:(k + 1) * P]) for k in range(2)]
                    up(0)
                    wait_a("GT", s)
                    b = open_v("l0_logits", s)
                    for i in range(T):
                        last = mm(b[:, i * NE:(i + 1) * NE], GT[:, i * P:(i + 1) * P], w["wg2"][:])
                    last.then_inc(dve_filled.sem, 1)
                    for e in range(NE):
                        if e + 1 < NE:
                            up(e + 1)
                        expert_down(base + 2 * e, [w["w_out"][:, 2 * e + k, :] for k in range(2)])

                def kv_products(a, s):
                    wk, wv = (w["wkv1"][:, 0, :], w["wkv1"][:, 1, :]) if a == 0 else (w["wkv3"][:, 0:D], w["wkv3"][:, D:2 * D])
                    b = open_v("kv", a, s)
                    mm(b[:, 0:128], CT[s][:, 0:P], wk)
                    mm(b[:, 128:256], CT[s][:, 0:P], wv)
                    mm(b[0:CR, 256:384], CT[s][:, P:C], wk)
                    mm(b[:, 384:512], CT4[s][:, :, :].rearrange("p j w -> p (j w)"), wv).then_inc(dve_filled.sem, 1)

                def k_transposes(a, s):
                    n = 2 * a + s + 1
                    pe.wait_ge(kh_ready.sem, kh_ready.at(rnd, n))
                    b = open_a("KTC", a, s)
                    tr(b[:, 0:P], KH[:, 0, :].bitcast(F32))
                    tr(b[:, P:C], KH[0:CR, 1, :].bitcast(F32)).then_inc(act_filled.sem, 1)
                    pe.wait_ge(kn_ready.sem, kn_ready.at(rnd, n))
                    for g0, g1 in ((0, 3), (3, G)):
                        b = open_a("KS", a, s, g0)
                        for g in range(g0, g1):
                            o = (g - g0) * C
                            tr(b[:, o:o + P], KN[:, J * g:J * g + J, :].rearrange("p j w -> p (j w)"))
                            last = tr(b[:, o + P:o + C], KNL[:, J * g:J * g + J, :].rearrange("p j w -> p (j w)"))
                        last.then_inc(act_filled.sem, 1)

                def queries(a, s):
                    norm_t(2 if a == 0 else 6, s)
                    wait_xt(2 if a == 0 else 6, s)
                    project(("q", a, s), XT[s], w["wq1"][:] if a == 0 else w["wq3"][:])
                    pe.wait_ge(qh_ready.sem, qh_ready.at(rnd, 2 * a + s + 1))
                    four_transposes(("QTC", a, s), lambda i: QH[:, i, :].bitcast(F32))
                    wait_a("QTC", a, s)
                    pe.wait_ge(kbn_ready.sem, kbn_ready.at(rnd, 2 * a + s + 1))
                    if a == 0:
                        pe.wait_ge(mask_ready.sem, mask_ready.at(rnd, s + 1))

                def natural_scores(a, s, i):
                    for c in range(NCH):
                        n = min(CH, H - c * CH)
                        b = open_v("natural", a, s, i, c)
                        o = b[:, 0:n * C]
                        last = mm(o, tile(QTC[s], i), KBN[s][:, c * CH:c * CH + n, :], stop=a == 1)
                        if a == 0:
                            m = MN[s][:, i:i + 1, :].broadcast_to([P, n, C])
                            last = mm(o, ident_bf[:], m, start=False)
                        last.then_inc(dve_filled.sem, 1)

                def split_queries(a, s, g):
                    if g == 0:
                        pe.wait_ge(max_done.sem, max_done.at(rnd, (2 * a + s + 1) * T))
                        pe.wait_ge(qhh_ready.sem, qhh_ready.at(rnd, 2 * a + s + 1))
                        pe.wait_ge(kb_ready.sem, kb_ready.at(rnd, 2 * a + s + 1))
                    four_transposes(("QS", a, s, g), lambda i: QN[s][:, i, J * g:J * g + J, :].rearrange("p j w -> p (j w)"))

                def scores(a, s, g):
                    n = (2 * a + s) * G + g
                    wait_a("QS", a, s, g)
                    q = QS[n % 2]
                    for j in range(J):
                        b = open_a("scores", a, s, g, j)
                        last = mm(b[:], KBM[s][:, g, j, :], q[:], stop=a == 1)
                        if a == 0:
                            last = mm(b[:], ident_bf[:], MT[s][:], start=False)
                        last.then_inc(act_filled.sem, 1)
                    b = open_a("scores", a, s, g, J)
                    last = mm(b[:], KBL[s][:, g, :, :].rearrange("p j w -> p (j w)"), q[:], stop=a == 1)
                    if a == 0:
                        last = mm(b[:], rsel_bf[0:CR, :], ML[s][:], start=False)
                    last.then_inc(act_filled.sem, 1)

                def values(a, s, g):
                    n = (2 * a + s) * G + g
                    if g == 0:
                        wait_v("kv", a, s)
                    b = open_a("UT", a, s, g)
                    base = (n % 2) * (J + 1)
                    wait_a("scores", a, s, g, J)
                    for j in range(J):
                        mm(b[W * j:W * j + W, :], VA[s][:, J * g + j, :], PT[:, base + j, :], stop=False, tile_position=(0, W * j))
                    for j in range(J):
                        last = mm(b[W * j:W * j + W, :], VL[s][:, J * g + j, :], PT[:, base + J, :], start=False, tile_position=(0, W * j))
                    last.then_inc(act_filled.sem, 1)

                def heads_back(a, s, g):
                    n = (2 * a + s) * G + g
                    wait_a("UT", a, s, g)
                    b = open_v("heads", a, s, g)
                    for i in range(T):
                        last = tr(tile(b, i), tile(UT[:, n % 2, :], i))
                    last.then_inc(dve_filled.sem, 1)

                def attention_out(n, wt):
                    pe.wait_ge(att_ready.sem, att_ready.at(rnd, n + 1))
                    four_transposes(("AT", n), lambda i: ATT[:, i, :])
                    wait_a("AT", n)
                    project(("att_out", n), AT, wt)

                def attention(a):
                    queries(a, 0)
                    for i in range(T):
                        natural_scores(a, 0, i)
                    queries(a, 1)
                    for s in range(SLOTS):
                        split_queries(a, s, 0)
                        for g in range(G + 2):
                            if s == 0 and g < T:
                                natural_scores(a, 1, g)
                            if g + 1 < G:
                                split_queries(a, s, g + 1)
                            if g < G:
                                scores(a, s, g)
                            if 1 <= g <= G:
                                values(a, s, g - 1)
                            if g >= 2:
                                heads_back(a, s, g - 2)
                        attention_out(4 * a + s, w["wp1"][:] if a == 0 else w["wp3"][:])

                def l1_ffn(s):
                    pe.wait_ge(xq_ready.sem, xq_ready.at(rnd, s + 1))
                    b = open_a("XQT", s)
                    for i in range(T):
                        last = tr(b[:].bitcast(BF16)[:, i * P:(i + 1) * P], XQ[s][:, i, :], ident_bf)
                    last.then_inc(act_filled.sem, 1)
                    pe.wait_ge(rs_ready.sem, rs_ready.at(rnd, s + 1))
                    b = open_a("SBC", s)
                    for i in range(T):
                        last = mm(tile(b, i), amax[:, 3 + s, i:i + 1].broadcast_to([P, P]), ident)
                    last.then_inc(act_filled.sem, 1)
                    wait_a("XQT", s)
                    for k in range(NH):
                        b = open_v("l1_hidden", s, k)
                        mm(b[:], w1q[:, k * P:(k + 1) * P], XQT[:]).then_inc(dve_filled.sem, 1)
                    for i in range(T):
                        b = open_v("z", s, i)
                        for k in range(NH):
                            if i == 0:
                                pe.wait_ge(z_ready.sem, z_ready.at(rnd, s * NH + k + 1))
                            last = tr(tile(b, k), CV[:, k, i * P:(i + 1) * P])
                        last.then_inc(dve_filled.sem, 1)
                    for i in range(T):
                        b = open_a("ZT", s, i)
                        pe.wait_ge(zq_ready.sem, zq_ready.at(rnd, s * T + i + 1))
                        for k in range(NH):
                            last = tr(b[:].bitcast(BF16)[:, k * P:(k + 1) * P], ZQ[:, i, k * P:(k + 1) * P], ident_bf)
                        last.then_inc(act_filled.sem, 1)
                    b = open_v("l1_out", s)
                    for i in range(T):
                        wait_a("ZT", s, i)
                        for k in range(NH):
                            last = mm(tile(b, i), ZT[:, k, i * P:(i + 1) * P], w2q[:, k, :], start=k == 0, stop=k == NH - 1)
                    last.then_inc(dve_filled.sem, 1)

                def kv2_products(s):
                    b = open_v("kv2", s)
                    r = w["wkv2"][:].rearrange("p i d -> p (i d)")
                    mm(b[:, 0:256], CT[s][:, 0:P], r)
                    mm(b[0:CR, 256:512], CT[s][:, P:C], r).then_inc(dve_filled.sem, 1)

                def kv2_sum(s):
                    pe.wait_ge(kv2_ready.sem, kv2_ready.at(rnd, s + 1))
                    b = open_v("kv2_sum", s)
                    mm(b[:, 0:D + 1], K2[:, 0, :], V2[:, 0, :], stop=False)
                    mm(b[:, 0:D + 1], K2[0:CR, 2, :], V2[0:CR, 1, :], start=False).then_inc(dve_filled.sem, 1)

                def l2_attention():
                    for s in range(SLOTS):
                        norm_t(4, s)
                    for s in range(SLOTS):
                        wait_xt(4, s)
                        project(("q2", s), XT[s], w["wq2"][:])
                    for s in range(SLOTS):
                        pe.wait_ge(q2_ready.sem, q2_ready.at(rnd, s + 1))
                        four_transposes(("Q2T", s), lambda i: Q2[s][:, i, :])
                    for s in range(SLOTS):
                        wait_a("Q2T", s)
                        pe.wait_ge(kvb_ready.sem, kvb_ready.at(rnd, s + 1))
                        for i in range(0, T, 2):
                            b = open_v("linear", s, i)
                            mm(b[:, 0:D + H], tile(Q2T[s], i), KVB[s][:])
                            mm(b[:, D + H:2 * (D + H)], tile(Q2T[s], i + 1), KVB[s][:]).then_inc(dve_filled.sem, 1)
                    if L > 6:
                        kv_products(1, 0)
                    for s in range(SLOTS):
                        pe.wait_ge(att_ready.sem, att_ready.at(rnd, 2 + s + 1))
                        four_transposes(("AT", 2 + s), lambda i: ATT2[s][:, i, :])
                    if L > 6:
                        k_transposes(1, 0)
                    for s in range(SLOTS):
                        pe.wait_ge(exchange_read[s].sem, exchange_read[s].at(rnd, 1, 16))
                        project(("att_out", 2 + s), GROUPS_T[s], w["wd2"][:])
                    if L > 6:
                        kv_products(1, 1)

                def l2_ffn(s):
                    wait_xt(5, s)
                    b = open_v("l2_logits", s)
                    for i in range(T):
                        last = mm(b[:, i * NE:(i + 1) * NE], tile(XT[s], i), w["wg"][:])
                    last.then_inc(dve_filled.sem, 1)
                    base = SLOTS * 2 * NE + s * NE
                    up = lambda e: expert_up(base + e, s, w["w1e"][:, e, :])
                    up(0)
                    up(1)
                    for e in range(NE):
                        if e + 2 < NE:
                            up(e + 2)
                        if e == NE - 3:
                            pe.wait_ge(oh_ready.sem, oh_ready.at(rnd, s + 1))
                            b = open_a("OHT", s)
                            for i in range(T):
                                last = tr(b[0:NE, i * P:(i + 1) * P], GATE[s][:, i, :])
                            last.then_inc(act_filled.sem, 1)
                        expert_down(base + e, [w["w2e"][:, e, :]])
                    wait_a("OHT", s)
                    b = open_v("b2", s)
                    for i in range(T):
                        last = mm(tile(b, i), OHT[:, i * P:(i + 1) * P], w["b2e"][:])
                    last.then_inc(dve_filled.sem, 1)

                def l3_ffn():
                    base = SLOTS * 3 * NE
                    for s in range(SLOTS):
                        norm_t(7, s)
                        wait_xt(7, s)
                        for k in range(NH):
                            expert_up(base + s * NH + k, s, w["w13"][:, k * P:(k + 1) * P])
                    for s in range(SLOTS):
                        b = open_v("l3_out", s)
                        pe.wait_ge(relu_ready.sem, relu_ready.at(rnd, (s + 1) * NH))
                        for i in range(T):
                            for k in range(NH):
                                last = mm(tile(b, i), HT[:, (base + s * NH + k) % NHT, i * P:(i + 1) * P], w["w23"][:, k, :], start=k == 0, stop=k == NH - 1)
                        last.then_inc(dve_filled.sem, 1)

                for s in range(SLOTS):
                    norm_t(0, s)
                l0_attention()
                wait_weights(pe, 1)
                wait_weights(pe, 2)
                if L > 2:
                    kv_products(0, 0)
                for s in range(SLOTS if L > 1 else 0):
                    norm_t(1, s)
                    if L > 4:
                        kv2_products(s)
                    l0_ffn(s)
                    if L > 4:
                        kv2_sum(s)
                    if L > 2:
                        k_transposes(0, s)
                        if s == 0:
                            kv_products(0, 1)
                if L > 2:
                    attention(0)
                for s in range(SLOTS if L > 3 else 0):
                    l1_ffn(s)
                if L > 4:
                    l2_attention()
                for s in range(SLOTS if L > 5 else 0):
                    norm_t(5, s)
                    l2_ffn(s)
                    if L > 6 and s == 0:
                        k_transposes(1, 1)
                if L > 6:
                    attention(1)
                if L > 7:
                    l3_ffn()
                assert (n_a[0], n_v[0]) == (fills_a, fills_v), (n_a[0], n_v[0])

        @block.sync
        def _(sp):
            sp.dma_start(consts[:], t["consts"]).then_inc(consts_loaded, 16)

            def load_slot(rnd, s, ctx_part):
                b = rnd * SLOTS + s
                if not ctx_part:
                    sp.dma_start(X[s][:], t["x"].rearrange("b (t p) d -> b p t d", p=P)[b]).then_inc(x_loaded[s].sem, 16)
                    return
                sp.dma_start(CT[s][:], t["ctxT"][b]).then_inc(ctx_loaded[s].sem, 16)
                sp.dma_start(CN[s][:], t["ctx"][b, 0:P, :]).then_inc(ctx_loaded[s].sem, 16)
                sp.dma_start(CL[s][:], t["ctx"][b, P:C, :]).then_inc(ctx_loaded[s].sem, 16)
                for j in range(J):
                    sp.dma_start(CT4[s][:, j, 0:CR], t["ctxT"][b, :, P:C]).then_inc(ctx_loaded[s].sem, 16)
                sp.dma_start(EM[s][:, 0:1], t["em"][b, 0:P, :]).then_inc(ctx_loaded[s].sem, 16)
                sp.dma_start(EM[s][0:CR, 1:2], t["em"][b, P:C, :]).then_inc(ctx_loaded[s].sem, 16)
                sp.dma_start(MRAW[s][:], t["mask"][b]).then_inc(mask_loaded[s].sem, 16)
                sp.dma_start(MTRAW[s][:], t["maskT"][b, 0:P, :]).then_inc(mask_loaded[s].sem, 16)
                sp.dma_start(MLRAW[s][:], t["maskT"][b, P:C, :]).then_inc(mask_loaded[s].sem, 16)

            load_slot(0, 0, False)
            for dst, src in wsrc[0]:
                sp.dma_start(dst, src).then_inc(loaded[0], 16)
            sp.wait_ge(setup_pool, 1)
            load_slot(0, 0, True)
            load_slot(0, 1, False)
            load_slot(0, 1, True)
            for k in (1, 2):
                for dst, src in wsrc[k]:
                    sp.dma_start(dst, src).then_inc(loaded[k], 16)

            def store(rnd, s):
                sp.wait_ge(x_done.sem, x_done.at(rnd, s + 1))
                sp.dma_start(out.rearrange("b (t p) d -> b p t d", p=P)[rnd * SLOTS + s], X[s][:]).then_inc(stored[s].sem, 16)

            def exchange_heads(rnd, s):
                sp.wait_ge(act_free.sem, drained(act_free, rnd, a_no["AT", 2 + s]))
                sp.dma_start(exchange[s].rearrange("m (e h) q -> (e h) m q", e=E8), HEADS_T[s].rearrange("p (m q) -> p m q", m=H)).then_inc(exchange_written.sem, 16)
                sp.wait_ge(exchange_written.sem, exchange_written.at(rnd, s + 1, 16))
                sp.dma_start(GROUPS_T[s], exchange[s].rearrange("m (e h) q -> (m e) (h q)", e=E8)).then_inc(exchange_read[s].sem, 16)

            with sp.Fori(0, ROUNDS - 1) as rnd:
                for s in range(SLOTS if L > 4 else 0):
                    exchange_heads(rnd, s)
                for s in range(SLOTS):
                    if L > 6:
                        sp.wait_ge(kn_ready.sem, kn_ready.at(rnd, 2 + s + 1))
                        sp.wait_ge(mask_ready.sem, mask_ready.at(rnd, s + 1))
                        load_slot(rnd + 1, s, True)
                for s in range(SLOTS):
                    store(rnd, s)
                    sp.wait_ge(stored[s].sem, stored[s].at(rnd, 1, 16))
                    load_slot(rnd + 1, s, False)
                    if L <= 6:
                        sp.wait_ge(x_done.sem, x_done.at(rnd, 2))
                        sp.wait_ge(mask_ready.sem, mask_ready.at(rnd, 2))
                        load_slot(rnd + 1, s, True)
            for s in range(SLOTS if L > 4 else 0):
                exchange_heads(ROUNDS - 1, s)
            for s in range(SLOTS):
                store(ROUNDS - 1, s)
            for s in range(SLOTS):
                sp.wait_ge(stored[s].sem, 16 * ROUNDS)

        @block.scalar
        def _(act):
            act.sem_inc(act_free.sem, RING)
            act.wait_ge(consts_loaded, 16)
            act.wait_ge(setup_dve, 2)
            act.activation(th[:, 4, :], th[:, 2, :], ACT.Sin, scale=SIN_SCALE)
            act.activation(th[:, 5, :], th[:, 3, :], ACT.Sin, scale=SIN_SCALE).then_inc(setup_act, 1)

            with act.Fori(0, ROUNDS) as rnd:
                n_a = [0]

                def bank():
                    n_a[0] += 1
                    act.wait_ge(act_filled.sem, act_filled.at(rnd, n_a[0]))
                    return bank_a[(n_a[0] - 1) % RING]

                def free(ins):
                    ins.then_inc(act_free.sem, 1)

                def drain(dst, src):
                    b = bank()
                    act.activation(dst, src(b), ACT.Copy).then_inc(act_free.sem, 1)

                whole = lambda b: b[:]

                def norm_t(s):
                    drain(XT[s][:], whole)

                def l0_attention():
                    for s in range(SLOTS):
                        for i in range(T):
                            b = bank()
                            act.wait_ge(l0_shift.sem, l0_shift.at(rnd, s * T + i + 1))
                            ins = act.activation(PN[s][:, i, :], b[:, 0:C], ACT.Exp, bias=mx[:, s, i:i + 1], accum_out=sums[:, s, i:i + 1])
                            ins.then_inc(act_free.sem, 1)
                    for s in range(SLOTS):
                        drain(PNT[s], whole)
                        drain(PNL[s], lambda b: b[0:CR, :])

                def hidden(n, func, bias=None):
                    b = bank()
                    if bias is None:
                        ins = act.activation(HT[:, n % NHT, :], b[:], func)
                    else:
                        ins = act.activation(HT[:, n % NHT, :], b[:], func, bias=bias)
                    ins.then_inc(act_free.sem, 1)

                def l0_ffn(s):
                    b = bank()
                    ins = act.activation(GT[:], b[0:32, :], ACT.Gelu, bias=w["bg1"][:])
                    ins.then_inc(act_free.sem, 1)
                    for n in range(2 * NE):
                        hidden(s * 2 * NE + n, ACT.Gelu)
                        if n == 3:
                            act.wait_ge(l0_shifted.sem, l0_shifted.at(rnd, s + 1))
                            act.activation(lg[:, 6], lg[:, 5], ACT.Exp).then_inc(l0_exps.sem, 1)

                def k_transposes(a, s):
                    if 2 * a + s > 0:
                        act.wait_ge(kb_ready.sem, kb_ready.at(rnd, 2 * a + s))
                    drain(KTC[:], lambda b: b[:, 0:C])
                    b = bank()
                    act.activation(KS[:, 0:3, :], b[:, 0:3 * C].rearrange("p (g c) -> p g c", c=C), ACT.Copy).then_inc(act_free.sem, 1)
                    b = bank()
                    ins = act.activation(KS[:, 3, :], b[:, 0:C], ACT.Copy)
                    ins.then_inc(act_free.sem, 1)

                def k3_root(s):
                    act.wait_ge(kms_ready.sem, kms_ready.at(rnd, s + 1))
                    act.activation(msk[:], msk[:], ACT.Sqrt).then_inc(krt_ready.sem, 1)

                def queries(a, s):
                    norm_t(s)
                    if a == 1:
                        act.wait_ge(qms_ready.sem, qms_ready.at(rnd, s + 1))
                        act.activation(ms[:], ms[:], ACT.Sqrt).then_inc(qrt_ready.sem, 1)
                    drain(QTC[s][:], whole)

                def split_queries(a, s, g):
                    drain(QS[((2 * a + s) * G + g) % 2][:], whole)

                def exps(a, s, g):
                    n = (2 * a + s) * G + g
                    for j in range(J + 1):
                        b = bank()
                        ins = act.activation(PT[:, (n % 2) * (J + 1) + j, :], b[:], ACT.Exp)
                        ins.then_inc(act_free.sem, 1)

                def values(a, s, g):
                    drain(UT[:, ((2 * a + s) * G + g) % 2, :], whole)

                def attention_out():
                    drain(AT[:], whole)

                def attention(a):
                    queries(a, 0)
                    queries(a, 1)
                    for s in range(SLOTS):
                        split_queries(a, s, 0)
                        for g in range(G + 2):
                            if g + 1 < G:
                                split_queries(a, s, g + 1)
                            if g < G:
                                exps(a, s, g)
                            if 1 <= g <= G:
                                values(a, s, g - 1)
                        attention_out()

                def l1_ffn(s):
                    drain(XQT[:], lambda b: b[:].bitcast(BF16)[:, 0:S])
                    drain(SB_[:], whole)
                    for k in range(NH + 1):
                        if k < NH:
                            act.wait_ge(hp_ready.sem, hp_ready.at(rnd, s * NH + k + 1))
                            act.activation(CV[:, k, :], HP[:, k, 1:S + 1], ACT.Identity, scale=w["cw"][:, k, 1:2], bias=w["cb"][:, k:k + 1]).then_inc(tap_ready.sem, 1)
                        if k > 0:
                            act.wait_ge(conv_ready.sem, conv_ready.at(rnd, s * NH + k))
                            act.activation(CV[:, k - 1, :], CV[:, k - 1, :], ACT.Silu).then_inc(z_ready.sem, 1)
                    for i in range(T):
                        drain(ZT[:, :, i * P:(i + 1) * P], lambda b: b[:].bitcast(BF16)[:, 0:S].rearrange("p (k c) -> p k c", k=NH))

                def l2_attention():
                    for s in range(SLOTS):
                        norm_t(s)
                    for s in range(SLOTS):
                        drain(Q2T[s], whole)
                    for s in range(SLOTS):
                        b = bank()
                        act.activation(HEADS_T[s].rearrange("p (m q) -> p q m", m=H), b[:].rearrange("p (q m) -> p q m", m=H), ACT.Copy).then_inc(act_free.sem, 1)
                    if L > 6:
                        k3_root(0)
                        k_transposes(1, 0)

                def l2_ffn(s):
                    for n in range(NE + 1):
                        if n == NE:
                            drain(OHT[:], lambda b: b[0:NE, :])
                        if n < NE:
                            hidden(SLOTS * 2 * NE + s * NE + n, ACT.Gelu, w["b1e"][:, n:n + 1])

                def l3_ffn():
                    for m in range(SLOTS * NH):
                        k = m % NH
                        if k == 0:
                            norm_t(m // NH)
                        b = bank()
                        act.wait_ge(turn_ready.sem, turn_ready.at(rnd, m + 1))
                        ins = act.activation(CV[:, k, :], b[:], ACT.Identity, bias=w["b13"][:, k:k + 1])
                        ins.then_inc(act_free.sem, 1)
                        act.wait_ge(phase_ready.sem, phase_ready.at(rnd, m + 1))
                        act.activation(HP[:, k, 1:S + 1], HP[:, k, 1:S + 1], ACT.Sin, scale=SIN_SCALE).then_inc(sin_ready.sem, 1)

                for s in range(SLOTS):
                    norm_t(s)
                l0_attention()
                wait_weights(act, 1)
                wait_weights(act, 2)
                for s in range(SLOTS if L > 1 else 0):
                    norm_t(s)
                    l0_ffn(s)
                    if L > 2:
                        k_transposes(0, s)
                if L > 2:
                    attention(0)
                for s in range(SLOTS if L > 3 else 0):
                    l1_ffn(s)
                if L > 4:
                    l2_attention()
                for s in range(SLOTS if L > 5 else 0):
                    norm_t(s)
                    if L > 6 and s == 0:
                        k3_root(1)
                    l2_ffn(s)
                    if L > 6 and s == 0:
                        k_transposes(1, 1)
                if L > 6:
                    attention(1)
                if L > 7:
                    l3_ffn()

        @block.gpsimd
        def _(pool):
            steps = [0]

            def step(ins):
                ins.then_inc(pool_step, 1)
                steps[0] += 1
                pool.wait_ge(pool_step, steps[0])

            for s in range(SLOTS):
                last = pool.memset(CT4[s][:], 0.0)
            last.then_inc(setup_pool, 1)
            pool.memset(ones_row[:], 1.0)
            pool.memset(mhalf[:], -0.5)
            pool.memset(mv[:], 1.0)
            for s in range(SLOTS):
                for a in (KBL[s], VA[s], VL[s], QN[s]):
                    last = pool.memset(a[:].bitcast(F32) if a is KBL[s] else a[:], 0.0)
            for a in (KN, KNL, K2, V2, HP, msk, KH):
                last = pool.memset(a[:].bitcast(F32) if a is KH else a[:], 0.0)
            step(last)
            for s in range(SLOTS):
                pool.memset(VA[s][:, :, E8:E8 + 1], 1.0)
            pool.memset(KN[:, :, 3 * E8:3 * E8 + 1], 1.0)
            pool.memset(KNL[:, :, 3 * E8:3 * E8 + 1], 1.0)
            pool.memset(V2[:, :, D:D + 1], 1.0).then_inc(setup_pool, 1)
            pool.wait_ge(consts_loaded, 16)

            with pool.Fori(0, ROUNDS) as rnd:
                n_ln = [0]

                def drained_a(*holds):
                    pool.wait_ge(act_free.sem, drained(act_free, rnd, a_no[holds]))

                def power(times=1):
                    for _ in range(times):
                        n = n_ln[0]
                        n_ln[0] += 1
                        pool.wait_ge(ln_var.sem, ln_var.at(rnd, n + 1))
                        pool.tensor_tensor(rstd[:, n % 2], var[:, n % 2], mhalf[:], ALU.pow).then_inc(ln_rstd.sem, 1)

                def masks():
                    for s in range(SLOTS):
                        pool.wait_ge(mask_loaded[s].sem, mask_loaded[s].at(rnd, mask_loaded[s].n, 16))
                        pool.sem_inc(pool_waited, 1)
                        pool.tensor_scalar(MN[s][:], MRAW[s][:].bitcast(U8).rearrange("p (t c) -> p t c", t=T), BIG, -BIG, ALU.mult, ALU.add)
                        pool.tensor_scalar(MT[s][:], MTRAW[s][:].bitcast(U8), BIG, -BIG, ALU.mult, ALU.add)
                        pool.tensor_scalar(ML[s][:], MLRAW[s][:].bitcast(U8), BIG, -BIG, ALU.mult, ALU.add).then_inc(mask_ready.sem, 1)

                def block_diagonal(a, s):
                    drained_a("KTC", a, s)
                    pool.tensor_tensor(KBN[s][:], KTC[:].rearrange("p (o c) -> p o c", o=1).broadcast_to([P, H, C]),
                                       const("ind16").rearrange("p (h o) -> p h o", o=1).broadcast_to([P, H, C]),
                                       ALU.mult).then_inc(kbn_ready.sem, 1)
                    drained_a("KS", a, s, 3)
                    i4 = const("ind4")
                    for g in range(G):
                        o1 = i4.rearrange("p (j o) -> p j o", o=1)
                        pool.tensor_tensor(KBM[s][:, g], KS[:, g, 0:P].rearrange("p (o c) -> p o c", o=1).broadcast_to([P, J, P]),
                                           o1.broadcast_to([P, J, P]), ALU.mult)
                        last = pool.tensor_tensor(KBL[s][:, g, :, 0:CR], KS[:, g, P:C].rearrange("p (o c) -> p o c", o=1).broadcast_to([P, J, CR]),
                                                  o1.broadcast_to([P, J, CR]), ALU.mult)
                    last.then_inc(kb_ready.sem, 1)

                def high_halves(a, s):
                    pool.wait_ge(qh_ready.sem, qh_ready.at(rnd, 2 * a + s + 1))
                    pool.sem_inc(pool_waited, 1)
                    q = QH[:].bitcast(F32).rearrange("p t (h e) -> p (t h) e", h=H)
                    n = QN[s][:].rearrange("p t h w -> p (t h) w")
                    for k in range(2):
                        last = pool.tensor_copy(n[:, :, k * E8:(k + 1) * E8], q)
                    last.then_inc(qhh_ready.sem, 1)

                def add_bias(n, s, bias, layer):
                    pool.wait_ge(xn_ready.sem, xn_ready.at(rnd, 2 * layer + s + 1))
                    pool.tensor_tensor(X[s][:], X[s][:], bias[:].rearrange("p (o d) -> p o d", o=1).broadcast_to([P, T, D]),
                                       ALU.add).then_inc(x_added.sem, 1)

                power(4)
                power()
                masks()
                wait_weights(pool, 2)
                power()
                add_bias(0, 0, w["bp1"], 2)
                power()
                block_diagonal(0, 0)
                power()
                high_halves(0, 0)
                block_diagonal(0, 1)
                add_bias(0, 1, w["bp1"], 2)
                high_halves(0, 1)
                power(2)
                power(2)
                power(4)
                power(2)
                block_diagonal(1, 0)
                power()
                block_diagonal(1, 1)
                power()
                high_halves(1, 0)
                high_halves(1, 1)
                for s in range(SLOTS):
                    power()
                    add_bias(1, s, w["b23"], 7)

        @block.vector
        def _(dve):
            steps = [0]

            def note(ins):
                ins.then_inc(dve_step, 1)
                steps[0] += 1

            def sync():
                dve.wait_ge(dve_step, steps[0])

            def link(ins):
                note(ins)
                sync()

            ts, tt, stt, red, cp = dve.tensor_scalar, dve.tensor_tensor, dve.scalar_tensor_tensor, dve.tensor_reduce, dve.tensor_copy
            dve.wait_ge(consts_loaded, 16)
            cp(ident_bf[:], ident)
            cp(rsel_bf[:], const("rsel"))
            dve.wait_ge(setup_pool, 2)
            for s in range(SLOTS):
                cp(VL[s][:, :, E8:E8 + 1], const("jrem").rearrange("p (h o) -> p h o", o=1))
            wait_weights(dve, 0)
            red(wsum[:, 0:1], w["w1b"], AX, ALU.add, apply_absolute_value=True)
            red(wsum[:, 1:2], w["w2b"].rearrange("p k d -> p (k d)"), AX, ALU.add, apply_absolute_value=True).then_inc(setup_dve, 1)
            link(ts(th[:, 0, :], w["ph"][:], 1 / TWO_PI, MAGIC, ALU.mult, ALU.add))
            link(ts(th[:, 0, :], th[:, 0, :], -MAGIC, None, ALU.add))
            link(stt(th[:, 1, :], th[:, 0, :], -PI_A, w["ph"][:], ALU.mult, ALU.add))
            link(stt(th[:, 1, :], th[:, 0, :], -PI_B, th[:, 1, :], ALU.mult, ALU.add))
            link(stt(th[:, 1, :], th[:, 0, :], -PI_C, th[:, 1, :], ALU.mult, ALU.add))
            link(ts(th[:, 1, :], th[:, 1, :], 1 / TWO_PI, None, ALU.mult))
            for k, ahead in ((2, 0.0), (3, 0.25)):
                link(ts(th[:, 6, :], th[:, 1, :], ahead, MAGIC, ALU.add, ALU.add))
                link(ts(th[:, 6, :], th[:, 6, :], -MAGIC, None, ALU.add))
                link(stt(th[:, k, :], th[:, 1, :], ahead, th[:, 6, :], ALU.add, ALU.subtract))
            dve.sem_inc(setup_dve, 1)
            dve.wait_ge(setup_pe, 1)
            link(ts(wsum[:, 2:4], bank_v[0][:, 0:2], 1 / (D * FF), 1e-5, ALU.mult, ALU.max))
            link(dve.reciprocal(wsum[:, 4:6], wsum[:, 2:4]))
            for src, dst, k in ((w["w1b"], w1q[:], 4), (w["w2b"], w2q[:], 5)):
                link(ts(src, src, wsum[:, k:k + 1], MAGIC, ALU.mult, ALU.add))
                link(ts(src, src, -MAGIC, 1.0, ALU.add, ALU.min))
                last = ts(dst, src, -1.0, None, ALU.max)
            last.then_inc(setup_dve, 1)
            note(ts(wsum[:, 6:8], wsum[:, 2:4], 1 / 127.0, None, ALU.mult))
            dve.wait_ge(setup_act, 1)
            note(tt(th[:, 6, :], th[:, 5, :], w["wr"][:], ALU.mult))
            link(tt(th[:, 7, :], th[:, 4, :], w["wi"][:], ALU.mult))
            link(tt(th[:, 6, :], th[:, 6, :], th[:, 7, :], ALU.add))
            note(stt(th[:, 8, :], th[:, 6, :], 0.1, w["wi"][:], ALU.mult, ALU.mult))
            note(stt(th[:, 9, :], w["b13"][:], 0.1 / TWO_PI, th[:, 2, :], ALU.mult, ALU.add))
            link(stt(gk[:], w["qg"][:], RSQ8, w["kg"][:], ALU.mult, ALU.mult))
            dve.sem_inc(dve_free.sem, RING)

            with dve.Fori(0, ROUNDS) as rnd:
                dve.wait_ge(dve_step, 1)
                dve.sem_clear(dve_step)
                steps[0] = 0
                n_v, n_ln = [0], [0]

                def bank(*holds):
                    assert v_no[holds] == n_v[0], (holds, v_no[holds], n_v[0])
                    n_v[0] += 1
                    dve.wait_ge(dve_filled.sem, dve_filled.at(rnd, n_v[0]))
                    return bank_v[(n_v[0] - 1) % RING]

                def free(ins):
                    ins.then_inc(dve_free.sem, 1)

                def freed():
                    dve.wait_ge(dve_free.sem, drained(dve_free, rnd, n_v[0] - 1))

                def drained_a(*holds):
                    dve.wait_ge(act_free.sem, drained(act_free, rnd, a_no[holds]))

                tile = lambda a, i: a[:, i * P:(i + 1) * P]
                quarters = lambda b: b[:].rearrange("p (t d) -> p t d", t=T)
                by_head = lambda a: a.rearrange("p (h e) -> p h e", e=E8)

                def over_d(v, n):
                    return v.rearrange("p (a o) -> p a o", o=1).broadcast_to([P, v.shape[1], n])

                def norm_start(srcs, eps, rows=(P,) * T):
                    n = n_ln[0]
                    n_ln[0] += 1
                    for i in range(T):
                        last = dve.bn_stats(stats[0:rows[i], i, :], srcs(i))
                    link(last)
                    for i in range(T):
                        last = dve.bn_aggr(mv[0:rows[i], n % 2, i, :], stats[0:rows[i], i, :])
                    link(last)
                    ts(var[:, n % 2], mv[:, n % 2, :, 1], eps, None, ALU.add).then_inc(ln_var.sem, 1)
                    return n

                def mean(n, i, k=P):
                    return mv[0:k, n % 2, i, 0:1]

                def wait_rstd(n):
                    dve.wait_ge(ln_rstd.sem, ln_rstd.at(rnd, n + 1))

                def ln_start(s):
                    return norm_start(lambda i: X[s][:, i, :], 1e-5)

                def ln_end(n, s):
                    wait_rstd(n)
                    for i in range(T):
                        last = ts(XN[s][:, i, :], X[s][:, i, :], mean(n, i), rstd[:, n % 2, i:i + 1], ALU.subtract, ALU.mult)
                    last.then_inc(xn_ready.sem, 1)

                def layer_norm(s):
                    ln_end(ln_start(s), s)

                def both_norms():
                    ns = [ln_start(s) for s in range(SLOTS)]
                    for s in range(SLOTS):
                        ln_end(ns[s], s)

                def centre(n, srcs, dst, rows=(P,) * T):
                    for i, k in enumerate(rows):
                        last = stt(dst(i), srcs(i), mean(n, i, k), w["lng"][0:k], ALU.subtract, ALU.mult)
                    return last

                def scale(n, dst, rows=(P,) * T):
                    wait_rstd(n)
                    for i, k in enumerate(rows):
                        last = stt(dst(i), dst(i), rstd[0:k, n % 2, i:i + 1], w["lnb"][0:k], ALU.mult, ALU.add)
                    link(last)

                def add_to_x(s, b):
                    free(tt(X[s][:], X[s][:], quarters(b), ALU.add))
                    freed()

                def l0_attention():
                    for s in range(SLOTS):
                        for i in range(T):
                            n = a_no["l0_scores", s, i]
                            dve.wait_ge(act_filled.sem, act_filled.at(rnd, n + 1))
                            red(mx[:, s, i:i + 1], bank_a[n % RING][:, 0:C], AX, ALU.max, negate=True).then_inc(l0_shift.sem, 1)
                    ns = []
                    for s in range(SLOTS):
                        drained_a("l0_scores", s, T - 1)
                        link(dve.reciprocal(rsum[:, s], sums[:, s]))
                        b = bank("l0_out", s)
                        for i in range(T):
                            last = stt(X[s][:, i, :], tile(b, i), rsum[:, s, i:i + 1], X[s][:, i, :], ALU.mult, ALU.add)
                        free(last)
                        freed()
                        ns.append(ln_start(s))
                    for s in range(SLOTS):
                        ln_end(ns[s], s)

                def first_best(x, k):
                    link(red(gm[:, k, :], lg[:, x], AX, ALU.max))
                    link(tt(lg[:, k], lg[:, x], over_d(gm[:, k, :], NE), ALU.is_equal))
                    link(tt(lg[:, k], lg[:, k], const("desc").rearrange("p (o e) -> p o e", o=1).broadcast_to([P, T, NE]), ALU.mult))
                    link(red(gm[:, 7, :], lg[:, k], AX, ALU.max))
                    link(tt(lg[:, k], lg[:, k], over_d(gm[:, 7, :], NE), ALU.is_equal))

                def l0_gates(s):
                    b = bank("l0_logits", s)
                    free(cp(lg[:, 0].rearrange("p t e -> p (t e)"), b[:, 0:T * NE]))
                    freed()
                    link(red(gm[:, 0, :], lg[:, 0], AX, ALU.max))
                    tt(lg[:, 5], lg[:, 0], over_d(gm[:, 0, :], NE), ALU.subtract).then_inc(l0_shifted.sem, 1)
                    first_best(0, 1)
                    link(stt(lg[:, 2], lg[:, 1], -3.0e38, lg[:, 0], ALU.mult, ALU.add))
                    first_best(2, 3)
                    link(tt(lg[:, 3], lg[:, 3], lg[:, 1], ALU.add))
                    dve.wait_ge(l0_exps.sem, l0_exps.at(rnd, s + 1))
                    link(red(gm[:, 4, :], lg[:, 6], AX, ALU.add))
                    note(dve.reciprocal(gm[:, 5, :], gm[:, 4, :]))
                    link(tt(lg[:, 3], lg[:, 3], lg[:, 6], ALU.mult))
                    link(tt(GATE[s][:], lg[:, 3], over_d(gm[:, 5, :], NE), ALU.mult))

                def expert_sums(s, base, per):
                    for e in range(NE):
                        b = bank("down", base + per * e)
                        for i in range(T):
                            last = stt(X[s][:, i, :], tile(b, i), GATE[s][:, i, e:e + 1], X[s][:, i, :], ALU.mult, ALU.add)
                        free(last)
                        freed()

                def keys(a, s):
                    b = bank("kv", a, s)
                    kb = b[:].rearrange("p (x d) -> p x d", d=D)
                    if a == 0:
                        note(ts(KH[:, 0, :], kb[:, 0], RSQ8, None, ALU.mult))
                        ts(KH[0:CR, 1, :], kb[0:CR, 2], RSQ8, None, ALU.mult).then_inc(kh_ready.sem, 1)
                        dve.wait_ge(kh_ready.sem, kh_ready.at(rnd, s + 1))
                        hi = KH[:].bitcast(F32)
                        stt(KN[:, :, E8:2 * E8], by_head(kb[:, 0]), RSQ8, by_head(hi[:, 0, :]), ALU.mult, ALU.subtract)
                        stt(KNL[:, :, E8:2 * E8], by_head(kb[0:CR, 2]), RSQ8, by_head(hi[0:CR, 1, :]), ALU.mult, ALU.subtract)
                    else:
                        k32 = SQ[:, 0:2, :]
                        note(cp(k32[:, 0, :], kb[:, 0]))
                        link(cp(k32[0:CR, 1, :], kb[0:CR, 2]))
                        note(tt(SQ[:, 2, :], k32[:, 0, :], k32[:, 0, :], ALU.mult))
                        link(tt(SQ[0:CR, 3, :], k32[0:CR, 1, :], k32[0:CR, 1, :], ALU.mult))
                        note(red(msk[:, 0:H], by_head(SQ[:, 2, :]), AX, ALU.add))
                        link(red(msk[0:CR, H:2 * H], by_head(SQ[0:CR, 3, :]), AX, ALU.add))
                        ts(msk[:], msk[:], 1 / E8, 1e-6, ALU.mult, ALU.add).then_inc(kms_ready.sem, 1)
                        dve.wait_ge(krt_ready.sem, krt_ready.at(rnd, s + 1))
                        link(dve.reciprocal(msk[:], msk[:]))
                        for i, k in ((0, P), (1, CR)):
                            wide = msk[0:k, i * H:(i + 1) * H].rearrange("p (h o) -> p h o", o=1).broadcast_to([k, H, E8])
                            last = tt(by_head(k32[0:k, i, :]), by_head(k32[0:k, i, :]), wide, ALU.mult)
                        link(last)
                        for i, k in ((0, P), (1, CR)):
                            wide = gk[0:k].rearrange("p (o e) -> p o e", o=1).broadcast_to([k, H, E8])
                            last = tt(by_head(k32[0:k, i, :]), by_head(k32[0:k, i, :]), wide, ALU.mult)
                        link(last)
                        note(cp(KH[:, 0, :], k32[:, 0, :]))
                        cp(KH[0:CR, 1, :], k32[0:CR, 1, :]).then_inc(kh_ready.sem, 1)
                        dve.wait_ge(kh_ready.sem, kh_ready.at(rnd, 2 + s + 1))
                        hi = KH[:].bitcast(F32)
                        tt(KN[:, :, E8:2 * E8], by_head(k32[:, 0, :]), by_head(hi[:, 0, :]), ALU.subtract)
                        tt(KNL[:, :, E8:2 * E8], by_head(k32[0:CR, 1, :]), by_head(hi[0:CR, 1, :]), ALU.subtract)
                    for k in (0, 2):
                        cp(KN[:, :, k * E8:(k + 1) * E8], by_head(hi[:, 0, :]))
                        last = cp(KNL[:, :, k * E8:(k + 1) * E8], by_head(hi[0:CR, 1, :]))
                    last.then_inc(kn_ready.sem, 1)
                    cp(VA[s][:, :, 0:E8], by_head(kb[:, 1]))
                    free(tt(VL[s][:, :, 0:E8], by_head(kb[:, 3]),
                            const("jind").rearrange("p (h o) -> p h o", o=1).broadcast_to([P, H, E8]), ALU.mult))

                def queries(a, s):
                    b = bank("q", a, s)
                    n = 2 * a + s + 1
                    lo = QN[s][:].rearrange("p t h w -> p (t h) w")[:, :, 2 * E8:3 * E8]
                    heads = lambda v: v.rearrange("p t (h e) -> p (t h) e", e=E8)
                    if n > 1:
                        dve.wait_ge(qhh_ready.sem, qhh_ready.at(rnd, n - 1))
                    if a == 0:
                        cp(QH[:], quarters(b)).then_inc(qh_ready.sem, 1)
                        dve.wait_ge(qh_ready.sem, qh_ready.at(rnd, n))
                        free(tt(lo, by_head(b[:]), heads(QH[:].bitcast(F32)), ALU.subtract))
                    else:
                        free(cp(Q32[:], quarters(b)))
                        freed()
                        link(tt(SQ[:], Q32[:], Q32[:], ALU.mult))
                        link(red(ms[:], heads(SQ[:]), AX, ALU.add))
                        ts(ms[:], ms[:], 1 / E8, 1e-6, ALU.mult, ALU.add).then_inc(qms_ready.sem, 1)
                        dve.wait_ge(qrt_ready.sem, qrt_ready.at(rnd, s + 1))
                        link(dve.reciprocal(ms[:], ms[:]))
                        link(tt(heads(Q32[:]), heads(Q32[:]), over_d(ms[:], E8), ALU.mult))
                        cp(QH[:], Q32[:]).then_inc(qh_ready.sem, 1)
                        dve.wait_ge(qh_ready.sem, qh_ready.at(rnd, n))
                        note(tt(lo, heads(Q32[:]), heads(QH[:].bitcast(F32)), ALU.subtract))

                def maxima(a, s, i):
                    for c in range(NCH):
                        n = min(CH, H - c * CH)
                        b = bank("natural", a, s, i, c)
                        last = red(QN[s][:, i, c * CH:c * CH + n, 3 * E8], b[:, 0:n * C].rearrange("p (h c) -> p h c", c=C), AX, ALU.max, negate=True)
                        free(last)
                    dve.wait_ge(dve_free.sem, drained(dve_free, rnd, n_v[0] - 1))
                    dve.sem_inc(max_done.sem, 1)

                def heads_back(a, s, g):
                    b = bank("heads", a, s, g)
                    if g > 0:
                        dve.wait_ge(dve_free.sem, drained(dve_free, rnd, v_no["heads", a, s, g - 1]))
                    v = b[:].rearrange("p (t j w) -> p t j w", t=T, j=J)
                    link(dve.reciprocal(r16[:], v[:, :, :, E8]))
                    o = ATT[:].rearrange("p t (g j e) -> p t g j e", g=G, j=J)[:, :, g]
                    free(tt(o, v[:, :, :, 0:E8], r16[:].rearrange("p t (j o) -> p t j o", o=1).broadcast_to([P, T, J, E8]), ALU.mult))

                def attention(a):
                    queries(a, 0)
                    for i in range(T):
                        maxima(a, 0, i)
                    queries(a, 1)
                    for s in range(SLOTS):
                        for g in range(G + 2):
                            if s == 0 and g < T:
                                maxima(a, 1, g)
                            if g >= 2:
                                heads_back(a, s, g - 2)
                        freed()
                        dve.sem_inc(att_ready.sem, 1)
                        dve.wait_ge(x_added.sem, x_added.at(rnd, s + 1)) if a == 0 else None
                        add_to_x(s, bank("att_out", 4 * a + s))
                        if L > 2 + 4 * a + 1:
                            layer_norm(s)
                            if a == 0:
                                quantise_x(s)

                def quantise_x(s):
                    dve.wait_ge(xn_ready.sem, xn_ready.at(rnd, 2 * 3 + s + 1))
                    link(red(amax[:, 0, :], XN[s][:], AX, ALU.max, apply_absolute_value=True))
                    link(ts(amax[:, 0, :], amax[:, 0, :], 1e-5, None, ALU.max))
                    link(dve.reciprocal(amax[:, 1, :], amax[:, 0, :]))
                    link(ts(amax[:, 1, :], amax[:, 1, :], 127.0, None, ALU.mult))
                    for i in range(T):
                        last = ts(SQ[:, i, :], XN[s][:, i, :], amax[:, 1, i:i + 1], MAGIC, ALU.mult, ALU.add)
                    link(last)
                    ts(XQ[s], SQ[:], -MAGIC, 127.0, ALU.add, ALU.min).then_inc(xq_ready.sem, 1)
                    ts(amax[:, 3 + s, :], amax[:, 0, :], wsum[:, 6:7], None, ALU.mult).then_inc(rs_ready.sem, 1)

                def l1_ffn(s):
                    drained_a("SBC", s)
                    for k in range(NH + 1):
                        if k < NH:
                            b = bank("l1_hidden", s, k)
                            ins = tt(HP[:, k, 1:S + 1], b[:], SB_[:], ALU.mult)
                            free(ins)
                            freed()
                            dve.sem_inc(hp_ready.sem, 1)
                        if k > 0:
                            j = k - 1
                            dve.wait_ge(tap_ready.sem, tap_ready.at(rnd, s * NH + j + 1))
                            link(stt(CV[:, j, :], HP[:, j, 0:S], w["cw"][:, j, 0:1], CV[:, j, :], ALU.mult, ALU.add))
                            stt(CV[:, j, :], HP[:, j, 2:S + 2], w["cw"][:, j, 2:3], CV[:, j, :], ALU.mult, ALU.add).then_inc(conv_ready.sem, 1)
                    zb = []
                    for i in range(T):
                        b = bank("z", s, i)
                        zb.append(b)
                        last = red(amax[:, 0, i:i + 1], b[:], AX, ALU.max, apply_absolute_value=True)
                    link(last)
                    link(ts(amax[:, 0, :], amax[:, 0, :], 1e-5, None, ALU.max))
                    link(dve.reciprocal(amax[:, 1, :], amax[:, 0, :]))
                    note(ts(amax[:, 2, :], amax[:, 0, :], wsum[:, 7:8], None, ALU.mult))
                    link(ts(amax[:, 1, :], amax[:, 1, :], 127.0, None, ALU.mult))
                    for i in range(T):
                        z = sn[:, i, :]
                        free(ts(z, zb[i][:], amax[:, 1, i:i + 1], MAGIC, ALU.mult, ALU.add))
                        dve.wait_ge(dve_free.sem, drained(dve_free, rnd, v_no["z", s, i]))
                        ts(ZQ[:, i, :], z, -MAGIC, 127.0, ALU.add, ALU.min).then_inc(zq_ready.sem, 1)
                    b = bank("l1_out", s)
                    for i in range(T):
                        last = stt(X[s][:, i, :], tile(b, i), amax[:, 2, i:i + 1], X[s][:, i, :], ALU.mult, ALU.add)
                    free(last)
                    freed()

                def keys2(s):
                    b = bank("kv2", s)
                    rows = (P, P, CR, CR)
                    src = lambda i: b[0:rows[i], i * D:(i + 1) * D]
                    dst = lambda i: K2[0:rows[i], i, :]
                    n = norm_start(src, 1e-6, rows)
                    free(centre(n, src, dst, rows))
                    freed()
                    scale(n, dst, rows)
                    for i, k in ((0, P), (2, CR)):
                        last = ts(K2[0:k, i, :], K2[0:k, i, :], 0.0, 1e-6, ALU.max, ALU.add)
                    link(last)
                    for i, k, m in ((0, P, 0), (2, CR, 1)):
                        ts(K2[0:k, i, :], K2[0:k, i, :], EM[s][0:k, m:m + 1], None, ALU.mult)
                        last = ts(V2[0:k, m, 0:D], K2[0:k, i + 1, :], EM[s][0:k, m:m + 1], None, ALU.mult)
                    last.then_inc(kv2_ready.sem, 1)

                def keys2_sum(s):
                    b = bank("kv2_sum", s)
                    tt(KVB[s][:, 0:D], b[:, 0:D], const("blk"), ALU.mult)
                    free(tt(KVB[s][:, D:D + H], b[:, D:D + 1].broadcast_to([P, H]), const("ind16"), ALU.mult))
                    freed()
                    dve.sem_inc(kvb_ready.sem, 1)

                def l2_attention():
                    ns = []
                    for s in range(SLOTS):
                        b = bank("q2", s)
                        src, dst = lambda i: tile(b, i), lambda i: Q2[s][:, i, :]
                        ns.append(norm_start(src, 1e-6))
                        free(centre(ns[s], src, dst))
                        freed()
                    for s in range(SLOTS):
                        scale(ns[s], lambda i: Q2[s][:, i, :])
                        ts(Q2[s], Q2[s], 0.0, 1e-6, ALU.max, ALU.add).then_inc(q2_ready.sem, 1)
                    for s in range(SLOTS):
                        for i in range(0, T, 2):
                            b = bank("linear", s, i)
                            if s + i > 0:
                                dve.wait_ge(dve_free.sem, drained(dve_free, rnd, n_v[0] - 2))
                            v = b[:, 0:2 * (D + H)].rearrange("p (t x) -> p t x", t=2)
                            link(ts(den[:], v[:, :, D:D + H], 1e-6, None, ALU.add))
                            link(dve.reciprocal(den[:], den[:]))
                            o = ATT2[s][:, i:i + 2, :].rearrange("p t (e h) -> p t h e", h=H)
                            free(tt(o, v[:, :, 0:D].rearrange("p t (h e) -> p t h e", h=H),
                                    den[:].rearrange("p t (h o) -> p t h o", o=1).broadcast_to([P, 2, H, E8]), ALU.mult))
                        freed()
                        dve.sem_inc(att_ready.sem, 1)
                    if L > 6:
                        keys(1, 0)
                    ns = []
                    for s in range(SLOTS):
                        b = bank("att_out", 2 + s)
                        free(tt(Q2[s], quarters(b), w["bd2"][:].rearrange("p (o d) -> p o d", o=1).broadcast_to([P, T, D]), ALU.add))
                        freed()
                        q = lambda i: Q2[s][:, i, :]
                        ns.append(norm_start(q, 1e-6))
                        link(centre(ns[s], q, q))
                    ms_ = []
                    for s in range(SLOTS):
                        scale(ns[s], lambda i: Q2[s][:, i, :])
                        link(tt(X[s][:], X[s][:], Q2[s], ALU.add))
                        ms_.append(ln_start(s))
                    for s in range(SLOTS):
                        ln_end(ms_[s], s)
                    if L > 6:
                        keys(1, 1)

                def l2_ffn(s):
                    b = bank("l2_logits", s)
                    free(tt(lg[:, 0], b[:, 0:T * NE].rearrange("p (t e) -> p t e", e=NE),
                            w["bg"][:].rearrange("p (o e) -> p o e", o=1).broadcast_to([P, T, NE]), ALU.add))
                    freed()
                    first_best(0, 1)
                    cp(GATE[s][:], lg[:, 1]).then_inc(oh_ready.sem, 1)
                    dve.wait_ge(oh_ready.sem, oh_ready.at(rnd, s + 1))
                    expert_sums(s, SLOTS * 2 * NE + s * NE, 1)
                    add_to_x(s, bank("b2", s))

                def l3_ffn():
                    base = SLOTS * 3 * NE
                    for m in range(SLOTS * NH + 1):
                        if m < SLOTS * NH:
                            k = m % NH
                            u, r_ = sn[:, m % 2, :], PT[:, 8 + m % 2, :]
                            if m >= 2:
                                dve.wait_ge(phase_ready.sem, phase_ready.at(rnd, m - 1))
                            n = a_no["hidden", base + m]
                            dve.wait_ge(act_filled.sem, act_filled.at(rnd, n + 1))
                            ts(u, bank_a[n % RING][:], 0.1 / TWO_PI, th[:, 9, k:k + 1], ALU.mult, ALU.add).then_inc(turn_ready.sem, 1)
                            dve.wait_ge(turn_ready.sem, turn_ready.at(rnd, m + 1))
                            link(ts(r_, u, MAGIC, -MAGIC, ALU.add, ALU.add))
                            tt(HP[:, k, 1:S + 1], u, r_, ALU.subtract).then_inc(phase_ready.sem, 1)
                        if m > 0:
                            j = m - 1
                            v = sn[:, 2 + j % 2, :]
                            if j >= 2:
                                dve.wait_ge(relu_ready.sem, relu_ready.at(rnd, j - 1))
                            dve.wait_ge(sin_ready.sem, sin_ready.at(rnd, j + 1))
                            link(stt(v, HP[:, j % NH, 1:S + 1], th[:, 8, j % NH:j % NH + 1], CV[:, j % NH, :], ALU.mult, ALU.add))
                            ts(HT[:, (base + j) % NHT, :], v, 0.0, None, ALU.max).then_inc(relu_ready.sem, 1)
                    for s in range(SLOTS):
                        dve.wait_ge(x_added.sem, x_added.at(rnd, 2 + s + 1))
                        add_to_x(s, bank("l3_out", s))
                        dve.sem_inc(x_done.sem, 1)

                for s in range(SLOTS):
                    dve.wait_ge(x_loaded[s].sem, x_loaded[s].at(rnd, 1, 16))
                both_norms()
                l0_attention()
                wait_weights(dve, 2)
                keys(0, 0)
                for s in range(SLOTS):
                    keys2(s)
                    l0_gates(s)
                    expert_sums(s, s * 2 * NE, 2)
                    n = ln_start(s)
                    keys2_sum(s)
                    ln_end(n, s)
                    if s == 0:
                        keys(0, 1)
                attention(0)
                for s in range(SLOTS):
                    l1_ffn(s)
                    layer_norm(s)
                l2_attention()
                for s in range(SLOTS):
                    l2_ffn(s)
                    layer_norm(s)
                attention(1)
                l3_ffn()
                sync()
                assert n_v[0] == fills_v, n_v
                assert n_ln[0] == ln_var.n, n_ln


def kernel(**inputs):
    import concourse.bacc as bacc
    from concourse.bass_utils import run_bass_kernel_spmd

    a = {k: np.asarray(v) for k, v in inputs.items()}
    tiles = lambda v: v.reshape(NH, P).T
    words = lambda v: np.ascontiguousarray(v).view(np.uint32)
    laid = dict(
        consts=constants(),
        x=a["x"], ctx=a["ctx_1024"], ctxT=a["ctx_1024"].transpose(0, 2, 1),
        mask=words(a["mask_Bx1xSxS2_bk0"].reshape(NB, T, P, C).transpose(0, 2, 1, 3).reshape(NB, P, T * C)),
        maskT=words(a["mask_Bx1xSxS2_bk0"][:, 0].transpose(0, 2, 1)),
        em=a["mask_BxS2_ff1"][:, :, None],
        wg1=a["L0_ffn_wg1"], bg1=a["L0_ffn_bg1"][:, None], wg2=a["L0_ffn_wg2"], w_in=a["L0_ffn_w_in"], w_out=a["L0_ffn_w_out"],
        wq1=a["L1_xattn_W_q"].T, wk1=a["L1_xattn_W_k"].T, wv1=a["L1_xattn_W_v"].T, wp1=a["L1_xattn_W_proj"].T, bp1=a["L1_xattn_b_proj"],
        w1b=a["L1_ffn_w1"].T, cw=a["L1_ffn_conv_w"].reshape(NH, P, 3).transpose(1, 0, 2), cb=tiles(a["L1_ffn_conv_b"]), w2b=a["L1_ffn_w2"].T,
        wq2=a["L2_xattn_wq"], wk2=a["L2_xattn_wk"], wv2=a["L2_xattn_wv"], lng=a["L2_xattn_ln_gamma"], lnb=a["L2_xattn_ln_beta"],
        wd2=a["L2_xattn_dense_w"], bd2=a["L2_xattn_dense_b"],
        wg=a["L2_ffn_Wg"], bg=a["L2_ffn_bg"], w1e=a["L2_ffn_W1"], b1e=a["L2_ffn_b1"].T, w2e=a["L2_ffn_W2"], b2e=a["L2_ffn_b2"],
        wq3=a["L3_xattn_Wq"], wkv3=a["L3_xattn_Wkv"], wp3=a["L3_xattn_Wproj"], qg=a["L3_xattn_q_gamma"], kg=a["L3_xattn_k_gamma"],
        w13=a["L3_ffn_W1"], b13=tiles(a["L3_ffn_b1"]), ph=tiles(a["L3_ffn_quantum_phases"]), wr=tiles(a["L3_ffn_quantum_weights_real"]),
        wi=tiles(a["L3_ffn_quantum_weights_imag"]), w23=a["L3_ffn_W2"], b23=a["L3_ffn_b2"],
    )
    nc = bacc.Bacc("TRN2", target_bir_lowering=False, num_devices=1)
    arrays, aps = {}, {}
    for name, v in laid.items():
        v = np.ascontiguousarray(v)
        arrays[f"in_{name}"] = v
        aps[name] = nc.dram_tensor(f"in_{name}", v.shape, mybir.dt.from_np(v.dtype), kind="ExternalInput").ap()
    out = nc.dram_tensor("out", (NB, S, D), F32, kind="ExternalOutput").ap()
    build(nc, aps, out)
    return run_bass_kernel_spmd(nc, [arrays], core_ids=[0]).results[0]["out"]
```

```python
from contextlib import ExitStack

import numpy as np

import concourse.bass as bass
from concourse import mybir

F32 = mybir.dt.float32
F32R = mybir.dt.float32r
BF16 = mybir.dt.bfloat16
U8 = mybir.dt.uint8
U32 = mybir.dt.uint32
ALU = mybir.AluOpType
ACT = mybir.ActivationFunctionType
AX = mybir.AxisListType.X

P = 128
NB, S, D = 4, 512, 128
T = S // P
C = 154
CR = C - P
H, E8 = 16, 8
G, J = 4, 4
W = 32
NE = 8
HID0 = 256
FF = 512
NH = FF // P
SLOTS, ROUNDS = 2, 2
RING = 4
CH = 3
NCH = -(-H // CH)
NPT = 10
NHT = 8
BIG = 2.0 ** 100
MAGIC = 1.5 * 2.0 ** 23
TWO_PI = 2 * np.pi
PI_A, PI_B = 6.28125, 0.0019350051879882812
PI_C = float(TWO_PI - PI_A - PI_B)
SIN_SCALE = 6.283185
RSQ8 = float(1 / np.sqrt(8.0))

FILLS_ACT, FILLS_DVE, NORMS = 234, 196, 22
N_ATT = 4

CONSTS = {}
_at = 0
for _n, _w in (("ident", 128), ("blk", 128), ("rsel", 128), ("ind16", 16), ("jind", 16), ("jrem", 16), ("ind4", 4), ("desc", 8)):
    CONSTS[_n] = (_at, _at + _w)
    _at += _w
NCONST = _at


def constants():
    c = np.zeros((P, NCONST), np.float32)
    p = np.arange(P)[:, None]

    def put(name, v):
        a, b = CONSTS[name]
        c[:, a:b] = v

    q = np.arange(P)[None]
    put("ident", p == q)
    put("blk", p // E8 == q // E8)
    put("rsel", (q % W == p) & (p < CR))
    h = np.arange(H)[None]
    put("ind16", p // E8 == h)
    put("jind", p // W == h % J)
    put("jrem", (p // W == h % J) & (p % W < CR))
    put("ind4", p // W == np.arange(J)[None])
    put("desc", NE - np.arange(NE)[None] + 0 * p)
    return c


def build(nc, t, out):
    ctx = ExitStack()
    with ctx:
        def sb(name, shape, dt=F32):
            return ctx.enter_context(nc.sbuf_tensor(name, shape, dt))

        def sem(name):
            return ctx.enter_context(nc.semaphore(name))

        bank_a = [ctx.enter_context(nc.psum_tensor(f"act_bank{i}", [P, 512], F32)) for i in range(RING)]
        bank_v = [ctx.enter_context(nc.psum_tensor(f"dve_bank{i}", [P, 512], F32)) for i in range(RING)]

        consts = sb("consts", [P, NCONST])

        def const(name):
            a, b = CONSTS[name]
            return consts[:, a:b]

        ident = const("ident")
        ident_bf = sb("ident_bf", [P, P], BF16)
        rsel_bf = sb("rsel_bf", [P, P], BF16)
        ones_row = sb("ones_row", [P, P])

        two = lambda name, shape, dt=F32: [sb(f"{name}{s}", shape, dt) for s in range(SLOTS)]
        X = two("X", [P, T, D])
        XN = two("XN", [P, T, D])
        XT = two("XT", [P, S])
        CT = two("CT", [P, C])
        CT4 = two("CT4", [P, J, W])
        CN = two("CN", [P, D])
        CL = two("CL", [CR, D])
        MRAW = two("MRAW", [P, T * C // 4], U32)
        MTRAW = two("MTRAW", [P, S // 4], U32)
        MLRAW = two("MLRAW", [CR, S // 4], U32)
        MN = two("MN", [P, T, C], BF16)
        MT = two("MT", [P, S], BF16)
        ML = two("ML", [CR, S], BF16)
        EM = two("EM", [P, 2])
        KBN = sb("KBN", [P, H, C], F32R)
        CV = sb("CV", [P, NH, S])
        KBM = two("KBM", [P, G, J, P], F32R)
        KBL = two("KBL", [P, G, J, W], F32R)
        VA = two("VA", [P, H, W])
        VL = two("VL", [P, H, W])
        QTC = two("QTC", [P, S], F32R)
        QN = two("QN", [P, T, H, W])
        KVB = two("KVB", [P, D + H])
        GATE = two("GATE", [P, T, NE])

        QH = sb("QH", [P, T, D], F32R)
        KH = sb("KH", [P, 2, D], F32R)
        KN = sb("KN", [P, H, W])
        KNL = sb("KNL", [CR, H, W])
        KTC = sb("KTC", [P, C])
        KS = sb("KS", [P, G, C])
        QS = [sb(f"QS{i}", [P, S], F32R) for i in range(2)]
        PT = sb("PT", [P, NPT, S])
        HT = sb("HT", [P, NHT, S])
        UT = sb("UT", [P, 2, S])
        K2 = sb("K2", [P, 4, D])
        V2 = sb("V2", [P, 2, D + 1])
        SQ = sb("SQ", [P, T, D])
        HP = sb("HP", [P, NH, S + 2])

        tokens = lambda a: a.rearrange("p (t d) -> p t d", t=T)
        slots = range(SLOTS)
        ht_bf = HT[:, 0:4, :].bitcast(BF16)
        ks_row = KS[:].rearrange("p g c -> p (g c)")[:, 0:S]
        XIN = [tokens(PT[:, 8 + s, :]) for s in slots]
        PN = [PT[:, 2 * s:2 * s + 2, :].rearrange("p a n -> p (a n)")[:, 0:T * C].rearrange("p (t c) -> p t c", t=T) for s in slots]
        PNT, PNL = [PT[:, 4 + s, :] for s in slots], [PT[0:CR, 6 + s, :] for s in slots]
        GT = UT[0:32, 0, :]
        ATT, AT, Q32 = tokens(HT[:, 7, :]), UT[:, 1, :], tokens(PT[:, 9, :])
        XQ = [HT[:, 4, :].bitcast(BF16)[:, s * S:(s + 1) * S].rearrange("p (t d) -> p t d", t=T) for s in slots]
        XQT, SB_ = HT[:, 5, :].bitcast(BF16)[:, 0:S], ks_row
        LEFT = [HT[:, 2 + i, :] for i in range(2)]
        ROUNDED = [SQ[:].rearrange("p t d -> p (t d)"), HT[:, 6, :]]
        ZQ = ht_bf[:, 0:2, :].rearrange("p a (b n) -> p (a b) n", b=2)
        ZT = ht_bf[:, 2:4, :].rearrange("p a (b n) -> p (a b) n", b=2)
        Q2, Q2T = [tokens(PT[:, s, :]) for s in slots], [UT[:, s, :] for s in slots]
        ATT2 = [tokens(PT[:, 2 + s, :]) for s in slots]
        HEADS_T, GROUPS_T = [PT[:, 4 + s, :] for s in slots], [PT[:, 6 + s, :] for s in slots]
        exchange = [nc.dram_tensor(f"exchange{s}", [H, P, S // H], F32).ap() for s in slots]
        OHT = UT[0:NE, 1, :]
        TURNS = [(HT[:, 4, :], ks_row), (HT[:, 5, :], HT[:, 6, :])]

        stats = sb("stats", [P, T, 6])
        mv = sb("mv", [P, 2, T, 2])
        var = sb("var", [P, 2, T])
        rstd = sb("rstd", [P, 2, T])
        mhalf = sb("mhalf", [P, T])
        mx = sb("mx", [P, 2, T])
        sums = sb("sums", [P, 2, T])
        rsum = sb("rsum", [P, 2, T])
        r16 = sb("r16", [P, T, J])
        den = sb("den", [P, 2, H])
        ms = sb("ms", [P, T * H])
        msk = sb("msk", [P, 2 * H])
        lg = sb("lg", [P, 8, T, NE])
        gm = sb("gm", [P, 8, T])
        amax = sb("amax", [P, 5, T])
        th = sb("th", [P, 12, NH])

        wshape = dict(
            wg1=[D, 32], bg1=[32, 1], wg2=[32, NE], w_in=[D, NE, HID0], w_out=[P, 2 * NE, D],
            wq1=[D, D], wkv1=[D, 2, D], wp1=[D, D], bp1=[P, D],
            cw=[P, NH, 3], cb=[P, NH],
            wq2=[D, D], wkv2=[D, 2, D], lng=[P, D], lnb=[P, D], wd2=[D, D], bd2=[P, D],
            wg=[D, NE], bg=[P, NE], w1e=[D, NE, P], b1e=[P, NE], w2e=[P, NE, D], b2e=[NE, D],
            wq3=[D, D], wkv3=[D, 2 * D], wp3=[D, D], qg=[P, E8], kg=[P, E8],
            w13=[D, FF], w23=[P, NH, D], b23=[P, D],
        )
        w = {k: sb("w_" + k, v) for k, v in wshape.items()}
        l3v = sb("l3v", [P, 4, NH])
        w["b13"], w["ph"], w["wr"], w["wi"] = [l3v[:, k, :] for k in range(4)]
        w["w1b"], w["w2b"] = PT[:, 0, :], PT[:, 1, :].rearrange("p (k d) -> p k d", k=NH)
        w1q = sb("w1q", [D, FF], BF16)
        w2q = sb("w2q", [P, NH, D], BF16)
        wsum = sb("wsum", [P, 8])
        gk = sb("gk", [P, E8])

        class Signal:
            def __init__(self, name, n):
                self.sem, self.n, self.name = sem(name), n, name

            def at(self, rnd, n, step=1):
                assert 1 <= n <= self.n, (self.name, n)
                return rnd * (self.n * step) + n * step

        fills_a, fills_v = FILLS_ACT, FILLS_DVE
        act_filled, act_free = Signal("act_bank_filled", fills_a), Signal("act_bank_free", fills_a)
        dve_filled, dve_free = Signal("dve_bank_filled", fills_v), Signal("dve_bank_free", fills_v)
        loaded = [sem(n) for n in ("first_weights_loaded", "layer0_weights_loaded", "weights_loaded")]
        consts_loaded = sem("consts_loaded")
        setup_pool = sem("setup_pool")
        setup_dve = sem("setup_dve")
        setup_act = sem("setup_act")
        setup_pe = sem("setup_pe")
        x_done = Signal("x_done", 2)
        x_loaded = [Signal(f"x_loaded{s}", 1) for s in range(SLOTS)]
        ctx_loaded = [Signal(f"ctx_loaded{s}", 6) for s in range(SLOTS)]
        mask_loaded = [Signal(f"mask_loaded{s}", 3) for s in range(SLOTS)]
        stored = [Signal(f"stored{s}", 1) for s in range(SLOTS)]
        mask_ready = Signal("mask_ready", 2)
        ln_var = Signal("ln_var", NORMS)
        ln_rstd = Signal("ln_rstd", NORMS)
        xn_ready = Signal("xn_ready", 16)
        x_added = Signal("x_added", 4)
        dve_step = sem("dve_step")
        pool_step = sem("pool_step")
        pool_waited = sem("pool_waited")
        l0_shift = Signal("l0_shift", 2 * T)
        l0_shifted = Signal("l0_shifted", 2)
        l0_exps = Signal("l0_exps", 2)
        kn_ready = Signal("kn_ready", N_ATT)
        kh_ready = Signal("kh_ready", N_ATT)
        kbn_ready = Signal("kbn_ready", N_ATT)
        kb_ready = Signal("kb_ready", N_ATT)
        kms_ready = Signal("kms_ready", 2)
        krt_ready = Signal("krt_ready", 2)
        qms_ready = Signal("qms_ready", 2)
        qrt_ready = Signal("qrt_ready", 2)
        qh_ready = Signal("qh_ready", N_ATT)
        qhh_ready = Signal("qhh_ready", N_ATT)
        exchange_written = Signal("exchange_written", 2)
        exchange_read = [Signal(f"exchange_read{s}", 1) for s in range(SLOTS)]
        xq_ready = Signal("xq_ready", 2)
        rs_ready = Signal("rs_ready", 2)
        tap_ready = Signal("tap_ready", 2 * NH)
        left_ready = Signal("left_ready", 2 * NH)
        conv_ready = Signal("conv_ready", 2 * NH)
        z_ready = Signal("z_ready", 2 * NH)
        zq_ready = Signal("zq_ready", 2 * T)
        kv2_ready = Signal("kv2_ready", 2)
        q2_ready = Signal("q2_ready", 2)
        oh_ready = Signal("oh_ready", 2)
        turn_ready = Signal("turn_ready", 2 * NH)
        phase_ready = Signal("phase_ready", 2 * NH)
        whole_ready = Signal("whole_ready", 2 * NH)
        turned_ready = Signal("turned_ready", 2 * NH)
        relu_ready = Signal("relu_ready", 2 * NH)
        sin_ready = Signal("sin_ready", 2 * NH)

        block = ctx.enter_context(nc.Block())

        a_no, v_no = {}, {}

        def drained(sig, rnd, n):
            return rnd * sig.n + RING + n + 1

        def free_value(sig, rnd, n):
            return rnd * sig.n + max(RING, n + 1)

        r = lambda n, pat, **k: t[n].rearrange(pat, **k)
        row = lambda n: t[n].rearrange("(o n) -> o n", o=1).broadcast_to([P, t[n].shape[0]])
        wsrc = [[
            (w["w1b"], t["w1b"]), (w["w2b"], r("w2b", "(k p) d -> p k d", p=P)),
            (w["qg"][:], row("qg")), (w["kg"][:], row("kg")),
            (l3v[:], t["l3v"]),
        ], [
            (w["wg1"][:], t["wg1"]), (w["bg1"][:], t["bg1"]), (w["wg2"][:], t["wg2"]),
            (w["w_in"][:], r("w_in", "e d h -> d e h")), (w["w_out"][:], r("w_out", "e (k p) d -> p (e k) d", p=P)),
        ], [
            (w["wkv1"][:, 0, :], t["wk1"]), (w["wkv1"][:, 1, :], t["wv1"]), (w["wq1"][:], t["wq1"]),
            (w["wp1"][:], t["wp1"]), (w["bp1"][:], row("bp1")),
            (w["cw"][:], t["cw"]), (w["cb"][:], t["cb"]),
            (w["wq2"][:], t["wq2"]), (w["wkv2"][:, 0, :], t["wk2"]), (w["wkv2"][:, 1, :], t["wv2"]),
            (w["lng"][:], row("lng")), (w["lnb"][:], row("lnb")), (w["wd2"][:], t["wd2"]), (w["bd2"][:], row("bd2")),
            (w["wg"][:], t["wg"]), (w["bg"][:], row("bg")), (w["w1e"][:], r("w1e", "e d h -> d e h")),
            (w["b1e"][:], t["b1e"]), (w["w2e"][:], r("w2e", "e h d -> h e d")), (w["b2e"][:], t["b2e"]),
            (w["wq3"][:], t["wq3"]), (w["wkv3"][:], t["wkv3"]), (w["wp3"][:], t["wp3"]),
            (w["w13"][:], t["w13"]),
            (w["w23"][:], r("w23", "(k p) d -> p k d", p=P)), (w["b23"][:], row("b23")),
        ]]

        def wait_weights(eng, k):
            eng.wait_ge(loaded[k], 16 * len(wsrc[k]))

        @block.tensor
        def _(pe):
            pe.wait_ge(consts_loaded, 16)
            pe.wait_ge(setup_pool, 1)
            pe.wait_ge(setup_dve, 1)
            pe.matmul(bank_v[0][:, 0:2], ones_row[:], wsum[:, 0:2], start=True, stop=True).then_inc(setup_pe, 1)
            pe.wait_ge(setup_dve, 3)

            with pe.Fori(0, ROUNDS) as rnd:
                n_a, n_v = [0], [0]

                def open_a(*holds):
                    a_no[holds] = n_a[0]
                    pe.wait_ge(act_free.sem, free_value(act_free, rnd, n_a[0]))
                    n_a[0] += 1
                    return bank_a[(n_a[0] - 1) % RING]

                def open_v(*holds):
                    v_no[holds] = n_v[0]
                    pe.wait_ge(dve_free.sem, free_value(dve_free, rnd, n_v[0]))
                    n_v[0] += 1
                    return bank_v[(n_v[0] - 1) % RING]

                def wait_a(*holds):
                    pe.wait_ge(act_free.sem, drained(act_free, rnd, a_no[holds]))

                def wait_v(*holds):
                    pe.wait_ge(dve_free.sem, drained(dve_free, rnd, v_no[holds]))

                def mm(o, lhs, rhs, start=True, stop=True, **k):
                    return pe.matmul(o, lhs, rhs, start=start, stop=stop, **k)

                def tr(o, i, id_=None):
                    k = i.shape[0]
                    return pe.matmul(o, i, (ident if id_ is None else id_)[0:k, 0:k], start=True, stop=True, is_transpose=True)

                def four_transposes(holds, src, rows=P):
                    b = open_a(*holds)
                    for i in range(T):
                        last = tr(b[0:rows, i * P:(i + 1) * P], src(i))
                    last.then_inc(act_filled.sem, 1)

                def norm_t(layer, s):
                    pe.wait_ge(xn_ready.sem, xn_ready.at(rnd, 2 * layer + s + 1))
                    four_transposes(("XT", layer, s), lambda i: XN[s][:, i, :])

                def wait_xt(layer, s):
                    wait_a("XT", layer, s)

                def tile(a, i):
                    return a[:, i * P:(i + 1) * P]

                def project(holds, src, wt):
                    b = open_v(*holds)
                    for i in range(T):
                        last = mm(tile(b, i), tile(src, i), wt)
                    last.then_inc(dve_filled.sem, 1)

                def l0_attention():
                    for s in range(SLOTS):
                        wait_xt(0, s)
                        pe.wait_ge(ctx_loaded[s].sem, ctx_loaded[s].at(rnd, ctx_loaded[s].n, 16))
                        for i in range(T):
                            b = open_a("l0_scores", s, i)
                            mm(b[:, 0:C], tile(XT[s], i), CT[s][:]).then_inc(act_filled.sem, 1)
                    for s in range(SLOTS):
                        wait_a("l0_scores", s, T - 1)
                        four_transposes(("PNT", s), lambda i: PN[s][:, i, 0:P])
                        four_transposes(("PNL", s), lambda i: PN[s][:, i, P:C], CR)
                    for s in range(SLOTS):
                        wait_a("PNL", s)
                        b = open_v("l0_out", s)
                        for i in range(T):
                            mm(tile(b, i), tile(PNT[s], i), CN[s][:], stop=False)
                            last = mm(tile(b, i), tile(PNL[s], i), CL[s][:], start=False)
                        last.then_inc(dve_filled.sem, 1)

                def expert_up(n, s, wt):
                    b = open_a("hidden", n)
                    mm(b[:], wt, XT[s][:]).then_inc(act_filled.sem, 1)

                def expert_down(n, wts):
                    b = open_v("down", n)
                    wait_a("hidden", n + len(wts) - 1)
                    for i in range(T):
                        for k, wt in enumerate(wts):
                            last = mm(tile(b, i), tile(HT[:, (n + k) % NHT, :], i), wt, start=k == 0, stop=k == len(wts) - 1)
                    last.then_inc(dve_filled.sem, 1)

                def l0_ffn(s):
                    wait_xt(1, s)
                    b = open_a("GT", s)
                    mm(b[0:32, :], w["wg1"][:], XT[s][:]).then_inc(act_filled.sem, 1)
                    base = s * 2 * NE
                    up = lambda e: [expert_up(base + 2 * e + k, s, w["w_in"][:, e, k * P:(k + 1) * P]) for k in range(2)]
                    up(0)
                    wait_a("GT", s)
                    b = open_v("l0_logits", s)
                    for i in range(T):
                        last = mm(b[:, i * NE:(i + 1) * NE], GT[:, i * P:(i + 1) * P], w["wg2"][:])
                    last.then_inc(dve_filled.sem, 1)
                    for e in range(NE):
                        if e + 1 < NE:
                            up(e + 1)
                        if s == 1 and e == 0:
                            queries_norm(0, 0)
                        if s == 1 and e == 1:
                            queries(0, 0)
                        if s == 1 and e == 2:
                            queries_back(0, 0)
                        if s == 1 and e in (5, 6):
                            natural_scores(0, 0, e - 5)
                        expert_down(base + 2 * e, [w["w_out"][:, 2 * e + k, :] for k in range(2)])

                def kv_products(a, s):
                    wk, wv = (w["wkv1"][:, 0, :], w["wkv1"][:, 1, :]) if a == 0 else (w["wkv3"][:, 0:D], w["wkv3"][:, D:2 * D])
                    b = open_v("kv", a, s)
                    mm(b[:, 0:128], CT[s][:, 0:P], wk)
                    mm(b[:, 128:256], CT[s][:, 0:P], wv)
                    mm(b[0:CR, 256:384], CT[s][:, P:C], wk)
                    mm(b[:, 384:512], CT4[s][:, :, :].rearrange("p j w -> p (j w)"), wv).then_inc(dve_filled.sem, 1)

                def k_transposes(a, s):
                    n = 2 * a + s + 1
                    pe.wait_ge(kh_ready.sem, kh_ready.at(rnd, n))
                    b = open_a("KTC", a, s)
                    tr(b[:, 0:P], KH[:, 0, :].bitcast(F32))
                    tr(b[:, P:C], KH[0:CR, 1, :].bitcast(F32)).then_inc(act_filled.sem, 1)
                    pe.wait_ge(kn_ready.sem, kn_ready.at(rnd, n))
                    for g0, g1 in ((0, 3), (3, G)):
                        b = open_a("KS", a, s, g0)
                        for g in range(g0, g1):
                            o = (g - g0) * C
                            tr(b[:, o:o + P], KN[:, J * g:J * g + J, :].rearrange("p j w -> p (j w)"))
                            last = tr(b[:, o + P:o + C], KNL[:, J * g:J * g + J, :].rearrange("p j w -> p (j w)"))
                        last.then_inc(act_filled.sem, 1)

                def queries_norm(a, s):
                    norm_t(2 if a == 0 else 6, s)

                def queries(a, s):
                    wait_xt(2 if a == 0 else 6, s)
                    project(("q", a, s), XT[s], w["wq1"][:] if a == 0 else w["wq3"][:])

                def queries_back(a, s):
                    pe.wait_ge(qh_ready.sem, qh_ready.at(rnd, 2 * a + s + 1))
                    four_transposes(("QTC", a, s), lambda i: QH[:, i, :].bitcast(F32))
                    wait_a("QTC", a, s)
                    if a == 0:
                        pe.wait_ge(mask_ready.sem, mask_ready.at(rnd, s + 1))

                def natural_scores(a, s, i):
                    if i == 0:
                        pe.wait_ge(kbn_ready.sem, kbn_ready.at(rnd, 2 * a + s + 1))
                    for c in range(NCH):
                        n = min(CH, H - c * CH)
                        b = open_v("natural", a, s, i, c)
                        o = b[:, 0:n * C]
                        last = mm(o, tile(QTC[s], i), KBN[:, c * CH:c * CH + n, :], stop=a == 1)
                        if a == 0:
                            m = MN[s][:, i:i + 1, :].broadcast_to([P, n, C])
                            last = mm(o, ident_bf[:], m, start=False)
                        last.then_inc(dve_filled.sem, 1)

                def split_queries(a, s, g):
                    if g == 0:
                        wait_v("natural", a, s, T - 1, NCH - 1)
                        pe.wait_ge(qhh_ready.sem, qhh_ready.at(rnd, 2 * a + s + 1))
                        pe.wait_ge(kb_ready.sem, kb_ready.at(rnd, 2 * a + s + 1))
                    four_transposes(("QS", a, s, g), lambda i: QN[s][:, i, J * g:J * g + J, :].rearrange("p j w -> p (j w)"))

                def scores(a, s, g):
                    n = (2 * a + s) * G + g
                    wait_a("QS", a, s, g)
                    q = QS[n % 2]
                    for j in range(J):
                        b = open_a("scores", a, s, g, j)
                        last = mm(b[:], KBM[s][:, g, j, :], q[:], stop=a == 1)
                        if a == 0:
                            last = mm(b[:], ident_bf[:], MT[s][:], start=False)
                        last.then_inc(act_filled.sem, 1)
                    b = open_a("scores", a, s, g, J)
                    last = mm(b[:], KBL[s][:, g, :, :].rearrange("p j w -> p (j w)"), q[:], stop=a == 1)
                    if a == 0:
                        last = mm(b[:], rsel_bf[0:CR, :], ML[s][:], start=False)
                    last.then_inc(act_filled.sem, 1)

                def values(a, s, g):
                    n = (2 * a + s) * G + g
                    if g == 0:
                        wait_v("kv", a, s)
                    b = open_a("UT", a, s, g)
                    base = (n % 2) * (J + 1)
                    wait_a("scores", a, s, g, J)
                    for j in range(J):
                        mm(b[W * j:W * j + W, :], VA[s][:, J * g + j, :], PT[:, base + j, :], stop=False, tile_position=(0, W * j))
                    for j in range(J):
                        last = mm(b[W * j:W * j + W, :], VL[s][:, J * g + j, :], PT[:, base + J, :], start=False, tile_position=(0, W * j))
                    last.then_inc(act_filled.sem, 1)

                def heads_back(a, s, g):
                    n = (2 * a + s) * G + g
                    wait_a("UT", a, s, g)
                    b = open_v("heads", a, s, g)
                    for i in range(T):
                        last = tr(tile(b, i), tile(UT[:, n % 2, :], i))
                    last.then_inc(dve_filled.sem, 1)

                def attention_back(n):
                    wait_v("heads", n // 4, n % 4, G - 1)
                    four_transposes(("AT", n), lambda i: ATT[:, i, :])

                def attention_out(n):
                    wait_a("AT", n)
                    project(("att_out", n), AT, w["wp1"][:] if n < 2 else w["wp3"][:])

                def attention(a):
                    natural_scores(a, 0, 2)
                    queries_norm(a, 1)
                    queries(a, 1)
                    natural_scores(a, 0, 3)
                    queries_back(a, 1)
                    split_queries(a, 0, 0)
                    for g in range(G + 2):
                        if 1 <= g <= T:
                            natural_scores(a, 1, g - 1)
                        if g + 1 < G:
                            split_queries(a, 0, g + 1)
                        if g < G:
                            scores(a, 0, g)
                        if 1 <= g <= G:
                            values(a, 0, g - 1)
                        if g >= 2:
                            heads_back(a, 0, g - 2)
                    split_queries(a, 1, 0)
                    for g in range(G + 2):
                        if g + 1 < G:
                            split_queries(a, 1, g + 1)
                        if g == 0:
                            attention_back(4 * a)
                        if g == 2 and a == 0:
                            l1_quantised(0)
                        if g == 2 and a == 1:
                            l3_up(0)
                        if g < G:
                            scores(a, 1, g)
                        if g == 0:
                            attention_out(4 * a)
                        if 1 <= g <= G:
                            values(a, 1, g - 1)
                        if g >= 2:
                            heads_back(a, 1, g - 2)
                        if g == 1 and a == 0:
                            kv_products(1, 0)
                        if g == 2 and a == 0:
                            l1_up(0)
                        if g == 4 and a == 0:
                            l1_z(0)
                        if g == 4 and a == 1:
                            l3_down(0)
                    if a == 0:
                        l1_zt(0)
                    attention_back(4 * a + 1)
                    if a == 0:
                        l1_down(0)
                    attention_out(4 * a + 1)

                def l1_quantised(s):
                    pe.wait_ge(xq_ready.sem, xq_ready.at(rnd, s + 1))
                    b = open_a("XQT", s)
                    for i in range(T):
                        last = tr(b[:].bitcast(BF16)[:, i * P:(i + 1) * P], XQ[s][:, i, :], ident_bf)
                    last.then_inc(act_filled.sem, 1)
                    pe.wait_ge(rs_ready.sem, rs_ready.at(rnd, s + 1))
                    b = open_a("SBC", s)
                    for i in range(T):
                        last = mm(tile(b, i), amax[:, 3 + s, i:i + 1].broadcast_to([P, P]), ident)
                    last.then_inc(act_filled.sem, 1)

                def l1_up(s):
                    wait_a("XQT", s)
                    for k in range(NH):
                        b = open_v("l1_hidden", s, k)
                        mm(b[:], w1q[:, k * P:(k + 1) * P], XQT[:]).then_inc(dve_filled.sem, 1)

                def l1_z(s):
                    for i in range(T):
                        b = open_v("z", s, i)
                        for k in range(NH):
                            if i == 0:
                                pe.wait_ge(z_ready.sem, z_ready.at(rnd, s * NH + k + 1))
                            last = tr(tile(b, k), CV[:, k, i * P:(i + 1) * P])
                        last.then_inc(dve_filled.sem, 1)

                def l1_zt(s):
                    for i in range(T):
                        b = open_a("ZT", s, i)
                        pe.wait_ge(zq_ready.sem, zq_ready.at(rnd, s * T + i + 1))
                        for k in range(NH):
                            last = tr(b[:].bitcast(BF16)[:, k * P:(k + 1) * P], ZQ[:, i, k * P:(k + 1) * P], ident_bf)
                        last.then_inc(act_filled.sem, 1)

                def l1_down(s):
                    b = open_v("l1_out", s)
                    for i in range(T):
                        wait_a("ZT", s, i)
                        for k in range(NH):
                            last = mm(tile(b, i), ZT[:, k, i * P:(i + 1) * P], w2q[:, k, :], start=k == 0, stop=k == NH - 1)
                    last.then_inc(dve_filled.sem, 1)

                def kv2_products(s):
                    b = open_v("kv2", s)
                    r = w["wkv2"][:].rearrange("p i d -> p (i d)")
                    mm(b[:, 0:256], CT[s][:, 0:P], r)
                    mm(b[0:CR, 256:512], CT[s][:, P:C], r).then_inc(dve_filled.sem, 1)

                def kv2_sum(s):
                    pe.wait_ge(kv2_ready.sem, kv2_ready.at(rnd, s + 1))
                    b = open_v("kv2_sum", s)
                    mm(b[:, 0:D + 1], K2[:, 0, :], V2[:, 0, :], stop=False)
                    mm(b[:, 0:D + 1], K2[0:CR, 2, :], V2[0:CR, 1, :], start=False).then_inc(dve_filled.sem, 1)

                def q2(s):
                    norm_t(4, s)
                    wait_xt(4, s)
                    project(("q2", s), XT[s], w["wq2"][:])

                def q2_back(s):
                    pe.wait_ge(q2_ready.sem, q2_ready.at(rnd, s + 1))
                    four_transposes(("Q2T", s), lambda i: Q2[s][:, i, :])

                def linear(s):
                    wait_a("Q2T", s)
                    assert v_no["kv2_sum", s] + RING <= n_v[0]
                    for i in range(0, T, 2):
                        b = open_v("linear", s, i)
                        mm(b[:, 0:D + H], tile(Q2T[s], i), KVB[s][:])
                        mm(b[:, D + H:2 * (D + H)], tile(Q2T[s], i + 1), KVB[s][:]).then_inc(dve_filled.sem, 1)

                def linear_back(s):
                    wait_v("linear", s, T - 2)
                    four_transposes(("AT", 2 + s), lambda i: ATT2[s][:, i, :])

                def linear_out(s):
                    pe.wait_ge(exchange_read[s].sem, exchange_read[s].at(rnd, 1, 16))
                    project(("att_out", 2 + s), GROUPS_T[s], w["wd2"][:])

                def l2_ffn(s):
                    wait_xt(5, s)
                    b = open_v("l2_logits", s)
                    for i in range(T):
                        last = mm(b[:, i * NE:(i + 1) * NE], tile(XT[s], i), w["wg"][:])
                    last.then_inc(dve_filled.sem, 1)
                    base = SLOTS * 2 * NE + s * NE
                    up = lambda e: expert_up(base + e, s, w["w1e"][:, e, :])
                    up(0)
                    up(1)
                    for e in range(NE):
                        if e + 2 < NE:
                            up(e + 2)
                        if s == 0 and e == 1:
                            linear_back(1)
                        if s == 0 and e == 5:
                            linear_out(1)
                        if s == 1 and e == 0:
                            queries_norm(1, 0)
                        if s == 1 and e == 1:
                            queries(1, 0)
                        if s == 1 and e == 2:
                            kv_products(1, 1)
                        if s == 1 and e == 3:
                            queries_back(1, 0)
                        if s == 1 and e in (5, 6):
                            natural_scores(1, 0, e - 5)
                        if e == NE - 3:
                            pe.wait_ge(oh_ready.sem, oh_ready.at(rnd, s + 1))
                            b = open_a("OHT", s)
                            for i in range(T):
                                last = tr(b[0:NE, i * P:(i + 1) * P], GATE[s][:, i, :])
                            last.then_inc(act_filled.sem, 1)
                        expert_down(base + e, [w["w2e"][:, e, :]])
                    wait_a("OHT", s)
                    b = open_v("b2", s)
                    for i in range(T):
                        last = mm(tile(b, i), OHT[:, i * P:(i + 1) * P], w["b2e"][:])
                    last.then_inc(dve_filled.sem, 1)

                def l3_up(s):
                    norm_t(7, s)
                    wait_xt(7, s)
                    for k in range(NH):
                        expert_up(SLOTS * 3 * NE + s * NH + k, s, w["w13"][:, k * P:(k + 1) * P])

                def l3_down(s):
                    base = SLOTS * 3 * NE + s * NH
                    b = open_v("l3_out", s)
                    pe.wait_ge(relu_ready.sem, relu_ready.at(rnd, (s + 1) * NH))
                    for i in range(T):
                        for k in range(NH):
                            last = mm(tile(b, i), HT[:, (base + k) % NHT, i * P:(i + 1) * P], w["w23"][:, k, :], start=k == 0, stop=k == NH - 1)
                    last.then_inc(dve_filled.sem, 1)

                for s in range(SLOTS):
                    norm_t(0, s)
                l0_attention()
                wait_weights(pe, 1)
                wait_weights(pe, 2)
                pe.wait_ge(setup_pool, 2)
                kv_products(0, 0)
                for s in range(SLOTS):
                    norm_t(1, s)
                    kv2_products(s)
                    l0_ffn(s)
                    kv2_sum(s)
                    k_transposes(0, s)
                    if s == 0:
                        kv_products(0, 1)
                attention(0)
                l1_quantised(1)
                l1_up(1)
                q2(0)
                q2_back(0)
                l1_z(1)
                linear(0)
                l1_zt(1)
                linear_back(0)
                l1_down(1)
                q2(1)
                linear_out(0)
                k_transposes(1, 0)
                q2_back(1)
                norm_t(5, 0)
                linear(1)
                l2_ffn(0)
                norm_t(5, 1)
                l2_ffn(1)
                k_transposes(1, 1)
                attention(1)
                l3_up(1)
                l3_down(1)
                assert (n_a[0], n_v[0]) == (fills_a, fills_v), (n_a[0], n_v[0])

        @block.sync
        def _(sp):
            sp.dma_start(consts[:], t["consts"]).then_inc(consts_loaded, 16)

            def load_slot(rnd, s, ctx_part):
                b = rnd * SLOTS + s
                if not ctx_part:
                    sp.dma_start(XIN[s], t["x"].rearrange("b (t p) d -> b p t d", p=P)[b]).then_inc(x_loaded[s].sem, 16)
                    return
                sp.dma_start(CT[s][:], t["ctxT"][b]).then_inc(ctx_loaded[s].sem, 16)
                sp.dma_start(CN[s][:], t["ctx"][b, 0:P, :]).then_inc(ctx_loaded[s].sem, 16)
                sp.dma_start(CL[s][:], t["ctx"][b, P:C, :]).then_inc(ctx_loaded[s].sem, 16)
                sp.dma_start(CT4[s][:, :, 0:CR], t["ctxT"][b, :, P:C].rearrange("p (o c) -> p o c", o=1).broadcast_to([P, J, CR])).then_inc(ctx_loaded[s].sem, 16)
                sp.dma_start(EM[s][:, 0:1], t["em"][b, 0:P, :]).then_inc(ctx_loaded[s].sem, 16)
                sp.dma_start(EM[s][0:CR, 1:2], t["em"][b, P:C, :]).then_inc(ctx_loaded[s].sem, 16)
                sp.dma_start(MRAW[s][:], t["mask"][b]).then_inc(mask_loaded[s].sem, 16)
                sp.dma_start(MTRAW[s][:], t["maskT"][b, 0:P, :]).then_inc(mask_loaded[s].sem, 16)
                sp.dma_start(MLRAW[s][:], t["maskT"][b, P:C, :]).then_inc(mask_loaded[s].sem, 16)

            for dst, src in wsrc[0][:2]:
                sp.dma_start(dst, src).then_inc(loaded[0], 16)
            for s in range(SLOTS):
                sp.sem_inc(stored[s].sem, 16)
                load_slot(0, s, False)
            sp.wait_ge(setup_pool, 1)
            load_slot(0, 0, True)
            load_slot(0, 1, True)
            for k in (1, 2):
                for dst, src in wsrc[k]:
                    sp.dma_start(dst, src).then_inc(loaded[k], 16)

            def store(rnd, s):
                sp.wait_ge(x_done.sem, x_done.at(rnd, s + 1))
                sp.dma_start(out.rearrange("b (t p) d -> b p t d", p=P)[rnd * SLOTS + s], X[s][:]).then_inc(stored[s].sem, 16)

            def exchange_heads(rnd, s):
                sp.wait_ge(act_free.sem, drained(act_free, rnd, a_no["AT", 2 + s]))
                sp.dma_start(exchange[s].rearrange("m (e h) q -> (e h) m q", e=E8), HEADS_T[s].rearrange("p (m q) -> p m q", m=H)).then_inc(exchange_written.sem, 16)
                sp.wait_ge(exchange_written.sem, exchange_written.at(rnd, s + 1, 16))
                sp.dma_start(GROUPS_T[s], exchange[s].rearrange("m (e h) q -> (m e) (h q)", e=E8)).then_inc(exchange_read[s].sem, 16)

            with sp.Fori(0, ROUNDS - 1) as rnd:
                for s in range(SLOTS):
                    exchange_heads(rnd, s)
                for s in range(SLOTS):
                    sp.wait_ge(kn_ready.sem, kn_ready.at(rnd, 2 + s + 1))
                    sp.wait_ge(mask_ready.sem, mask_ready.at(rnd, s + 1))
                    load_slot(rnd + 1, s, True)
                sp.wait_ge(dve_free.sem, drained(dve_free, rnd, v_no["heads", 1, 1, G - 1]))
                for s in range(SLOTS):
                    load_slot(rnd + 1, s, False)
                for s in range(SLOTS):
                    store(rnd, s)
            for s in range(SLOTS):
                exchange_heads(ROUNDS - 1, s)
            for s in range(SLOTS):
                store(ROUNDS - 1, s)
            for s in range(SLOTS):
                sp.wait_ge(stored[s].sem, 16 * (ROUNDS + 1))

        @block.scalar
        def _(act):
            for dst, src in wsrc[0][2:]:
                act.dma_start(dst, src).then_inc(loaded[0], 16)
            act.sem_inc(act_free.sem, RING)
            act.wait_ge(consts_loaded, 16)
            act.wait_ge(setup_dve, 2)
            act.activation(th[:, 4, :], th[:, 2, :], ACT.Sin, scale=SIN_SCALE)
            act.activation(th[:, 5, :], th[:, 3, :], ACT.Sin, scale=SIN_SCALE).then_inc(setup_act, 1)

            with act.Fori(0, ROUNDS) as rnd:
                n_a = [0]

                def bank():
                    n_a[0] += 1
                    act.wait_ge(act_filled.sem, act_filled.at(rnd, n_a[0]))
                    return bank_a[(n_a[0] - 1) % RING]

                def free(ins):
                    ins.then_inc(act_free.sem, 1)

                def drain(dst, src):
                    b = bank()
                    act.activation(dst, src(b), ACT.Copy).then_inc(act_free.sem, 1)

                whole = lambda b: b[:]

                def norm_t(s):
                    drain(XT[s][:], whole)

                def l0_attention():
                    for s in range(SLOTS):
                        for i in range(T):
                            b = bank()
                            act.wait_ge(l0_shift.sem, l0_shift.at(rnd, s * T + i + 1))
                            ins = act.activation(PN[s][:, i, :], b[:, 0:C], ACT.Exp, bias=mx[:, s, i:i + 1], accum_out=sums[:, s, i:i + 1])
                            ins.then_inc(act_free.sem, 1)
                    for s in range(SLOTS):
                        drain(PNT[s], whole)
                        drain(PNL[s], lambda b: b[0:CR, :])

                def hidden(n, func, bias=None):
                    b = bank()
                    if bias is None:
                        ins = act.activation(HT[:, n % NHT, :], b[:], func)
                    else:
                        ins = act.activation(HT[:, n % NHT, :], b[:], func, bias=bias)
                    ins.then_inc(act_free.sem, 1)

                def l0_ffn(s):
                    b = bank()
                    ins = act.activation(GT[:], b[0:32, :], ACT.Gelu, bias=w["bg1"][:])
                    ins.then_inc(act_free.sem, 1)
                    for n in range(2 * NE):
                        hidden(s * 2 * NE + n, ACT.Gelu)
                        if s == 1 and n == 3:
                            norm_t(0)
                        if s == 1 and n == 7:
                            queries_back(0, 0)
                        if n == 3:
                            act.wait_ge(l0_shifted.sem, l0_shifted.at(rnd, s + 1))
                            act.activation(lg[:, 6], lg[:, 5], ACT.Exp).then_inc(l0_exps.sem, 1)

                def k_transposes(a, s):
                    if 2 * a + s > 0:
                        act.wait_ge(kb_ready.sem, kb_ready.at(rnd, 2 * a + s))
                        if s == 0:
                            act.wait_ge(kbn_ready.sem, kbn_ready.at(rnd, 2 * a + s))
                    drain(KTC[:], lambda b: b[:, 0:C])
                    b = bank()
                    act.activation(KS[:, 0:3, :], b[:, 0:3 * C].rearrange("p (g c) -> p g c", c=C), ACT.Copy).then_inc(act_free.sem, 1)
                    b = bank()
                    ins = act.activation(KS[:, 3, :], b[:, 0:C], ACT.Copy)
                    ins.then_inc(act_free.sem, 1)

                def k3_root(s):
                    act.wait_ge(kms_ready.sem, kms_ready.at(rnd, s + 1))
                    act.activation(msk[:], msk[:], ACT.Sqrt).then_inc(krt_ready.sem, 1)

                def q3_root(s):
                    act.wait_ge(qms_ready.sem, qms_ready.at(rnd, s + 1))
                    act.activation(ms[:], ms[:], ACT.Sqrt).then_inc(qrt_ready.sem, 1)

                def queries_back(a, s):
                    drain(QTC[s][:], whole)

                def split_queries(a, s, g):
                    drain(QS[((2 * a + s) * G + g) % 2][:], whole)

                def exps(a, s, g):
                    n = (2 * a + s) * G + g
                    for j in range(J + 1):
                        b = bank()
                        ins = act.activation(PT[:, (n % 2) * (J + 1) + j, :], b[:], ACT.Exp)
                        ins.then_inc(act_free.sem, 1)

                def values(a, s, g):
                    drain(UT[:, ((2 * a + s) * G + g) % 2, :], whole)

                def attention_back():
                    drain(AT[:], whole)

                def attention(a):
                    norm_t(1)
                    if a == 1:
                        q3_root(1)
                    queries_back(a, 1)
                    split_queries(a, 0, 0)
                    for g in range(G + 2):
                        if g + 1 < G:
                            split_queries(a, 0, g + 1)
                        if g < G:
                            exps(a, 0, g)
                        if 1 <= g <= G:
                            values(a, 0, g - 1)
                    split_queries(a, 1, 0)
                    for g in range(G + 2):
                        if g + 1 < G:
                            split_queries(a, 1, g + 1)
                        if g == 0:
                            attention_back()
                        if g == 2 and a == 0:
                            k3_root(0)
                            l1_quantised()
                        if g == 2 and a == 1:
                            norm_t(0)
                            l3_hidden(0)
                        if g < G:
                            exps(a, 1, g)
                        if g == 3 and a == 0:
                            l1_taps(0)
                        if g == 3 and a == 1:
                            l3_sines(0)
                        if 1 <= g <= G:
                            values(a, 1, g - 1)
                        if g == 3 and a == 1:
                            l3_relus(0)
                        if g == 3 and a == 0:
                            l1_silus(0)
                    if a == 0:
                        l1_zt()
                    attention_back()

                def l1_quantised():
                    drain(XQT[:], lambda b: b[:].bitcast(BF16)[:, 0:S])
                    drain(SB_[:], whole)

                def l1_taps(s):
                    for k in range(NH):
                        act.wait_ge(dve_free.sem, drained(dve_free, rnd, v_no["l1_hidden", s, k]))
                        act.activation(CV[:, k, :], HP[:, k, 1:S + 1], ACT.Identity, scale=w["cw"][:, k, 1:2], bias=w["cb"][:, k:k + 1])
                        if k >= 2:
                            act.wait_ge(left_ready.sem, left_ready.at(rnd, s * NH + k - 1))
                        act.activation(LEFT[k % 2], HP[:, k, 0:S], ACT.Copy, scale=w["cw"][:, k, 0:1]).then_inc(tap_ready.sem, 1)

                def l1_silus(s):
                    for k in range(NH):
                        act.wait_ge(conv_ready.sem, conv_ready.at(rnd, s * NH + k + 1))
                        act.activation(CV[:, k, :], CV[:, k, :], ACT.Silu).then_inc(z_ready.sem, 1)

                def l1_zt():
                    for i in range(T):
                        drain(ZT[:, :, i * P:(i + 1) * P], lambda b: b[:].bitcast(BF16)[:, 0:S].rearrange("p (k c) -> p k c", k=NH))

                def q2_back(s):
                    drain(Q2T[s], whole)

                def linear_back(s):
                    b = bank()
                    act.activation(HEADS_T[s].rearrange("p (m q) -> p q m", m=H), b[:].rearrange("p (q m) -> p q m", m=H), ACT.Copy).then_inc(act_free.sem, 1)

                def l2_ffn(s):
                    for n in range(NE + 1):
                        if n == NE:
                            drain(OHT[:], lambda b: b[0:NE, :])
                        if n == 4 and s == 0:
                            linear_back(1)
                        if n == 3 and s == 1:
                            norm_t(0)
                        if n == 4 and s == 1:
                            q3_root(0)
                            k3_root(1)
                        if n == 6 and s == 1:
                            queries_back(1, 0)
                        if n < NE:
                            hidden(SLOTS * 2 * NE + s * NE + n, ACT.Gelu, w["b1e"][:, n:n + 1])

                def l3_hidden(s):
                    for k in range(NH):
                        b = bank()
                        act.wait_ge(turn_ready.sem, turn_ready.at(rnd, s * NH + k + 1))
                        ins = act.activation(CV[:, k, :], b[:], ACT.Identity, bias=w["b13"][:, k:k + 1])
                        ins.then_inc(act_free.sem, 1)

                def l3_relus(s):
                    for k in range(NH):
                        act.wait_ge(turned_ready.sem, turned_ready.at(rnd, s * NH + k + 1))
                        act.activation(HT[:, (SLOTS * 3 * NE + s * NH + k) % NHT, :], CV[:, k, :], ACT.Relu).then_inc(relu_ready.sem, 1)

                def l3_sines(s):
                    for k in range(NH):
                        act.wait_ge(phase_ready.sem, phase_ready.at(rnd, s * NH + k + 1))
                        act.activation(HP[:, k, 1:S + 1], HP[:, k, 1:S + 1], ACT.Sin, scale=SIN_SCALE).then_inc(sin_ready.sem, 1)

                for s in range(SLOTS):
                    norm_t(s)
                l0_attention()
                wait_weights(act, 1)
                wait_weights(act, 2)
                for s in range(SLOTS):
                    norm_t(s)
                    l0_ffn(s)
                    k_transposes(0, s)
                attention(0)
                l1_quantised()
                norm_t(0)
                l1_taps(1)
                l1_silus(1)
                q2_back(0)
                l1_zt()
                linear_back(0)
                norm_t(1)
                k_transposes(1, 0)
                q2_back(1)
                norm_t(0)
                l2_ffn(0)
                norm_t(1)
                l2_ffn(1)
                k_transposes(1, 1)
                attention(1)
                norm_t(1)
                l3_hidden(1)
                l3_sines(1)
                l3_relus(1)

        @block.gpsimd
        def _(pool):
            steps = [0]

            def step(ins):
                ins.then_inc(pool_step, 1)
                steps[0] += 1
                pool.wait_ge(pool_step, steps[0])

            pool.memset(ones_row[:], 1.0)
            pool.memset(mhalf[:], -0.5)
            pool.memset(mv[:], 1.0)
            for s in range(SLOTS):
                last = pool.memset(CT4[s][:], 0.0)
            last.then_inc(setup_pool, 1)
            for s in range(SLOTS):
                for a in (KBL[s], VA[s], VL[s], QN[s]):
                    last = pool.memset(a[:].bitcast(F32) if a is KBL[s] else a[:], 0.0)
            for a in (KN, KNL, K2, V2, HP, msk, KH):
                last = pool.memset(a[:].bitcast(F32) if a is KH else a[:], 0.0)
            step(last)
            pool.wait_ge(consts_loaded, 16)
            for s in range(SLOTS):
                pool.tensor_copy(VL[s][:, :, E8:E8 + 1], const("jrem").rearrange("p (h o) -> p h o", o=1))
                pool.memset(VA[s][:, :, E8:E8 + 1], 1.0)
            pool.memset(KN[:, :, 3 * E8:3 * E8 + 1], 1.0)
            pool.memset(KNL[:, :, 3 * E8:3 * E8 + 1], 1.0)
            pool.memset(V2[:, :, D:D + 1], 1.0).then_inc(setup_pool, 1)

            with pool.Fori(0, ROUNDS) as rnd:
                n_ln = [0]

                def drained_a(*holds):
                    pool.wait_ge(act_free.sem, drained(act_free, rnd, a_no[holds]))

                def power(times=1):
                    for _ in range(times):
                        n = n_ln[0]
                        n_ln[0] += 1
                        pool.wait_ge(ln_var.sem, ln_var.at(rnd, n + 1))
                        pool.tensor_tensor(rstd[:, n % 2], var[:, n % 2], mhalf[:], ALU.pow).then_inc(ln_rstd.sem, 1)

                def masks():
                    for s in range(SLOTS):
                        pool.wait_ge(mask_loaded[s].sem, mask_loaded[s].at(rnd, mask_loaded[s].n, 16))
                        pool.sem_inc(pool_waited, 1)
                        pool.tensor_scalar(MN[s][:], MRAW[s][:].bitcast(U8).rearrange("p (t c) -> p t c", t=T), BIG, -BIG, ALU.mult, ALU.add)
                        pool.tensor_scalar(MT[s][:], MTRAW[s][:].bitcast(U8), BIG, -BIG, ALU.mult, ALU.add)
                        pool.tensor_scalar(ML[s][:], MLRAW[s][:].bitcast(U8), BIG, -BIG, ALU.mult, ALU.add).then_inc(mask_ready.sem, 1)

                def keys_natural(a, s):
                    drained_a("KTC", a, s)
                    if s > 0:
                        pool.wait_ge(dve_free.sem, drained(dve_free, rnd, v_no["natural", a, s - 1, T - 1, NCH - 1]))
                    pool.tensor_tensor(KBN[:], KTC[:].rearrange("p (o c) -> p o c", o=1).broadcast_to([P, H, C]),
                                       const("ind16").rearrange("p (h o) -> p h o", o=1).broadcast_to([P, H, C]),
                                       ALU.mult).then_inc(kbn_ready.sem, 1)

                def keys_grouped(a, s):
                    drained_a("KS", a, s, 3)
                    i4 = const("ind4")
                    for g in range(G):
                        o1 = i4.rearrange("p (j o) -> p j o", o=1)
                        pool.tensor_tensor(KBM[s][:, g], KS[:, g, 0:P].rearrange("p (o c) -> p o c", o=1).broadcast_to([P, J, P]),
                                           o1.broadcast_to([P, J, P]), ALU.mult)
                        last = pool.tensor_tensor(KBL[s][:, g, :, 0:CR], KS[:, g, P:C].rearrange("p (o c) -> p o c", o=1).broadcast_to([P, J, CR]),
                                                  o1.broadcast_to([P, J, CR]), ALU.mult)
                    last.then_inc(kb_ready.sem, 1)

                def l1_left_taps(s, ks):
                    for k in ks:
                        pool.wait_ge(tap_ready.sem, tap_ready.at(rnd, s * NH + k + 1))
                        pool.tensor_tensor(CV[:, k, :], CV[:, k, :], LEFT[k % 2], ALU.add).then_inc(left_ready.sem, 1)

                def high_halves(a, s):
                    pool.wait_ge(qh_ready.sem, qh_ready.at(rnd, 2 * a + s + 1))
                    pool.sem_inc(pool_waited, 1)
                    q = QH[:].bitcast(F32).rearrange("p t (h e) -> p (t h) e", h=H)
                    n = QN[s][:].rearrange("p t h w -> p (t h) w")
                    for k in range(2):
                        last = pool.tensor_copy(n[:, :, k * E8:(k + 1) * E8], q)
                    last.then_inc(qhh_ready.sem, 1)

                def add_bias(n, s, bias, layer):
                    pool.wait_ge(xn_ready.sem, xn_ready.at(rnd, 2 * layer + s + 1))
                    pool.tensor_tensor(X[s][:], X[s][:], bias[:].rearrange("p (o d) -> p o d", o=1).broadcast_to([P, T, D]),
                                       ALU.add).then_inc(x_added.sem, 1)

                power(4)
                power()
                masks()
                wait_weights(pool, 2)
                power()
                add_bias(0, 0, w["bp1"], 2)
                power()
                keys_natural(0, 0)
                keys_grouped(0, 0)
                high_halves(0, 0)
                power()
                add_bias(0, 1, w["bp1"], 2)
                keys_grouped(0, 1)
                keys_natural(0, 1)
                high_halves(0, 1)
                power()
                l1_left_taps(0, range(NH))
                power()
                power()
                l1_left_taps(1, (0, 1))
                power()
                l1_left_taps(1, (2, 3))
                power(2)
                power(2)
                keys_natural(1, 0)
                keys_grouped(1, 0)
                power(2)
                power()
                high_halves(1, 0)
                power()
                keys_grouped(1, 1)
                keys_natural(1, 1)
                high_halves(1, 1)
                for s in range(SLOTS):
                    power()
                    add_bias(1, s, w["b23"], 7)
                    for m in range(s * NH, (s + 1) * NH):
                        pool.wait_ge(whole_ready.sem, whole_ready.at(rnd, m + 1))
                        u, whole = TURNS[m % 2]
                        pool.tensor_tensor(HP[:, m % NH, 1:S + 1], u, whole, ALU.subtract).then_inc(phase_ready.sem, 1)

        @block.vector
        def _(dve):
            steps = [0]

            def note(ins):
                ins.then_inc(dve_step, 1)
                steps[0] += 1

            def sync():
                dve.wait_ge(dve_step, steps[0])

            def link(ins):
                note(ins)
                sync()

            ts, tt, stt, red, cp = dve.tensor_scalar, dve.tensor_tensor, dve.scalar_tensor_tensor, dve.tensor_reduce, dve.tensor_copy
            dve.wait_ge(consts_loaded, 16)
            cp(ident_bf[:], ident)
            cp(rsel_bf[:], const("rsel"))
            wait_weights(dve, 0)
            red(wsum[:, 0:1], w["w1b"], AX, ALU.add, apply_absolute_value=True)
            red(wsum[:, 1:2], w["w2b"].rearrange("p k d -> p (k d)"), AX, ALU.add, apply_absolute_value=True).then_inc(setup_dve, 1)
            link(ts(th[:, 0, :], w["ph"][:], 1 / TWO_PI, MAGIC, ALU.mult, ALU.add))
            link(ts(th[:, 0, :], th[:, 0, :], -MAGIC, None, ALU.add))
            link(stt(th[:, 1, :], th[:, 0, :], -PI_A, w["ph"][:], ALU.mult, ALU.add))
            link(stt(th[:, 1, :], th[:, 0, :], -PI_B, th[:, 1, :], ALU.mult, ALU.add))
            link(stt(th[:, 1, :], th[:, 0, :], -PI_C, th[:, 1, :], ALU.mult, ALU.add))
            link(ts(th[:, 1, :], th[:, 1, :], 1 / TWO_PI, None, ALU.mult))
            for k, ahead in ((2, 0.0), (3, 0.25)):
                link(ts(th[:, 6, :], th[:, 1, :], ahead, MAGIC, ALU.add, ALU.add))
                link(ts(th[:, 6, :], th[:, 6, :], -MAGIC, None, ALU.add))
                link(stt(th[:, k, :], th[:, 1, :], ahead, th[:, 6, :], ALU.add, ALU.subtract))
            dve.sem_inc(setup_dve, 1)
            dve.wait_ge(setup_pe, 1)
            link(ts(wsum[:, 2:4], bank_v[0][:, 0:2], 1 / (D * FF), 1e-5, ALU.mult, ALU.max))
            link(dve.reciprocal(wsum[:, 4:6], wsum[:, 2:4]))
            for src, dst, k in ((w["w1b"], w1q[:], 4), (w["w2b"], w2q[:], 5)):
                link(ts(src, src, wsum[:, k:k + 1], MAGIC, ALU.mult, ALU.add))
                link(ts(src, src, -MAGIC, 1.0, ALU.add, ALU.min))
                last = ts(dst, src, -1.0, None, ALU.max)
            last.then_inc(setup_dve, 1)
            note(ts(wsum[:, 6:8], wsum[:, 2:4], 1 / 127.0, None, ALU.mult))
            dve.wait_ge(setup_act, 1)
            note(tt(th[:, 6, :], th[:, 5, :], w["wr"][:], ALU.mult))
            link(tt(th[:, 7, :], th[:, 4, :], w["wi"][:], ALU.mult))
            link(tt(th[:, 6, :], th[:, 6, :], th[:, 7, :], ALU.add))
            note(stt(th[:, 8, :], th[:, 6, :], 0.1, w["wi"][:], ALU.mult, ALU.mult))
            note(stt(th[:, 9, :], w["b13"][:], 0.1 / TWO_PI, th[:, 2, :], ALU.mult, ALU.add))
            link(stt(gk[:], w["qg"][:], RSQ8, w["kg"][:], ALU.mult, ALU.mult))
            dve.wait_ge(setup_pool, 1)
            dve.sem_inc(dve_free.sem, RING)

            with dve.Fori(0, ROUNDS) as rnd:
                dve.wait_ge(dve_step, 1)
                dve.sem_clear(dve_step)
                steps[0] = 0
                n_v, n_ln = [0], [0]

                def bank(*holds):
                    assert v_no[holds] == n_v[0], (holds, v_no[holds], n_v[0])
                    n_v[0] += 1
                    dve.wait_ge(dve_filled.sem, dve_filled.at(rnd, n_v[0]))
                    return bank_v[(n_v[0] - 1) % RING]

                def free(ins):
                    ins.then_inc(dve_free.sem, 1)

                def freed():
                    dve.wait_ge(dve_free.sem, drained(dve_free, rnd, n_v[0] - 1))

                def drained_a(*holds):
                    dve.wait_ge(act_free.sem, drained(act_free, rnd, a_no[holds]))

                tile = lambda a, i: a[:, i * P:(i + 1) * P]
                quarters = lambda b: b[:].rearrange("p (t d) -> p t d", t=T)
                by_head = lambda a: a.rearrange("p (h e) -> p h e", e=E8)

                def over_d(v, n):
                    return v.rearrange("p (a o) -> p a o", o=1).broadcast_to([P, v.shape[1], n])

                def norm_start(srcs, eps, rows=(P,) * T):
                    n = n_ln[0]
                    n_ln[0] += 1
                    for i in range(T):
                        last = dve.bn_stats(stats[0:rows[i], i, :], srcs(i))
                    link(last)
                    for i in range(T):
                        last = dve.bn_aggr(mv[0:rows[i], n % 2, i, :], stats[0:rows[i], i, :])
                    link(last)
                    ts(var[:, n % 2], mv[:, n % 2, :, 1], eps, None, ALU.add).then_inc(ln_var.sem, 1)
                    return n

                def mean(n, i, k=P):
                    return mv[0:k, n % 2, i, 0:1]

                def wait_rstd(n):
                    dve.wait_ge(ln_rstd.sem, ln_rstd.at(rnd, n + 1))

                def ln_start(s, x=X):
                    return norm_start(lambda i: x[s][:, i, :], 1e-5)

                def ln_end(n, s, x=X):
                    wait_rstd(n)
                    for i in range(T):
                        last = ts(XN[s][:, i, :], x[s][:, i, :], mean(n, i), rstd[:, n % 2, i:i + 1], ALU.subtract, ALU.mult)
                    last.then_inc(xn_ready.sem, 1)

                def layer_norm(s):
                    ln_end(ln_start(s), s)

                def centre(n, srcs, dst, rows=(P,) * T):
                    for i, k in enumerate(rows):
                        last = stt(dst(i), srcs(i), mean(n, i, k), w["lng"][0:k], ALU.subtract, ALU.mult)
                    return last

                def scale(n, dst, rows=(P,) * T):
                    wait_rstd(n)
                    for i, k in enumerate(rows):
                        last = stt(dst(i), dst(i), rstd[0:k, n % 2, i:i + 1], w["lnb"][0:k], ALU.mult, ALU.add)
                    link(last)

                def add_to_x(s, b):
                    free(tt(X[s][:], X[s][:], quarters(b), ALU.add))
                    freed()

                def l0_attention():
                    for s in range(SLOTS):
                        for i in range(T):
                            n = a_no["l0_scores", s, i]
                            dve.wait_ge(act_filled.sem, act_filled.at(rnd, n + 1))
                            red(mx[:, s, i:i + 1], bank_a[n % RING][:, 0:C], AX, ALU.max, negate=True).then_inc(l0_shift.sem, 1)
                    ns = []
                    for s in range(SLOTS):
                        drained_a("l0_scores", s, T - 1)
                        link(dve.reciprocal(rsum[:, s], sums[:, s]))
                        b = bank("l0_out", s)
                        dve.wait_ge(stored[s].sem, stored[s].at(rnd, 1, 16))
                        for i in range(T):
                            last = stt(X[s][:, i, :], tile(b, i), rsum[:, s, i:i + 1], XIN[s][:, i, :], ALU.mult, ALU.add)
                        free(last)
                        freed()
                        ns.append(ln_start(s))
                    for s in range(SLOTS):
                        ln_end(ns[s], s)

                def first_best(x, k):
                    link(red(gm[:, k, :], lg[:, x], AX, ALU.max))
                    link(tt(lg[:, k], lg[:, x], over_d(gm[:, k, :], NE), ALU.is_equal))
                    link(tt(lg[:, k], lg[:, k], const("desc").rearrange("p (o e) -> p o e", o=1).broadcast_to([P, T, NE]), ALU.mult))
                    link(red(gm[:, 7, :], lg[:, k], AX, ALU.max))
                    link(tt(lg[:, k], lg[:, k], over_d(gm[:, 7, :], NE), ALU.is_equal))

                def l0_gates(s):
                    b = bank("l0_logits", s)
                    free(cp(lg[:, 0].rearrange("p t e -> p (t e)"), b[:, 0:T * NE]))
                    freed()
                    link(red(gm[:, 0, :], lg[:, 0], AX, ALU.max))
                    tt(lg[:, 5], lg[:, 0], over_d(gm[:, 0, :], NE), ALU.subtract).then_inc(l0_shifted.sem, 1)
                    first_best(0, 1)
                    link(stt(lg[:, 2], lg[:, 1], -3.0e38, lg[:, 0], ALU.mult, ALU.add))
                    first_best(2, 3)
                    link(tt(lg[:, 3], lg[:, 3], lg[:, 1], ALU.add))
                    dve.wait_ge(l0_exps.sem, l0_exps.at(rnd, s + 1))
                    link(red(gm[:, 4, :], lg[:, 6], AX, ALU.add))
                    note(dve.reciprocal(gm[:, 5, :], gm[:, 4, :]))
                    link(tt(lg[:, 3], lg[:, 3], lg[:, 6], ALU.mult))
                    link(tt(GATE[s][:], lg[:, 3], over_d(gm[:, 5, :], NE), ALU.mult))

                def expert_sums(s, base, per, beside=None):
                    for e in range(NE):
                        if beside is not None:
                            beside(e)
                        b = bank("down", base + per * e)
                        for i in range(T):
                            last = stt(X[s][:, i, :], tile(b, i), GATE[s][:, i, e:e + 1], X[s][:, i, :], ALU.mult, ALU.add)
                        free(last)
                        freed()

                def keys(a, s):
                    b = bank("kv", a, s)
                    kb = b[:].rearrange("p (x d) -> p x d", d=D)
                    if a == 0:
                        note(ts(KH[:, 0, :], kb[:, 0], RSQ8, None, ALU.mult))
                        ts(KH[0:CR, 1, :], kb[0:CR, 2], RSQ8, None, ALU.mult).then_inc(kh_ready.sem, 1)
                        dve.wait_ge(kh_ready.sem, kh_ready.at(rnd, s + 1))
                        hi = KH[:].bitcast(F32)
                        stt(KN[:, :, E8:2 * E8], by_head(kb[:, 0]), RSQ8, by_head(hi[:, 0, :]), ALU.mult, ALU.subtract)
                        stt(KNL[:, :, E8:2 * E8], by_head(kb[0:CR, 2]), RSQ8, by_head(hi[0:CR, 1, :]), ALU.mult, ALU.subtract)
                    else:
                        k32 = SQ[:, 0:2, :]
                        dve.wait_ge(rs_ready.sem, rs_ready.at(rnd, s + 1))
                        note(cp(k32[:, 0, :], kb[:, 0]))
                        link(cp(k32[0:CR, 1, :], kb[0:CR, 2]))
                        note(tt(SQ[:, 2, :], k32[:, 0, :], k32[:, 0, :], ALU.mult))
                        link(tt(SQ[0:CR, 3, :], k32[0:CR, 1, :], k32[0:CR, 1, :], ALU.mult))
                        note(red(msk[:, 0:H], by_head(SQ[:, 2, :]), AX, ALU.add))
                        link(red(msk[0:CR, H:2 * H], by_head(SQ[0:CR, 3, :]), AX, ALU.add))
                        ts(msk[:], msk[:], 1 / E8, 1e-6, ALU.mult, ALU.add).then_inc(kms_ready.sem, 1)
                        dve.wait_ge(krt_ready.sem, krt_ready.at(rnd, s + 1))
                        link(dve.reciprocal(msk[:], msk[:]))
                        for i, k in ((0, P), (1, CR)):
                            wide = msk[0:k, i * H:(i + 1) * H].rearrange("p (h o) -> p h o", o=1).broadcast_to([k, H, E8])
                            last = tt(by_head(k32[0:k, i, :]), by_head(k32[0:k, i, :]), wide, ALU.mult)
                        link(last)
                        for i, k in ((0, P), (1, CR)):
                            wide = gk[0:k].rearrange("p (o e) -> p o e", o=1).broadcast_to([k, H, E8])
                            last = tt(by_head(k32[0:k, i, :]), by_head(k32[0:k, i, :]), wide, ALU.mult)
                        link(last)
                        note(cp(KH[:, 0, :], k32[:, 0, :]))
                        cp(KH[0:CR, 1, :], k32[0:CR, 1, :]).then_inc(kh_ready.sem, 1)
                        dve.wait_ge(kh_ready.sem, kh_ready.at(rnd, 2 + s + 1))
                        hi = KH[:].bitcast(F32)
                        tt(KN[:, :, E8:2 * E8], by_head(k32[:, 0, :]), by_head(hi[:, 0, :]), ALU.subtract)
                        tt(KNL[:, :, E8:2 * E8], by_head(k32[0:CR, 1, :]), by_head(hi[0:CR, 1, :]), ALU.subtract)
                    for k in (0, 2):
                        cp(KN[:, :, k * E8:(k + 1) * E8], by_head(hi[:, 0, :]))
                        last = cp(KNL[:, :, k * E8:(k + 1) * E8], by_head(hi[0:CR, 1, :]))
                    last.then_inc(kn_ready.sem, 1)
                    cp(VA[s][:, :, 0:E8], by_head(kb[:, 1]))
                    free(tt(VL[s][:, :, 0:E8], by_head(kb[:, 3]),
                            const("jind").rearrange("p (h o) -> p h o", o=1).broadcast_to([P, H, E8]), ALU.mult))

                def queries(a, s):
                    b = bank("q", a, s)
                    n = 2 * a + s + 1
                    lo = QN[s][:].rearrange("p t h w -> p (t h) w")[:, :, 2 * E8:3 * E8]
                    heads = lambda v: v.rearrange("p t (h e) -> p (t h) e", e=E8)
                    if n > 1:
                        dve.wait_ge(qhh_ready.sem, qhh_ready.at(rnd, n - 1))
                    if a == 0:
                        cp(QH[:], quarters(b)).then_inc(qh_ready.sem, 1)
                        dve.wait_ge(qh_ready.sem, qh_ready.at(rnd, n))
                        free(tt(lo, by_head(b[:]), heads(QH[:].bitcast(F32)), ALU.subtract))
                    else:
                        free(cp(Q32[:], quarters(b)))
                        freed()
                        link(tt(SQ[:], Q32[:], Q32[:], ALU.mult))
                        link(red(ms[:], heads(SQ[:]), AX, ALU.add))
                        ts(ms[:], ms[:], 1 / E8, 1e-6, ALU.mult, ALU.add).then_inc(qms_ready.sem, 1)
                        dve.wait_ge(qrt_ready.sem, qrt_ready.at(rnd, s + 1))
                        link(dve.reciprocal(ms[:], ms[:]))
                        link(tt(heads(Q32[:]), heads(Q32[:]), over_d(ms[:], E8), ALU.mult))
                        cp(QH[:], Q32[:]).then_inc(qh_ready.sem, 1)
                        dve.wait_ge(qh_ready.sem, qh_ready.at(rnd, n))
                        note(tt(lo, heads(Q32[:]), heads(QH[:].bitcast(F32)), ALU.subtract))

                def maxima(a, s, i):
                    for c in range(NCH):
                        n = min(CH, H - c * CH)
                        b = bank("natural", a, s, i, c)
                        last = red(QN[s][:, i, c * CH:c * CH + n, 3 * E8], b[:, 0:n * C].rearrange("p (h c) -> p h c", c=C), AX, ALU.max, negate=True)
                        free(last)

                def heads_back(a, s, g):
                    b = bank("heads", a, s, g)
                    if g > 0:
                        dve.wait_ge(dve_free.sem, drained(dve_free, rnd, v_no["heads", a, s, g - 1]))
                    v = b[:].rearrange("p (t j w) -> p t j w", t=T, j=J)
                    link(dve.reciprocal(r16[:], v[:, :, :, E8]))
                    o = ATT[:].rearrange("p t (g j e) -> p t g j e", g=G, j=J)[:, :, g]
                    free(tt(o, v[:, :, :, 0:E8], r16[:].rearrange("p t (j o) -> p t j o", o=1).broadcast_to([P, T, J, E8]), ALU.mult))

                def attention_added(a, s):
                    if a == 0:
                        dve.wait_ge(x_added.sem, x_added.at(rnd, s + 1))
                    add_to_x(s, bank("att_out", 4 * a + s))
                    layer_norm(s)

                def attention(a):
                    maxima(a, 0, 2)
                    queries(a, 1)
                    maxima(a, 0, 3)
                    for g in range(G + 2):
                        if 1 <= g <= T:
                            maxima(a, 1, g - 1)
                        if g >= 2:
                            heads_back(a, 0, g - 2)
                    attention_added(a, 0)
                    if a == 0:
                        quantise_x(0)
                        keys(1, 0)
                    else:
                        l3_phases(0)
                    for g in range(G):
                        heads_back(a, 1, g)
                        if g == 0 and a == 0:
                            l1_hidden(0)
                        if g == 1 and a == 0:
                            l1_conv(0)
                        if g == 1 and a == 1:
                            l3_relus(0)
                        if g == 2 and a == 0:
                            l1_z(0)
                        if g == 2 and a == 1:
                            l3_added(0)
                    if a == 0:
                        l1_added(0)
                    attention_added(a, 1)
                    if a == 0:
                        quantise_x(1)
                        layer_norm(0)
                    else:
                        l3_phases(1)

                def quantise_x(s):
                    dve.wait_ge(xn_ready.sem, xn_ready.at(rnd, 2 * 3 + s + 1))
                    link(red(amax[:, 0, :], XN[s][:], AX, ALU.max, apply_absolute_value=True))
                    link(ts(amax[:, 0, :], amax[:, 0, :], 1e-5, None, ALU.max))
                    link(dve.reciprocal(amax[:, 1, :], amax[:, 0, :]))
                    link(ts(amax[:, 1, :], amax[:, 1, :], 127.0, None, ALU.mult))
                    for i in range(T):
                        last = ts(SQ[:, i, :], XN[s][:, i, :], amax[:, 1, i:i + 1], MAGIC, ALU.mult, ALU.add)
                    link(last)
                    ts(XQ[s], SQ[:], -MAGIC, 127.0, ALU.add, ALU.min).then_inc(xq_ready.sem, 1)
                    ts(amax[:, 3 + s, :], amax[:, 0, :], wsum[:, 6:7], None, ALU.mult).then_inc(rs_ready.sem, 1)

                def l1_hidden(s):
                    drained_a("SBC", s)
                    for k in range(NH):
                        b = bank("l1_hidden", s, k)
                        free(tt(HP[:, k, 1:S + 1], b[:], SB_[:], ALU.mult))

                def l1_conv(s):
                    for k in range(NH):
                        dve.wait_ge(left_ready.sem, left_ready.at(rnd, s * NH + k + 1))
                        stt(CV[:, k, :], HP[:, k, 2:S + 2], w["cw"][:, k, 2:3], CV[:, k, :], ALU.mult, ALU.add).then_inc(conv_ready.sem, 1)

                def l1_z(s):
                    zb = []
                    for i in range(T):
                        b = bank("z", s, i)
                        zb.append(b)
                        last = red(amax[:, 0, i:i + 1], b[:], AX, ALU.max, apply_absolute_value=True)
                    link(last)
                    link(ts(amax[:, 0, :], amax[:, 0, :], 1e-5, None, ALU.max))
                    link(dve.reciprocal(amax[:, 1, :], amax[:, 0, :]))
                    note(ts(amax[:, 2, :], amax[:, 0, :], wsum[:, 7:8], None, ALU.mult))
                    link(ts(amax[:, 1, :], amax[:, 1, :], 127.0, None, ALU.mult))
                    for i in range(T):
                        z = ROUNDED[i % 2]
                        if i >= 2:
                            dve.wait_ge(zq_ready.sem, zq_ready.at(rnd, s * T + i - 1))
                        free(ts(z, zb[i][:], amax[:, 1, i:i + 1], MAGIC, ALU.mult, ALU.add))
                        dve.wait_ge(dve_free.sem, drained(dve_free, rnd, v_no["z", s, i]))
                        ts(ZQ[:, i, :], z, -MAGIC, 127.0, ALU.add, ALU.min).then_inc(zq_ready.sem, 1)

                def l1_added(s):
                    b = bank("l1_out", s)
                    for i in range(T):
                        last = stt(X[s][:, i, :], tile(b, i), amax[:, 2, i:i + 1], X[s][:, i, :], ALU.mult, ALU.add)
                    free(last)
                    freed()

                def keys2(s):
                    b = bank("kv2", s)
                    rows = (P, P, CR, CR)
                    src = lambda i: b[0:rows[i], i * D:(i + 1) * D]
                    dst = lambda i: K2[0:rows[i], i, :]
                    n = norm_start(src, 1e-6, rows)
                    free(centre(n, src, dst, rows))
                    freed()
                    scale(n, dst, rows)
                    for i, k in ((0, P), (2, CR)):
                        last = ts(K2[0:k, i, :], K2[0:k, i, :], 0.0, 1e-6, ALU.max, ALU.add)
                    link(last)
                    for i, k, m in ((0, P, 0), (2, CR, 1)):
                        ts(K2[0:k, i, :], K2[0:k, i, :], EM[s][0:k, m:m + 1], None, ALU.mult)
                        last = ts(V2[0:k, m, 0:D], K2[0:k, i + 1, :], EM[s][0:k, m:m + 1], None, ALU.mult)
                    last.then_inc(kv2_ready.sem, 1)

                def keys2_sum(s):
                    b = bank("kv2_sum", s)
                    tt(KVB[s][:, 0:D], b[:, 0:D], const("blk"), ALU.mult)
                    free(tt(KVB[s][:, D:D + H], b[:, D:D + 1].broadcast_to([P, H]), const("ind16"), ALU.mult))

                def q2_start(s):
                    b = bank("q2", s)
                    src = lambda i: tile(b, i)
                    n = norm_start(src, 1e-6)
                    free(centre(n, src, lambda i: Q2[s][:, i, :]))
                    freed()
                    return n

                def q2_end(n, s):
                    scale(n, lambda i: Q2[s][:, i, :])
                    ts(Q2[s], Q2[s], 0.0, 1e-6, ALU.max, ALU.add).then_inc(q2_ready.sem, 1)

                def linear(s):
                    for i in range(0, T, 2):
                        b = bank("linear", s, i)
                        if i > 0:
                            dve.wait_ge(dve_free.sem, drained(dve_free, rnd, n_v[0] - 2))
                        v = b[:, 0:2 * (D + H)].rearrange("p (t x) -> p t x", t=2)
                        link(ts(den[:], v[:, :, D:D + H], 1e-6, None, ALU.add))
                        link(dve.reciprocal(den[:], den[:]))
                        o = ATT2[s][:, i:i + 2, :].rearrange("p t (e h) -> p t h e", h=H)
                        free(tt(o, v[:, :, 0:D].rearrange("p t (h e) -> p t h e", h=H),
                                den[:].rearrange("p t (h o) -> p t h o", o=1).broadcast_to([P, 2, H, E8]), ALU.mult))

                def linear_out_start(s):
                    b = bank("att_out", 2 + s)
                    free(tt(Q2[s], quarters(b), w["bd2"][:].rearrange("p (o d) -> p o d", o=1).broadcast_to([P, T, D]), ALU.add))
                    freed()
                    q = lambda i: Q2[s][:, i, :]
                    n = norm_start(q, 1e-6)
                    link(centre(n, q, q))
                    return n

                def linear_out_end(n, s):
                    scale(n, lambda i: Q2[s][:, i, :])
                    link(tt(X[s][:], X[s][:], Q2[s], ALU.add))
                    layer_norm(s)

                def l2_ffn(s, beside=None):
                    b = bank("l2_logits", s)
                    free(tt(lg[:, 0], b[:, 0:T * NE].rearrange("p (t e) -> p t e", e=NE),
                            w["bg"][:].rearrange("p (o e) -> p o e", o=1).broadcast_to([P, T, NE]), ALU.add))
                    freed()
                    first_best(0, 1)
                    cp(GATE[s][:], lg[:, 1]).then_inc(oh_ready.sem, 1)
                    dve.wait_ge(oh_ready.sem, oh_ready.at(rnd, s + 1))
                    expert_sums(s, SLOTS * 2 * NE + s * NE, 1, beside)
                    add_to_x(s, bank("b2", s))

                def l3_phases(s):
                    for k in range(NH):
                        m = s * NH + k
                        u, r_ = TURNS[m % 2]
                        if m >= 2:
                            dve.wait_ge(phase_ready.sem, phase_ready.at(rnd, m - 1))
                        n = a_no["hidden", SLOTS * 3 * NE + m]
                        dve.wait_ge(act_filled.sem, act_filled.at(rnd, n + 1))
                        ts(u, bank_a[n % RING][:], 0.1 / TWO_PI, th[:, 9, k:k + 1], ALU.mult, ALU.add).then_inc(turn_ready.sem, 1)
                        dve.wait_ge(turn_ready.sem, turn_ready.at(rnd, m + 1))
                        ts(r_, u, MAGIC, -MAGIC, ALU.add, ALU.add).then_inc(whole_ready.sem, 1)

                def l3_relus(s):
                    for k in range(NH):
                        m = s * NH + k
                        dve.wait_ge(sin_ready.sem, sin_ready.at(rnd, m + 1))
                        stt(CV[:, k, :], HP[:, k, 1:S + 1], th[:, 8, k:k + 1], CV[:, k, :], ALU.mult, ALU.add).then_inc(turned_ready.sem, 1)

                def l3_added(s):
                    dve.wait_ge(x_added.sem, x_added.at(rnd, 2 + s + 1))
                    add_to_x(s, bank("l3_out", s))
                    dve.sem_inc(x_done.sem, 1)

                for s in range(SLOTS):
                    dve.wait_ge(x_loaded[s].sem, x_loaded[s].at(rnd, 1, 16))
                ns = [ln_start(s, XIN) for s in range(SLOTS)]
                for s in range(SLOTS):
                    ln_end(ns[s], s, XIN)
                l0_attention()
                wait_weights(dve, 2)
                dve.wait_ge(setup_pool, 2)
                keys(0, 0)

                def beside_layer0(e):
                    if e == 1:
                        queries(0, 0)
                    if e in (5, 6):
                        maxima(0, 0, e - 5)

                for s in range(SLOTS):
                    keys2(s)
                    l0_gates(s)
                    expert_sums(s, s * 2 * NE, 2, beside_layer0 if s == 1 else None)
                    n = ln_start(s)
                    keys2_sum(s)
                    ln_end(n, s)
                    if s == 0:
                        keys(0, 1)
                attention(0)
                l1_hidden(1)
                n = q2_start(0)
                l1_conv(1)
                q2_end(n, 0)
                l1_z(1)
                linear(0)
                l1_added(1)
                layer_norm(1)
                n1 = q2_start(1)
                n0 = linear_out_start(0)
                q2_end(n1, 1)
                linear_out_end(n0, 0)
                linear(1)

                def beside_layer2(e):
                    if e == 5:
                        n = linear_out_start(1)
                        linear_out_end(n, 1)

                def beside_layer2_1(e):
                    if e == 1:
                        queries(1, 0)
                    if e == 2:
                        keys(1, 1)
                    if e in (5, 6):
                        maxima(1, 0, e - 5)

                l2_ffn(0, beside_layer2)
                layer_norm(0)
                l2_ffn(1, beside_layer2_1)
                layer_norm(1)
                attention(1)
                l3_relus(1)
                l3_added(1)
                sync()
                assert n_v[0] == fills_v, n_v
                assert n_ln[0] == ln_var.n, n_ln


def kernel(**inputs):
    import concourse.bacc as bacc
    from concourse.bass_utils import run_bass_kernel_spmd

    a = {k: np.asarray(v) for k, v in inputs.items()}
    tiles = lambda v: v.reshape(NH, P).T
    words = lambda v: np.ascontiguousarray(v).view(np.uint32)
    laid = dict(
        consts=constants(),
        x=a["x"], ctx=a["ctx_1024"], ctxT=a["ctx_1024"].transpose(0, 2, 1),
        mask=words(a["mask_Bx1xSxS2_bk0"].reshape(NB, T, P, C).transpose(0, 2, 1, 3).reshape(NB, P, T * C)),
        maskT=words(a["mask_Bx1xSxS2_bk0"][:, 0].transpose(0, 2, 1)),
        em=a["mask_BxS2_ff1"][:, :, None],
        wg1=a["L0_ffn_wg1"], bg1=a["L0_ffn_bg1"][:, None], wg2=a["L0_ffn_wg2"], w_in=a["L0_ffn_w_in"], w_out=a["L0_ffn_w_out"],
        wq1=a["L1_xattn_W_q"].T, wk1=a["L1_xattn_W_k"].T, wv1=a["L1_xattn_W_v"].T, wp1=a["L1_xattn_W_proj"].T, bp1=a["L1_xattn_b_proj"],
        w1b=a["L1_ffn_w1"].T, cw=a["L1_ffn_conv_w"].reshape(NH, P, 3).transpose(1, 0, 2), cb=tiles(a["L1_ffn_conv_b"]), w2b=a["L1_ffn_w2"].T,
        wq2=a["L2_xattn_wq"], wk2=a["L2_xattn_wk"], wv2=a["L2_xattn_wv"], lng=a["L2_xattn_ln_gamma"], lnb=a["L2_xattn_ln_beta"],
        wd2=a["L2_xattn_dense_w"], bd2=a["L2_xattn_dense_b"],
        wg=a["L2_ffn_Wg"], bg=a["L2_ffn_bg"], w1e=a["L2_ffn_W1"], b1e=a["L2_ffn_b1"].T, w2e=a["L2_ffn_W2"], b2e=a["L2_ffn_b2"],
        wq3=a["L3_xattn_Wq"], wkv3=a["L3_xattn_Wkv"], wp3=a["L3_xattn_Wproj"], qg=a["L3_xattn_q_gamma"], kg=a["L3_xattn_k_gamma"],
        w13=a["L3_ffn_W1"], 
        l3v=np.stack([tiles(a["L3_ffn_" + k]) for k in ("b1", "quantum_phases", "quantum_weights_real", "quantum_weights_imag")], axis=1),
        w23=a["L3_ffn_W2"], b23=a["L3_ffn_b2"],
    )
    nc = bacc.Bacc("TRN2", target_bir_lowering=False, num_devices=1)
    arrays, aps = {}, {}
    for name, v in laid.items():
        v = np.ascontiguousarray(v)
        arrays[f"in_{name}"] = v
        aps[name] = nc.dram_tensor(f"in_{name}", v.shape, mybir.dt.from_np(v.dtype), kind="ExternalInput").ap()
    out = nc.dram_tensor("out", (NB, S, D), F32, kind="ExternalOutput").ap()
    build(nc, aps, out)
    return run_bass_kernel_spmd(nc, [arrays], core_ids=[0]).results[0]["out"]
```
